# Optimizing a Trainium2 kernel written in Bass

```python
import numpy as np
import jax
import jax.numpy as jnp

def _softmax(x, axis=-1):
    return jax.nn.softmax(x, axis=axis)

def _gelu(x):
    return jax.nn.gelu(x, approximate=True)

def _silu(x):
    return jax.nn.silu(x)

def _sigmoid(x):
    return jax.nn.sigmoid(x)

def _layernorm(x, axis=-1, eps=1e-05):
    m = jnp.mean(x, axis=axis, keepdims=True)
    v = jnp.var(x, axis=axis, keepdims=True)
    return (x - m) / jnp.sqrt(v + eps)

def _scatter_add(tgt, idx, src, axis=0):
    return tgt.at[idx].add(src)

def _segment_sum(src, seg, n):
    return jax.ops.segment_sum(src, seg, n)
kernel_name = 'mk_decoder_preln_d1_seqx_r4_6cbac6'

def setup_inputs(seed: int=0):
    np.random.seed(seed)
    _w = jnp.asarray

    def _rec_inputs():
        import jax
        import jax.numpy as jnp
        _rk = jax.random.key(seed)
        x = 7.22e-05 + 1 * jax.random.normal(jax.random.fold_in(_rk, 1), (4, 512, 256), jnp.float32)
        _lenS = 512 - jax.random.randint(jax.random.fold_in(_rk, 7), (4,), 0, max(1, 512 // 4) + 1, jnp.int32)
        _lenS2 = 1601 - jax.random.randint(jax.random.fold_in(_rk, 8), (4,), 0, max(1, 1601 // 4) + 1, jnp.int32)
        _ctx_1024P = jax.random.normal(jax.random.fold_in(_rk, 11), (4, 16, 256), jnp.float32)
        _ctx_1024c = jax.random.dirichlet(jax.random.fold_in(_rk, 511), 0.3 * jnp.ones((16,), jnp.float32), (4, 1601))
        _ctx_1024t = jnp.einsum('bsk,bkd->bsd', _ctx_1024c, _ctx_1024P)
        _ctx_1024t = _ctx_1024t * jax.lax.rsqrt(jnp.mean(jnp.square(_ctx_1024t)) + 1e-12) * 0.953939
        ctx_1024 = 4.13588e-05 + 0.999923 * (_ctx_1024t + 0.3 * jax.random.normal(jax.random.fold_in(_rk, 611), (4, 1601, 256), jnp.float32))
        _validS = jnp.arange(512)[None, :] < _lenS[:, None]
        _validS2 = jnp.arange(1601)[None, :] < _lenS2[:, None]
        _causal = jnp.tril(jnp.ones((512, 512), dtype=bool))
        mask_BxSxS2_bk1 = jnp.broadcast_to(_validS2[:, None, :], (4, 512, 1601))
        return (x, ctx_1024, mask_BxSxS2_bk1)
    x, ctx_1024, mask_BxSxS2_bk1 = _rec_inputs()

    def _L0_attn_setup():
        import jax, jax.numpy as jnp
        import numpy as np
        from jax import lax
        D_MODEL = 256
        D_STATE = 16
        D_CONV = 4
        EXPAND = 2
        D_INNER = D_MODEL * EXPAND
        BATCH = 4
        SEQ = 512

        def _selective_scan(x, dt, A, B, D):
            b, L, d_inner = x.shape
            h0 = jnp.zeros((b, d_inner, A.shape[1]), x.dtype)

            def step(h, inp):
                x_t, dt_t, B_t = inp
                dA = jnp.exp(dt_t[:, :, None] * A[None])
                h = dA * h + dt_t[:, :, None] * B_t[:, None, :] * x_t[:, :, None]
                y_t = h.sum(-1) + D[None, :] * x_t
                return (h, y_t)
            xs = (jnp.swapaxes(x, 0, 1), jnp.swapaxes(dt, 0, 1), jnp.swapaxes(B, 0, 1))
            _, ys = lax.scan(step, h0, xs)
            return jnp.swapaxes(ys, 0, 1)
        key = jax.random.key(seed)
        ks = jax.random.split(key, 10)

        def lin(k, out_f, in_f):
            return jax.random.normal(k, (out_f, in_f), jnp.float32) / np.sqrt(in_f)
        x = jax.random.normal(ks[0], (BATCH, SEQ, D_MODEL), jnp.float32)
        W_in = lin(ks[1], 2 * D_INNER, D_MODEL)
        W_conv = jax.random.normal(ks[2], (D_INNER, 1, D_CONV), jnp.float32) / np.sqrt(D_CONV)
        b_conv = jax.random.normal(ks[3], (D_INNER,), jnp.float32) * 0.02
        W_x = lin(ks[4], 2 * D_STATE, D_INNER)
        W_dt = lin(ks[5], D_INNER, D_INNER)
        b_dt = jax.random.normal(ks[6], (D_INNER,), jnp.float32) * 0.02
        W_out = lin(ks[7], D_MODEL, D_INNER)
        A_log = jax.random.normal(ks[8], (D_INNER, D_STATE), jnp.float32)
        D = jnp.ones((D_INNER,), jnp.float32)
        return {'x': x, 'W_in': W_in, 'W_conv': W_conv, 'b_conv': b_conv, 'W_x': W_x, 'W_dt': W_dt, 'b_dt': b_dt, 'W_out': W_out, 'A_log': A_log, 'D': D}
    _L0_attn_all = _L0_attn_setup()
    _L0_attn_in = {k: v for k, v in _L0_attn_all.items() if k in ('W_in', 'W_conv', 'b_conv', 'W_x', 'W_dt', 'b_dt', 'W_out', 'A_log', 'D')}
    del _L0_attn_all

    def _L0_xattn_setup():
        import jax, jax.numpy as jnp
        import numpy as np
        B, S, D = (4, 512, 256)
        key = jax.random.key(seed)
        ks = jax.random.split(key, 11)
        scale = 1.0 / np.sqrt(D)
        x = jax.random.normal(ks[0], (B, S, D), jnp.float32)
        y = jax.random.normal(ks[1], (B, S, D), jnp.float32)
        z = jax.random.normal(ks[2], (B, S, D), jnp.float32)
        mask = jnp.broadcast_to(jnp.triu(jnp.ones((S, S), bool), k=1), (B, S, S))
        Wq = jax.random.normal(ks[3], (D, D), jnp.float32) * scale
        bq = jax.random.normal(ks[4], (D,), jnp.float32) * scale
        Wk = jax.random.normal(ks[5], (D, D), jnp.float32) * scale
        bk = jax.random.normal(ks[6], (D,), jnp.float32) * scale
        Wv = jax.random.normal(ks[7], (D, D), jnp.float32) * scale
        bv = jax.random.normal(ks[8], (D,), jnp.float32) * scale
        Wo = jax.random.normal(ks[9], (D, D), jnp.float32) * scale
        bo = jax.random.normal(ks[10], (D,), jnp.float32) * scale
        return {'x': x, 'y': y, 'z': z, 'mask': mask, 'Wq': Wq, 'bq': bq, 'Wk': Wk, 'bk': bk, 'Wv': Wv, 'bv': bv, 'Wo': Wo, 'bo': bo}
    _L0_xattn_all = _L0_xattn_setup()
    _L0_xattn_in = {k: v for k, v in _L0_xattn_all.items() if k in ('Wq', 'bq', 'Wk', 'bk', 'Wv', 'bv', 'Wo', 'bo')}
    del _L0_xattn_all

    def _L0_ffn_setup():
        import jax, jax.numpy as jnp
        import numpy as np
        TOP_K = 2
        key = jax.random.key(seed)
        ks = jax.random.split(key, 5)
        B, S, D, H, E = (2, 512, 256, 704, 8)
        x = jax.random.normal(ks[0], (B, S, D), dtype=jnp.float32)
        Wg = jax.random.normal(ks[1], (E, D), dtype=jnp.float32) * 0.02
        W1 = jax.random.normal(ks[2], (E, H, D), dtype=jnp.float32) * 0.02
        W2 = jax.random.normal(ks[3], (E, H, D), dtype=jnp.float32) * 0.02
        W3 = jax.random.normal(ks[4], (E, D, H), dtype=jnp.float32) * 0.02
        return {'x': x, 'Wg': Wg, 'W1': W1, 'W2': W2, 'W3': W3}
    _L0_ffn_all = _L0_ffn_setup()
    _L0_ffn_in = {k: v for k, v in _L0_ffn_all.items() if k in ('Wg', 'W1', 'W2', 'W3')}
    del _L0_ffn_all
    return {'x': x, 'ctx_1024': ctx_1024, 'mask_BxSxS2_bk1': mask_BxSxS2_bk1, 'L0_attn_W_in': _L0_attn_in['W_in'], 'L0_attn_W_conv': _L0_attn_in['W_conv'], 'L0_attn_b_conv': _L0_attn_in['b_conv'], 'L0_attn_W_x': _L0_attn_in['W_x'], 'L0_attn_W_dt': _L0_attn_in['W_dt'], 'L0_attn_b_dt': _L0_attn_in['b_dt'], 'L0_attn_W_out': _L0_attn_in['W_out'], 'L0_attn_A_log': _L0_attn_in['A_log'], 'L0_attn_D': _L0_attn_in['D'], 'L0_xattn_Wq': _L0_xattn_in['Wq'], 'L0_xattn_bq': _L0_xattn_in['bq'], 'L0_xattn_Wk': _L0_xattn_in['Wk'], 'L0_xattn_bk': _L0_xattn_in['bk'], 'L0_xattn_Wv': _L0_xattn_in['Wv'], 'L0_xattn_bv': _L0_xattn_in['bv'], 'L0_xattn_Wo': _L0_xattn_in['Wo'], 'L0_xattn_bo': _L0_xattn_in['bo'], 'L0_ffn_Wg': _L0_ffn_in['Wg'], 'L0_ffn_W1': _L0_ffn_in['W1'], 'L0_ffn_W2': _L0_ffn_in['W2'], 'L0_ffn_W3': _L0_ffn_in['W3']}

def reference(x, ctx_1024, mask_BxSxS2_bk1, L0_attn_W_in, L0_attn_W_conv, L0_attn_b_conv, L0_attn_W_x, L0_attn_W_dt, L0_attn_b_dt, L0_attn_W_out, L0_attn_A_log, L0_attn_D, L0_xattn_Wq, L0_xattn_bq, L0_xattn_Wk, L0_xattn_bk, L0_xattn_Wv, L0_xattn_bv, L0_xattn_Wo, L0_xattn_bo, L0_ffn_Wg, L0_ffn_W1, L0_ffn_W2, L0_ffn_W3):
    import jax
    import jax.numpy as jnp

    def _L0_attn_ref(x, W_in, W_conv, b_conv, W_x, W_dt, b_dt, W_out, A_log, D):
        import jax, jax.numpy as jnp
        import numpy as np
        from jax import lax
        D_MODEL = 256
        D_STATE = 16
        D_CONV = 4
        EXPAND = 2
        D_INNER = D_MODEL * EXPAND
        BATCH = 4
        SEQ = 512

        def _selective_scan(x, dt, A, B, D):
            b, L, d_inner = x.shape
            h0 = jnp.zeros((b, d_inner, A.shape[1]), x.dtype)

            def step(h, inp):
                x_t, dt_t, B_t = inp
                dA = jnp.exp(dt_t[:, :, None] * A[None])
                h = dA * h + dt_t[:, :, None] * B_t[:, None, :] * x_t[:, :, None]
                y_t = h.sum(-1) + D[None, :] * x_t
                return (h, y_t)
            xs = (jnp.swapaxes(x, 0, 1), jnp.swapaxes(dt, 0, 1), jnp.swapaxes(B, 0, 1))
            _, ys = lax.scan(step, h0, xs)
            return jnp.swapaxes(ys, 0, 1)
        seq_len = x.shape[1]
        x_and_res = x @ W_in.T
        x_ssm, res = jnp.split(x_and_res, 2, axis=-1)
        xc = jnp.swapaxes(x_ssm, 1, 2)
        xc = lax.conv_general_dilated(xc, W_conv, window_strides=(1,), padding=[(D_CONV - 1, 0)], feature_group_count=W_conv.shape[0], dimension_numbers=('NCH', 'OIH', 'NCH'))
        xc = xc + b_conv[None, :, None]
        x_ssm = jax.nn.silu(jnp.swapaxes(xc, 1, 2))
        A = -jnp.exp(A_log)
        deltaBC = x_ssm @ W_x.T
        _delta, B_C = jnp.split(deltaBC, 2, axis=-1)
        dt = jax.nn.softplus(x_ssm @ W_dt.T + b_dt)
        y = _selective_scan(x_ssm, dt, A, B_C, D)
        y = y * jax.nn.silu(res)
        return y @ W_out.T

    def _L0_xattn_ref(x, y, z, mask, Wq, bq, Wk, bk, Wv, bv, Wo, bo):
        import jax, jax.numpy as jnp
        import numpy as np
        B, S, D = (4, 512, 256)
        Q = jnp.einsum('bsd,ed->bse', x, Wq) + bq
        K = jnp.einsum('bsd,ed->bse', y, Wk) + bk
        V = jnp.einsum('bsd,ed->bse', z, Wv) + bv
        sim = jnp.einsum('bqd,bkd->bqk', Q, K)
        sim = jnp.where(mask, jnp.float32(-1000000000.0), sim)
        attn = jax.nn.softmax(sim, axis=-1)
        out = jnp.einsum('bqk,bkd->bqd', attn, V)
        return jnp.einsum('bsd,ed->bse', out, Wo) + bo

    def _L0_ffn_ref(x, Wg, W1, W2, W3):
        import jax, jax.numpy as jnp
        import numpy as np
        TOP_K = 2
        B, S, D = x.shape
        E = Wg.shape[0]
        xt = x.reshape(B * S, D)
        scores = xt @ Wg.T
        topk_scores, topk_idx = jax.lax.top_k(scores, TOP_K)
        gate = jax.nn.silu(jnp.einsum('td,ehd->teh', xt, W1))
        up = jnp.einsum('td,ehd->teh', xt, W2)
        y = jnp.einsum('teh,edh->ted', gate * up, W3)
        onehot = jax.nn.one_hot(topk_idx, E, dtype=x.dtype)
        w = jnp.einsum('tke,tk->te', onehot, topk_scores)
        out = jnp.einsum('te,ted->td', w, y)
        return out.reshape(B, S, D)
    x = x + _L0_attn_ref(_layernorm(x, axis=-1), L0_attn_W_in, L0_attn_W_conv, L0_attn_b_conv, L0_attn_W_x, L0_attn_W_dt, L0_attn_b_dt, L0_attn_W_out, L0_attn_A_log, L0_attn_D)
    x = x + _L0_xattn_ref(_layernorm(x, axis=-1), ctx_1024, ctx_1024, mask_BxSxS2_bk1, L0_xattn_Wq, L0_xattn_bq, L0_xattn_Wk, L0_xattn_bk, L0_xattn_Wv, L0_xattn_bv, L0_xattn_Wo, L0_xattn_bo)
    x = x + _L0_ffn_ref(_layernorm(x, axis=-1), L0_ffn_Wg, L0_ffn_W1, L0_ffn_W2, L0_ffn_W3)
    return x

_drawn_inputs = setup_inputs


def setup_inputs(seed=0):
    import zlib

    import numpy as np

    out = dict(_drawn_inputs(seed))
    spreads = {'L0_attn_D': (1.0, 0.2)}
    factors = {'L0_attn_b_dt': 4.015,
     'L0_xattn_bk': 8.0,
     'L0_ffn_Wg': 7.97,
     'L0_ffn_W1': 7.172,
     'L0_ffn_W2': 7.136,
     'L0_ffn_W3': 7.142}
    for name, (base, spread) in spreads.items():
        noise = np.random.default_rng([zlib.crc32(name.encode()), seed]).standard_normal(out[name].shape)
        drawn = base * np.exp(spread * noise) if base else spread * noise
        out[name] = jnp.asarray(drawn.astype(out[name].dtype))
    for name, factor in factors.items():
        out[name] = (out[name] * factor).astype(out[name].dtype)
    return out
```

```python
from contextlib import ExitStack

import concourse.bass as bass
from concourse import mybir

F32 = mybir.dt.float32
I32 = mybir.dt.int32
U32 = mybir.dt.uint32
U8 = mybir.dt.uint8
ACT = mybir.ActivationFunctionType
ALU = mybir.AluOpType
AX_X = mybir.AxisListType.X

P = 128
EPS = 1e-5
MASKED = -1000000000.0
NEG_HUGE = -3.0e38


def at(i, n=1):
    return bass.ds(i, n)


def wait(eng, sem, value):
    if isinstance(value, int) and value <= 0:
        return
    eng.wait_ge(sem, value)


def decoder_kernel(nc, io, dims):
    B, S, D, S2, DI, NST, TAPS, E, HF = dims
    KD = D // P
    KI = DI // P
    T = S // P
    G = B * T
    KC = -(-S2 // P)
    S2_LAST = S2 - (KC - 1) * P
    CH = -(-S2 // 4)
    CHUNKS = [(c * CH, min(S2, (c + 1) * CH)) for c in range(4)]
    KH = -(-HF // P)
    H_LAST = HF - (KH - 1) * P
    HH = HF // 2
    NT = (2 * B * S + E * (P - 1)) // P

    tok_sorted = nc.dram_tensor("tok_sorted", [NT * P, D], F32).ap()
    ffn_sorted = nc.dram_tensor("ffn_sorted", [NT * P, D], F32).ap()
    xn3_dram = nc.dram_tensor("xn3_dram", [G * P, D], F32).ap()
    b_dram = nc.dram_tensor("b_dram", [B, NST * S], F32).ap()

    top = ExitStack()
    with top:
        def sem(name):
            return top.enter_context(nc.semaphore(name))

        def buf(ctx, name, shape, dt=F32):
            return ctx.enter_context(nc.sbuf_tensor(name, shape, dt))

        zeros = buf(top, "zeros", [P, D])
        x_all = buf(top, "x_all", [P, G, D])
        ident = buf(top, "ident", [P, P])
        scores = buf(top, "scores", [P, G, E])

        mixer_phase(nc, io, dims, locals(), sem, buf)
        routed_ffn_phase(nc, io, dims, locals(), sem, buf)


def mixer_phase(nc, io, dims, env, sem, buf):
    B, S, D, S2, DI, NST, TAPS, E, HF = dims
    KD, KI, T, KC = env["KD"], env["KI"], env["T"], env["KC"]
    S2_LAST, CHUNKS = env["S2_LAST"], env["CHUNKS"]
    x_all, ident, scores = env["x_all"], env["ident"], env["scores"]
    xn3_dram, b_dram, tok_sorted, zeros, NT = (env[k] for k in ("xn3_dram", "b_dram", "tok_sorted", "zeros", "NT"))

    with ExitStack() as ctx:
        def sb(name, shape, dt=F32):
            return buf(ctx, name, shape, dt)

        def ps(name):
            return ctx.enter_context(nc.psum_tensor(name, [P, 512], F32))

        w_in = sb("w_in", [P, KD, 2 * DI])
        w_dt = sb("w_dt", [P, KI, DI])
        w_b = sb("w_b", [P, KI, NST])
        w_out = sb("w_out", [P, KI, D])
        w_conv = sb("w_conv", [P, KI, TAPS])
        b_conv = sb("b_conv", [P, KI])
        b_dt = sb("b_dt", [P, KI])
        d_skip = sb("d_skip", [P, KI])
        a_neg = sb("a_neg", [P, KI, NST])
        w_qk = sb("w_qk", [P, KD, D])
        w_vo = sb("w_vo", [P, KD, D])
        bq_k = sb("bq_k", [P, KD])
        wq_bk = sb("wq_bk", [P, KD])
        neg_c0 = sb("neg_c0", [P, 1])
        c_vo = sb("c_vo", [P, D])
        w_g = sb("w_g", [P, KD, E])
        xn_m = sb("xn_m", [P, T, D])
        xnT_m = sb("xnT_m", [P, KD, S])
        conv = sb("conv", [P, 2, S])
        xs = sb("xs", [P, KI, S])
        gate = sb("gate", [P, KI, S])
        dt_ = sb("dt_", [P, KI, S])
        dtx = sb("dtx", [P, KI, S])
        sp_abs = sb("sp_abs", [P, S])
        sp_pos = sb("sp_pos", [P, S])
        b_row = sb("b_row", [NST, S])
        b_all = sb("b_all", [P, NST, S])
        u = sb("u", [P, 2, S])
        h = sb("h", [P, 4, S])
        xn_a = sb("xn_a", [P, T, D])
        xnT_a = sb("xnT_a", [P, KD, S])
        qT = sb("qT", [P, KD, S])
        neg_c = sb("neg_c", [P, T])
        ctx_n = sb("ctx_n", [P, KC, D])
        ctx_t = sb("ctx_t", [P, KD, S2])
        mask = sb("mask", [P, 2, -(-S2 // 4) * 4], U8)
        sim = sb("sim", [P, 2, S2])
        pT = sb("pT", [P, KC, P])
        row_max = sb("row_max", [P, 2])
        row_sum = sb("row_sum", [P, 2])
        row_inv = sb("row_inv", [P, 2])
        att = sb("att", [P, D])
        attT = sb("attT", [P, KD, P])
        ln_buf = [(sb(f"ln_stat{i}", [P, T, 6]), sb(f"ln_mv{i}", [P, T, 2]), sb(f"ln_var{i}", [P, T]),
                   sb(f"ln_log{i}", [P, T]), sb(f"ln_r{i}", [P, T]), sb(f"ln_t{i}", [P, T])) for i in range(3)]
        wq = h[:, 0, :].rearrange("p (k d) -> p k d", k=KD)
        wk = h[:, 1, :].rearrange("p (k d) -> p k d", k=KD)
        wv = h[:, 2, :].rearrange("p (k d) -> p k d", k=KD)
        wo = h[:, 3, :].rearrange("p (k d) -> p k d", k=KD)
        bk_b = u[:, 0, 0:KD * P].rearrange("p (k m) -> p k m", k=KD)
        bv_b = u[:, 1, 0:KD * P].rearrange("p (k m) -> p k m", k=KD)
        b_qkv = sb("b_qkv", [P, 3, KD])
        scrap = sb("scrap", [P, 96])
        pool_scrap = sb("pool_scrap", [P, T])
        bo_row = sb("bo_row", [1, D])
        ones = sb("ones", [P, P])

        da = [ps("da0"), ps("da1")]
        ysum = [ps("ysum0"), ps("ysum1")]
        pm = [ps("pm0"), ps("pm1")]
        pa = [ps("pa0"), ps("pa1")]

        x_ld, w_ld, wa_ld = sem("x_ld"), sem("w_ld"), sem("wa_ld")
        b_st, b_ld, ctx_ld, mask_ld, xn3_st = (sem(n) for n in ("b_st", "b_ld", "ctx_ld", "mask_ld", "xn3_st"))
        zero_ok, zero_st = sem("zero_ok"), sem("zero_st")
        id_zero, id_ok, ones_ok, a_exp, a_ok = (sem(n) for n in ("id_zero", "id_ok", "ones_ok", "a_exp", "a_ok"))
        bias_b, setup_mm, setup_ok = sem("bias_b"), sem("setup_mm"), sem("setup_ok")
        ip_mm, conv_step, silu_ok, b_mm, b_ev = (sem(n) for n in ("ip_mm", "conv_step", "silu_ok", "b_mm", "b_ev"))
        res_ok, dt_mm, sp_step, pos_ok, dt_ok, dtx_ok = (
            sem(n) for n in ("res_ok", "dt_mm", "sp_step", "pos_ok", "dt_ok", "dtx_ok"))
        da_ok, u_ok, scan_ok, sum_ok, y_ok, yg_ok = (
            sem(n) for n in ("da_ok", "u_ok", "scan_ok", "sum_ok", "y_ok", "yg_ok"))
        op_mm, x1_ok = sem("op_mm"), sem("x1_ok")
        q_mm, q_ok, c_mm, c_ok, s_mm, fill_ok, inv_ok, pick_ok, max_ok, nmax_ok, exp_ok, rinv_ok = (
            sem(n) for n in ("q_mm", "q_ok", "c_mm", "c_ok", "s_mm", "fill_ok", "inv_ok", "pick_ok", "max_ok",
                             "nmax_ok", "exp_ok", "rinv_ok"))
        pt_mm, pt_ok, av_mm, av_ok, at_mm, at_ok, o_mm, xc_ok, x2_ok, r_mm, r_ok = (
            sem(n) for n in ("pt_mm", "pt_ok", "av_mm", "av_ok", "at_mm", "at_ok", "o_mm", "xc_ok", "x2_ok",
                             "r_mm", "r_ok"))
        LN = [{k: sem(f"ln{i}_{k}") for k in ("stat", "mv", "var", "log", "r0", "newton", "xn", "tr", "xT")}
              for i in range(3)]
        XN, XNT = (xn_m, xn_a, xn_a), (xnT_m, xnT_a, xnT_a)

        m_uses = [(LN[0]["xT"], KD, k + 1) for k in range(KD)]
        m_uses += [(conv_step, TAPS * KI, TAPS * (j + 1)) for j in range(KI)]
        m_uses += [(res_ok, KI, j + 1) for j in range(KI)]
        m_uses += [(b_ev, 1, 1)]
        m_uses += [(pos_ok, KI, j + 1) for j in range(KI)]
        m_uses += [(x1_ok, T, t + 1) for t in range(T)]
        M_IP, M_RES, M_B, M_DT, M_OUT = KD, KD + KI, KD + 2 * KI, KD + 2 * KI + 1, KD + 3 * KI + 1
        m_bank = [i % 2 for i in range(len(m_uses))]
        m_bank[-T:] = [(i + 1) % 2 for i in range(T)] if len(m_uses) % 2 == 0 else m_bank[-T:]

        n_pt = -(-KC // 4)
        a_uses = [(LN[1]["xT"], KD, k + 1) for k in range(KD)]
        a_uses += [(q_ok, KD, m + 1) for m in range(KD)]
        a_uses += [(c_ok, 1, 1)]
        A_Q, A_C = KD, 2 * KD
        A_S, A_PT, A_AV, A_AT, A_O = {}, {}, {}, {}, {}

        def plan_scores(q):
            A_S[q] = len(a_uses)
            a_uses.extend((pick_ok, 4 * T, 4 * q + c + 1) for c in range(4))

        plan_scores(0)
        for q in range(T):
            if q + 1 < T:
                plan_scores(q + 1)
            A_PT[q] = len(a_uses)
            a_uses.extend((pt_ok, n_pt * T, n_pt * q + g + 1) for g in range(n_pt))
            A_AV[q] = len(a_uses)
            a_uses.append((av_ok, T, q + 1))
            A_AT[q] = len(a_uses)
            a_uses.append((at_ok, T, q + 1))
            A_O[q] = len(a_uses)
            a_uses.append((x2_ok, T, q + 1))
        A_L3 = len(a_uses)
        a_uses += [(LN[2]["xT"], KD, k + 1) for k in range(KD)]
        A_R = len(a_uses)
        a_uses.append((r_ok, 1, 1))
        a_bank = [i % 2 for i in range(len(a_uses))]

        def bank_free(eng, uses, banks, i, b):
            before = [k for k in range(i) if banks[k] == banks[i]]
            if before:
                s, per, n = uses[before[-1]]
                wait(eng, s, b * per + n)
            else:
                last = [k for k in range(len(uses)) if banks[k] == banks[i]][-1]
                s, per, n = uses[last]
                wait(eng, s, (b - 1) * per + n)

        def rows(b, t):
            return x_all[:, at(b * T + t), :].rearrange("p a d -> p (a d)")

        scrap_used = [0]

        def take_wait():
            nc.vector.memset(scrap[:, at(scrap_used[0])], 0.0)
            scrap_used[0] += 1

        def ln_vector(dve, i, b, ready, consumed):
            s, (stat, mv, var, log, r, tmp) = LN[i], ln_buf[i]
            ready(dve, b)
            take_wait()
            for t in range(T):
                nc.vector.bn_stats(stat[:, t, :], rows(b, t)).then_inc(s["stat"], 1)
            dve.wait_ge(s["stat"], b * T + T)
            take_wait()
            for t in range(T):
                nc.vector.bn_aggr(mv[:, t, :], stat[:, t, :]).then_inc(s["mv"], 1)
            dve.wait_ge(s["mv"], b * T + T)
            nc.vector.tensor_scalar(var[:], mv[:, :, 1], EPS, None, ALU.add).then_inc(s["var"], 1)
            dve.wait_ge(s["r0"], b + 1)
            nc.vector.tensor_tensor(tmp[:], r[:], r[:], ALU.mult).then_inc(s["newton"], 1)
            dve.wait_ge(s["newton"], b * 4 + 1)
            nc.vector.tensor_tensor(tmp[:], tmp[:], var[:], ALU.mult).then_inc(s["newton"], 1)
            dve.wait_ge(s["newton"], b * 4 + 2)
            nc.vector.tensor_scalar(tmp[:], tmp[:], -0.5, 1.5, ALU.mult, ALU.add).then_inc(s["newton"], 1)
            dve.wait_ge(s["newton"], b * 4 + 3)
            nc.vector.tensor_tensor(r[:], r[:], tmp[:], ALU.mult).then_inc(s["newton"], 1)
            dve.wait_ge(s["newton"], b * 4 + 4)
            consumed(dve, b)
            for t in range(T):
                nc.vector.tensor_scalar(XN[i][:, t, :], rows(b, t), mv[:, t, 0:1], r[:, t:t + 1],
                                        ALU.subtract, ALU.mult).then_inc(s["xn"], 1)

        def ln_scalar(act, i, b):
            s, (stat, mv, var, log, r, tmp) = LN[i], ln_buf[i]
            act.wait_ge(s["var"], b + 1)
            nc.scalar.activation(log[:], var[:], ACT.Ln).then_inc(s["log"], 1)
            act.wait_ge(s["log"], b + 1)
            nc.scalar.activation(r[:], log[:], ACT.Exp, scale=-0.5).then_inc(s["r0"], 1)

        def ln_transpose(pe, i, b, uses, banks, first, out):
            s = LN[i]
            for k in range(KD):
                bank_free(pe, uses, banks, first + k, b)
                for t in range(T):
                    pe.wait_ge(s["xn"], b * T + t + 1)
                    last = nc.tensor.transpose(out[banks[first + k]][:, t * P:(t + 1) * P],
                                               XN[i][:, t, k * P:(k + 1) * P], ident[:])
                last.then_inc(s["tr"], 1)

        def ln_evacuate(act, i, b, banks, first, src, consumed):
            s = LN[i]
            for k in range(KD):
                act.wait_ge(s["tr"], b * KD + k + 1)
                consumed(act, b)
                nc.scalar.copy(XNT[i][:, k, :], src[banks[first + k]][:]).then_inc(s["xT"], 1)

        with nc.Block() as block:

            @block.sync
            def _(sp):
                sp.dma_start(x_all[:], io["x"].rearrange("(g p) d -> p g d", p=P)).then_inc(x_ld, 16)
                for dst, src in (
                    (w_in, io["w_inT"].rearrange("(k p) o -> p k o", p=P)),
                    (w_conv, io["w_conv"].rearrange("(j p) k -> p j k", p=P)),
                    (b_conv, io["b_conv"]),
                    (w_b, io["w_bT"].rearrange("(k p) n -> p k n", p=P)),
                    (w_dt, io["w_dtT"].rearrange("(k p) o -> p k o", p=P)),
                    (b_dt, io["b_dt"]),
                    (a_neg, io["a_log"].rearrange("(j p) n -> p j n", p=P)),
                    (d_skip, io["d_skip"]),
                    (w_out, io["w_outT"].rearrange("(k p) o -> p k o", p=P)),
                ):
                    sp.dma_start(dst[:], src).then_inc(w_ld, 16)

                def body(b):
                    wait(sp, pt_ok, b * n_pt * T)
                    wait(sp, av_mm, b * T)
                    wait(sp, s_mm, b * 4 * T)
                    wait(sp, ctx_ld, b * 48)
                    full = (KC - 1) * P
                    sp.dma_start(ctx_n[:, 0:KC - 1, :], io["ctx"][at(b), 0:full, :].rearrange(
                        "a (c p) d -> p (a c) d", p=P)).then_inc(ctx_ld, 16)
                    sp.dma_start(ctx_n[0:S2_LAST, KC - 1, :], io["ctx"][at(b), full:S2, :].rearrange(
                        "a p d -> p (a d)")).then_inc(ctx_ld, 16)
                    sp.dma_start(ctx_t[:], io["ctxT"][at(b), :, :].rearrange(
                        "a (k p) s -> p (a k) s", p=P)).then_inc(ctx_ld, 16)
                    sp.wait_ge(b_ev, b + 1)
                    sp.dma_start(b_dram[at(b), :].rearrange("a (n s) -> (a n) s", n=NST), b_row[:]).then_inc(b_st, 16)
                    sp.wait_ge(b_st, 16 * (b + 1))
                    wait(sp, u_ok, b * KI * NST)
                    sp.dma_start(b_all[:], b_dram[at(b), :].to_broadcast((P, NST * S)).rearrange(
                        "p (n s) -> p n s", n=NST)).then_inc(b_ld, 16)
                    for q in range(T):
                        wait(sp, pick_ok, b * 4 * T + 4 * (q - 1))
                        wait(sp, mask_ld, 16 * (b * T + q))
                        sp.dma_start(mask[:, q % 2, 0:S2], io["mask"][at(b), q * P:(q + 1) * P, :].rearrange(
                            "a p s -> p (a s)")).then_inc(mask_ld, 16)
                    for t in range(T):
                        sp.wait_ge(LN[2]["xn"], b * T + t + 1)
                        sp.dma_start(xn3_dram[at(b * S + t * P, P), :], xn_a[:, t, :]).then_inc(xn3_st, 16)

                sp.wait_ge(zero_ok, 1)
                sp.dma_start(tok_sorted.rearrange("(n p) d -> p n d", p=P),
                             zeros[:].unsqueeze(1).to_broadcast([P, NT, D])).then_inc(zero_st, 16)
                for b in range(B):
                    body(b)
                sp.wait_ge(zero_st, 16)
                sp.wait_ge(xn3_st, 16 * B * T)

            @block.gpsimd
            def _(pool):
                pool.dma_start(wq, io["wq"].rearrange("(k p) d -> p k d", p=P)).then_inc(wa_ld, 16)
                pool.dma_start(wk, io["wk"].rearrange("(k p) d -> p k d", p=P)).then_inc(wa_ld, 16)
                pool.dma_start(wv, io["wv"].rearrange("(k p) d -> p k d", p=P)).then_inc(wa_ld, 16)
                pool.dma_start(wo, io["woT"].rearrange("(k p) d -> p k d", p=P)).then_inc(wa_ld, 16)
                for n, name in enumerate(("bq", "bk", "bv")):
                    pool.dma_start(b_qkv[:, n, :], io[name]).then_inc(wa_ld, 16)
                pool.dma_start(bo_row[:], io["bo"].rearrange("(a d) -> a d", a=1)).then_inc(wa_ld, 16)
                pool.dma_start(w_g[:], io["w_gT"].rearrange("(k p) e -> p k e", p=P)).then_inc(wa_ld, 16)
                nc.gpsimd.memset(zeros[:], 0.0).then_inc(zero_ok, 1)
                nc.gpsimd.memset(ident[:], 0.0).then_inc(id_zero, 1)
                nc.gpsimd.memset(ones[:], 1.0).then_inc(ones_ok, 1)
                pool.wait_ge(id_zero, 1)
                nc.gpsimd.affine_select(out=ident[:], in_=ident[:], compare_op=ALU.not_equal, fill=1.0, base=0,
                                        pattern=[[-1, P]], channel_multiplier=1).then_inc(id_ok, 1)
                pool.wait_ge(setup_mm, 1)

                def body(b):
                    for j in range(KI):
                        pool.wait_ge(dt_ok, b * KI + j + 1)
                        nc.gpsimd.tensor_tensor(dtx[:, j, :], dt_[:, j, :], xs[:, j, :], ALU.mult).then_inc(dtx_ok, 1)
                    pool.wait_ge(b_ld, 16 * (b + 1))
                    for j in range(KI):
                        pool.wait_ge(dtx_ok, b * KI + j + 1)
                        for n in range(NST):
                            i = j * NST + n
                            wait(pool, scan_ok, b * KI * NST + i - 1)
                            nc.gpsimd.tensor_tensor(u[:, i % 2, :], dtx[:, j, :], b_all[:, n, :],
                                                    ALU.mult).then_inc(u_ok, 1)
                    for t in range(T):
                        pool.wait_ge(LN[1]["xn"], b * T + T)
                        nc.gpsimd.tensor_tensor(rows(b, t), rows(b, t), c_vo[:], ALU.add).then_inc(xc_ok, 1)
                    pool.wait_ge(c_ok, b + 1)
                    for q in range(T):
                        pool.wait_ge(mask_ld, 16 * (b * T + q + 1))
                        wait(pool, pt_mm, b * n_pt * T + n_pt * (q - 1))
                        nc.gpsimd.tensor_tensor(pool_scrap[:, q:q + 1], ones[:, 0:1], ones[:, 0:1], ALU.mult)
                        nc.gpsimd.tensor_scalar(sim[:, q % 2, :], mask[:, q % 2, 0:S2], 0.0, neg_c[:, q:q + 1],
                                                ALU.mult, ALU.add).then_inc(fill_ok, 1)
                        nc.gpsimd.tensor_scalar(mask[:, q % 2, 0:S2], mask[:, q % 2, 0:S2], -1.0, 1.0, ALU.mult,
                                                ALU.add).then_inc(inv_ok, 1)

                body(0)
                with pool.Fori(1, B) as b:
                    body(b)

            @block.scalar
            def _(act):
                act.wait_ge(w_ld, 16 * 9)
                nc.scalar.activation(a_neg[:], a_neg[:], ACT.Exp).then_inc(a_exp, 1)

                def mamba_in(b):
                    ln_scalar(act, 0, b)
                    ln_evacuate(act, 0, b, m_bank, 0, pm, lambda e, b: wait(e, ip_mm, b * 2 * KI))
                    for j in range(KI):
                        act.wait_ge(conv_step, b * TAPS * KI + TAPS * (j + 1))
                        wait(act, yg_ok, b * KI)
                        nc.scalar.activation(xs[:, j, :], conv[:, j % 2, :], ACT.Silu).then_inc(silu_ok, 1)
                    for j in range(KI):
                        act.wait_ge(ip_mm, b * 2 * KI + KI + j + 1)
                        wait(act, op_mm, b * T)
                        nc.scalar.activation(gate[:, j, :], pm[m_bank[M_RES + j]][:], ACT.Silu).then_inc(res_ok, 1)
                    act.wait_ge(b_mm, b + 1)
                    wait(act, b_st, 16 * b)
                    nc.scalar.copy(b_row[:], pm[m_bank[M_B]][0:NST, :]).then_inc(b_ev, 1)
                    for j in range(KI):
                        act.wait_ge(dt_mm, b * KI + j + 1)
                        wait(act, dt_ok, b * KI + j)
                        z = pm[m_bank[M_DT + j]]
                        nc.scalar.activation(sp_abs[:], z[:], ACT.Abs, bias=b_dt[:, j:j + 1]).then_inc(sp_step, 1)
                        nc.scalar.activation(sp_pos[:], z[:], ACT.Relu, bias=b_dt[:, j:j + 1]).then_inc(pos_ok, 1)
                        act.wait_ge(sp_step, b * 3 * KI + 3 * j + 1)
                        nc.scalar.activation(sp_abs[:], sp_abs[:], ACT.Exp, scale=-1.0).then_inc(sp_step, 1)
                        act.wait_ge(sp_step, b * 3 * KI + 3 * j + 2)
                        nc.scalar.activation(sp_abs[:], sp_abs[:], ACT.Ln, bias=1.0).then_inc(sp_step, 1)

                def decay(b):
                    act.wait_ge(a_ok, 1)
                    for j in range(KI):
                        act.wait_ge(dt_ok, b * KI + j + 1)
                        for n in range(NST):
                            i = j * NST + n
                            wait(act, scan_ok, b * KI * NST + i - 1)
                            nc.scalar.activation(da[i % 2][:], dt_[:, j, :], ACT.Exp,
                                                 scale=a_neg[:, j, n:n + 1]).then_inc(da_ok, 1)

                def attention(b):
                    ln_scalar(act, 1, b)
                    ln_evacuate(act, 1, b, a_bank, 0, pa, lambda e, b: wait(e, r_mm, b))
                    for m in range(KD):
                        act.wait_ge(q_mm, b * KD + m + 1)
                        wait(act, s_mm, b * 4 * T)
                        nc.scalar.activation(qT[:, m, :], pa[a_bank[A_Q + m]][:], ACT.Identity,
                                             bias=bq_k[:, m:m + 1]).then_inc(q_ok, 1)
                    for q in range(T):
                        act.wait_ge(nmax_ok, b * T + q + 1)
                        nc.scalar.activation(sim[:, q % 2, :], sim[:, q % 2, :], ACT.Exp, bias=row_max[:, q % 2:q % 2 + 1],
                                             accum_out=row_sum[:, q % 2:q % 2 + 1]).then_inc(exp_ok, 1)
                        for g in range(n_pt):
                            act.wait_ge(pt_mm, b * n_pt * T + n_pt * q + g + 1)
                            wait(act, av_mm, b * T + q)
                            chunks = min(4, KC - 4 * g)
                            rows_in = S2_LAST if chunks == 1 else P
                            assert g < n_pt - 1 or chunks == 1
                            nc.scalar.copy(pT[0:rows_in, 4 * g:4 * g + chunks, :],
                                           pa[a_bank[A_PT[q] + g]][0:rows_in, 0:chunks * P].rearrange(
                                               "p (c m) -> p c m", m=P)).then_inc(pt_ok, 1)
                        act.wait_ge(av_mm, b * T + q + 1)
                        act.wait_ge(rinv_ok, b * T + q + 1)
                        wait(act, at_mm, b * T + q)
                        nc.scalar.activation(att[:], pa[a_bank[A_AV[q]]][:, 0:D], ACT.Copy,
                                             scale=row_inv[:, q % 2:q % 2 + 1]).then_inc(av_ok, 1)
                    ln_scalar(act, 2, b)
                    ln_evacuate(act, 2, b, a_bank, A_L3, pa, lambda e, b: e.wait_ge(c_mm, b + 1))

                def body(b):
                    mamba_in(b)
                    decay(b)
                    attention(b)

                body(0)
                with act.Fori(1, B) as b:
                    body(b)

            @block.vector
            def _(dve):
                dve.wait_ge(a_exp, 1)
                nc.vector.tensor_scalar(a_neg[:], a_neg[:], -1.0, None, ALU.mult).then_inc(a_ok, 1)
                dve.wait_ge(ones_ok, 1)
                dve.wait_ge(wa_ld, 16 * 9)
                for k in range(KD):
                    nc.vector.tensor_scalar(bk_b[:, k, :], ones[:], b_qkv[:, 1, k:k + 1], None, ALU.mult).then_inc(bias_b, 1)
                    nc.vector.tensor_scalar(bv_b[:, k, :], ones[:], b_qkv[:, 2, k:k + 1], None, ALU.mult).then_inc(bias_b, 1)
                dve.wait_ge(setup_mm, 1)
                flat = "p k d -> p (k d)"
                nc.vector.tensor_copy(w_qk[:].rearrange(flat), pa[0][:, 0:KD * D]).then_inc(setup_ok, 1)
                nc.vector.tensor_copy(w_vo[:].rearrange(flat), pa[1][:, 0:KD * D]).then_inc(setup_ok, 1)
                nc.vector.tensor_copy(c_vo[:], pm[0][:, 0:D]).then_inc(setup_ok, 1)
                nc.vector.tensor_copy(wq_bk[:], pm[0][:, D:D + KD]).then_inc(setup_ok, 1)
                nc.vector.tensor_copy(bq_k[:], pm[0][:, D + KD:D + 2 * KD]).then_inc(setup_ok, 1)
                nc.vector.tensor_scalar(neg_c0[:], pm[0][:, D + 2 * KD:D + 2 * KD + 1], -1.0, MASKED, ALU.mult,
                                        ALU.add).then_inc(setup_ok, 1)
                dve.wait_ge(setup_ok, 6)

                def mamba_in(b):
                    ln_vector(dve, 0, b, lambda e, b: e.wait_ge(x_ld, 16),
                              lambda e, b: wait(e, LN[0]["tr"], b * KD))
                    for j in range(KI):
                        dve.wait_ge(ip_mm, b * 2 * KI + j + 1)
                        wait(dve, silu_ok, b * KI + j - 1)
                        x_ps, c = pm[m_bank[M_IP + j]], conv[:, j % 2, :]
                        nc.vector.tensor_scalar(c, x_ps[:], w_conv[:, j, TAPS - 1:TAPS], b_conv[:, j:j + 1],
                                                ALU.mult, ALU.add).then_inc(conv_step, 1)
                        for s in range(1, TAPS):
                            dve.wait_ge(conv_step, b * TAPS * KI + TAPS * j + s)
                            nc.vector.scalar_tensor_tensor(
                                out=c[:, s:S], in0=x_ps[:, 0:S - s], scalar=w_conv[:, j, TAPS - 1 - s:TAPS - s],
                                in1=c[:, s:S], op0=ALU.mult, op1=ALU.add).then_inc(conv_step, 1)
                    for j in range(KI):
                        dve.wait_ge(sp_step, b * 3 * KI + 3 * j + 3)
                        dve.wait_ge(pos_ok, b * KI + j + 1)
                        nc.vector.tensor_tensor(dt_[:, j, :], sp_pos[:], sp_abs[:], ALU.add).then_inc(dt_ok, 1)

                def scan(b):
                    for j in range(KI):
                        for n in range(NST):
                            i = j * NST + n
                            dve.wait_ge(da_ok, b * KI * NST + i + 1)
                            dve.wait_ge(u_ok, b * KI * NST + i + 1)
                            wait(dve, sum_ok, b * KI * NST + i - 3)
                            nc.vector.tensor_tensor_scan(h[:, i % 4, :], da[i % 2][:], u[:, i % 2, :], 0.0,
                                                         ALU.mult, ALU.add).then_inc(scan_ok, 1)
                        dve.wait_ge(sum_ok, b * KI * NST + NST * (j + 1))
                        dve.wait_ge(u_ok, b * KI * NST + NST * (j + 1))
                        nc.vector.scalar_tensor_tensor(out=dtx[:, j, :], in0=xs[:, j, :], scalar=d_skip[:, j:j + 1],
                                                       in1=ysum[j % 2][:], op0=ALU.mult, op1=ALU.add).then_inc(y_ok, 1)
                        dve.wait_ge(y_ok, b * KI + j + 1)
                        dve.wait_ge(res_ok, b * KI + j + 1)
                        nc.vector.tensor_tensor(gate[:, j, :], dtx[:, j, :], gate[:, j, :], ALU.mult).then_inc(yg_ok, 1)
                    for t in range(T):
                        dve.wait_ge(op_mm, b * T + t + 1)
                        nc.vector.tensor_tensor(rows(b, t), rows(b, t), pm[m_bank[M_OUT + t]][:, 0:D],
                                                ALU.add).then_inc(x1_ok, 1)

                def attention(b):
                    def reads_xn(e, b):
                        wait(e, LN[2]["tr"], b * KD)
                        wait(e, xn3_st, 16 * b * T)

                    ln_vector(dve, 1, b, lambda e, b: e.wait_ge(x1_ok, b * T + T), reads_xn)
                    dve.wait_ge(c_mm, b + 1)
                    wait(dve, fill_ok, b * T)
                    nc.vector.tensor_scalar(neg_c[:], pa[a_bank[A_C]][:, 0:T], -1.0, neg_c0[:], ALU.mult,
                                            ALU.add).then_inc(c_ok, 1)

                    def pick(q):
                        dve.wait_ge(fill_ok, b * T + q + 1)
                        dve.wait_ge(inv_ok, b * T + q + 1)
                        for c, (lo, hi) in enumerate(CHUNKS):
                            dve.wait_ge(s_mm, b * 4 * T + 4 * q + c + 1)
                            take_wait()
                            nc.vector.copy_predicated(sim[:, q % 2, lo:hi], mask[:, q % 2, lo:hi],
                                                      pa[a_bank[A_S[q] + c]][:, 0:hi - lo]).then_inc(pick_ok, 1)
                        dve.wait_ge(pick_ok, b * 4 * T + 4 * q + 4)
                        nc.vector.reduce_max(row_max[:, q % 2:q % 2 + 1], sim[:, q % 2, :], AX_X).then_inc(max_ok, 1)
                        dve.wait_ge(max_ok, b * T + q + 1)
                        nc.vector.tensor_scalar(row_max[:, q % 2:q % 2 + 1], row_max[:, q % 2:q % 2 + 1], -1.0, None,
                                                ALU.mult).then_inc(nmax_ok, 1)

                    pick(0)
                    for q in range(T):
                        if q + 1 < T:
                            pick(q + 1)
                        dve.wait_ge(exp_ok, b * T + q + 1)
                        nc.vector.reciprocal(row_inv[:, q % 2:q % 2 + 1], row_sum[:, q % 2:q % 2 + 1]).then_inc(rinv_ok, 1)
                        dve.wait_ge(at_mm, b * T + q + 1)
                        wait(dve, o_mm, b * T + q)
                        nc.vector.tensor_copy(attT[:], pa[a_bank[A_AT[q]]][:, 0:D].rearrange(
                            "p (k m) -> p k m", k=KD)).then_inc(at_ok, 1)
                        dve.wait_ge(o_mm, b * T + q + 1)
                        dve.wait_ge(xc_ok, b * T + q + 1)
                        nc.vector.tensor_tensor(rows(b, q), rows(b, q), pa[a_bank[A_O[q]]][:, 0:D],
                                                ALU.add).then_inc(x2_ok, 1)
                    ln_vector(dve, 2, b, lambda e, b: e.wait_ge(x2_ok, b * T + T),
                              lambda e, b: e.wait_ge(LN[1]["tr"], (b + 1) * KD))
                    dve.wait_ge(r_mm, b + 1)
                    nc.vector.tensor_copy(scores[:, at(b * T, T), :], pa[a_bank[A_R]][:, 0:T * E].rearrange(
                        "p (t e) -> p t e", e=E)).then_inc(r_ok, 1)

                def body(b):
                    mamba_in(b)
                    scan(b)
                    attention(b)

                body(0)
                with dve.Fori(1, B) as b:
                    body(b)

            @block.tensor
            def _(pe):
                pe.wait_ge(id_ok, 1)
                pe.wait_ge(wa_ld, 16 * 9)
                pe.wait_ge(bias_b, 2 * KD)
                for k in range(KD):
                    for out, lhs, rhs in ((pa[0], wq, wk), (pa[1], wv, wo)):
                        for e in range(KD):
                            nc.tensor.matmul(out[:, k * D:(k + 1) * D], lhs[:, e, k * P:(k + 1) * P], rhs[:, e, :],
                                             start=e == 0, stop=e == KD - 1)
                for e in range(KD):
                    nc.tensor.matmul(pm[0][:, 0:D], bv_b[:, e, :], wo[:, e, :], start=e == 0, stop=False)
                nc.tensor.matmul(pm[0][:, 0:D], ones[0:1, :], bo_row[:], start=False, stop=True)
                for k in range(KD):
                    for col, w, v in ((D + k, wq, 1), (D + KD + k, wk, 0)):
                        for e in range(KD):
                            nc.tensor.matmul(pm[0][:, col:col + 1], w[:, e, k * P:(k + 1) * P], b_qkv[:, v, e:e + 1],
                                             start=e == 0, stop=e == KD - 1)
                col = D + 2 * KD
                for e in range(KD):
                    last = nc.tensor.matmul(pm[0][:, col:col + 1], bk_b[:, e, :], b_qkv[:, 0, e:e + 1],
                                            start=e == 0, stop=e == KD - 1)
                last.then_inc(setup_mm, 1)
                pe.wait_ge(setup_ok, 6)
                pe.wait_ge(w_ld, 16 * 9)

                def mamba_in(b):
                    ln_transpose(pe, 0, b, m_uses, m_bank, 0, pm)
                    for j in range(2 * KI):
                        bank_free(pe, m_uses, m_bank, M_IP + j, b)
                        pe.wait_ge(LN[0]["xT"], b * KD + KD)
                        for k in range(KD):
                            last = nc.tensor.matmul(pm[m_bank[M_IP + j]][:], w_in[:, k, j * P:(j + 1) * P], xnT_m[:, k, :],
                                                    start=k == 0, stop=k == KD - 1)
                        last.then_inc(ip_mm, 1)
                    bank_free(pe, m_uses, m_bank, M_B, b)
                    pe.wait_ge(silu_ok, b * KI + KI)
                    for k in range(KI):
                        last = nc.tensor.matmul(pm[m_bank[M_B]][0:NST, :], w_b[:, k, :], xs[:, k, :],
                                                start=k == 0, stop=k == KI - 1)
                    last.then_inc(b_mm, 1)
                    for j in range(KI):
                        bank_free(pe, m_uses, m_bank, M_DT + j, b)
                        for k in range(KI):
                            last = nc.tensor.matmul(pm[m_bank[M_DT + j]][:], w_dt[:, k, j * P:(j + 1) * P], xs[:, k, :],
                                                    start=k == 0, stop=k == KI - 1)
                        last.then_inc(dt_mm, 1)

                def state_sum(b):
                    for j in range(KI):
                        wait(pe, y_ok, b * KI + j - 1)
                        for n in range(NST):
                            i = j * NST + n
                            pe.wait_ge(scan_ok, b * KI * NST + i + 1)
                            nc.tensor.matmul(ysum[j % 2][:], ident[:], h[:, i % 4, :], start=n == 0,
                                             stop=n == NST - 1).then_inc(sum_ok, 1)
                    pe.wait_ge(yg_ok, b * KI + KI)
                    for t in range(T):
                        bank_free(pe, m_uses, m_bank, M_OUT + t, b)
                        for j in range(KI):
                            last = nc.tensor.matmul(pm[m_bank[M_OUT + t]][:, 0:D], gate[:, j, t * P:(t + 1) * P],
                                                    w_out[:, j, :], start=j == 0, stop=j == KI - 1)
                        last.then_inc(op_mm, 1)

                def attention(b):
                    ln_transpose(pe, 1, b, a_uses, a_bank, 0, pa)
                    pe.wait_ge(LN[1]["xT"], b * KD + KD)
                    for m in range(KD):
                        bank_free(pe, a_uses, a_bank, A_Q + m, b)
                        for k in range(KD):
                            last = nc.tensor.matmul(pa[a_bank[A_Q + m]][:], w_qk[:, k, m * P:(m + 1) * P], xnT_a[:, k, :],
                                                    start=k == 0, stop=k == KD - 1)
                        last.then_inc(q_mm, 1)
                    bank_free(pe, a_uses, a_bank, A_C, b)
                    for t in range(T):
                        for k in range(KD):
                            last = nc.tensor.matmul(pa[a_bank[A_C]][:, t:t + 1], xnT_a[:, k, t * P:(t + 1) * P],
                                                    wq_bk[:, k:k + 1], start=k == 0, stop=k == KD - 1)
                    last.then_inc(c_mm, 1)
                    pe.wait_ge(q_ok, b * KD + KD)
                    pe.wait_ge(ctx_ld, 48 * (b + 1))

                    def score(q):
                        for c, (lo, hi) in enumerate(CHUNKS):
                            bank_free(pe, a_uses, a_bank, A_S[q] + c, b)
                            for k in range(KD):
                                last = nc.tensor.matmul(pa[a_bank[A_S[q] + c]][:, 0:hi - lo], qT[:, k, q * P:(q + 1) * P],
                                                        ctx_t[:, k, lo:hi], start=k == 0, stop=k == KD - 1)
                            last.then_inc(s_mm, 1)

                    score(0)
                    for q in range(T):
                        if q + 1 < T:
                            score(q + 1)
                        pe.wait_ge(exp_ok, b * T + q + 1)
                        for g in range(n_pt):
                            bank_free(pe, a_uses, a_bank, A_PT[q] + g, b)
                            for c in range(4 * g, min(4 * g + 4, KC)):
                                n = P if c < KC - 1 else S2_LAST
                                last = nc.tensor.transpose(pa[a_bank[A_PT[q] + g]][0:n, (c - 4 * g) * P:(c - 4 * g + 1) * P],
                                                           sim[:, q % 2, c * P:c * P + n], ident[:])
                            last.then_inc(pt_mm, 1)
                        bank_free(pe, a_uses, a_bank, A_AV[q], b)
                        pe.wait_ge(pt_ok, b * n_pt * T + n_pt * (q + 1))
                        for c in range(KC):
                            n = P if c < KC - 1 else S2_LAST
                            last = nc.tensor.matmul(pa[a_bank[A_AV[q]]][:, 0:D], pT[0:n, c, :], ctx_n[0:n, c, :],
                                                    start=c == 0, stop=c == KC - 1)
                        last.then_inc(av_mm, 1)
                        bank_free(pe, a_uses, a_bank, A_AT[q], b)
                        pe.wait_ge(av_ok, b * T + q + 1)
                        for k in range(KD):
                            last = nc.tensor.transpose(pa[a_bank[A_AT[q]]][:, k * P:(k + 1) * P], att[:, k * P:(k + 1) * P],
                                                       ident[:])
                        last.then_inc(at_mm, 1)
                        bank_free(pe, a_uses, a_bank, A_O[q], b)
                        pe.wait_ge(at_ok, b * T + q + 1)
                        for k in range(KD):
                            last = nc.tensor.matmul(pa[a_bank[A_O[q]]][:, 0:D], attT[:, k, :], w_vo[:, k, :],
                                                    start=k == 0, stop=k == KD - 1)
                        last.then_inc(o_mm, 1)
                    ln_transpose(pe, 2, b, a_uses, a_bank, A_L3, pa)
                    bank_free(pe, a_uses, a_bank, A_R, b)
                    pe.wait_ge(LN[2]["xT"], b * KD + KD)
                    for t in range(T):
                        for k in range(KD):
                            last = nc.tensor.matmul(pa[a_bank[A_R]][:, t * E:(t + 1) * E], xnT_a[:, k, t * P:(t + 1) * P],
                                                    w_g[:, k, :], start=k == 0, stop=k == KD - 1)
                    last.then_inc(r_mm, 1)

                def body(b):
                    mamba_in(b)
                    state_sum(b)
                    attention(b)

                body(0)
                with pe.Fori(1, B) as b:
                    body(b)


def routed_ffn_phase(nc, io, dims, env, sem, buf):
    B, S, D, S2, DI, NST, TAPS, E, HF = dims
    KD, G, KH, H_LAST, HH, NT = (env[k] for k in ("KD", "G", "KH", "H_LAST", "HH", "NT"))
    x_all, ident, scores = env["x_all"], env["ident"], env["scores"]
    tok_sorted, ffn_sorted, xn3_dram = env["tok_sorted"], env["ffn_sorted"], env["xn3_dram"]
    LOOP = NT + 2

    with ExitStack() as ctx:
        def sb(name, shape, dt=F32):
            return buf(ctx, name, shape, dt)

        w1 = sb("w1", [P, E * KD * HF])
        w2 = sb("w2", [P, E * KD * HF])
        w3 = sb("w3", [P, E * KH * D])
        xn = sb("xn", [P, G, D])
        tok = sb("tok", [P, 2, D])
        tokT = sb("tokT", [P, 2, KD, P])
        act_ = sb("act_", [P, HF])
        hid = sb("hid", [P, 2, HF])
        hidT = sb("hidT", [P, KH, P])
        y_sb = sb("y_sb", [P, 2, D])
        tri = sb("tri", [P, P])
        ones = sb("ones2", [P, P])
        iot = sb("iot", [P, 64], I32)
        rev = sb("rev", [P, E])
        tile_id = sb("tile_id", [1, LOOP])
        w_top = sb("w_top", [P, 2, G])
        eq = sb("eq", [P, G, E])
        oh = sb("oh", [P, 2, G, E])
        rest = sb("rest", [P, G, E])
        km = sb("km", [P, G])
        both = sb("both", [P, G, E])
        tot = sb("tot", [P, E, G])
        seg = sb("seg", [P, E, G])
        inc = sb("inc", [P, E, G])
        slot = sb("slot", [P, G, E])
        pos_f = sb("pos_f", [P, 2, G])
        pos = sb("pos", [P, 2, G], U32)
        cnt_i = sb("cnt_i", [P, E], I32)
        cnt_f = sb("cnt_f", [P, E])
        tiles = sb("tiles", [P, E])
        tend = sb("tend", [P, E])
        ge = sb("ge", [1, LOOP, E])
        tile_e = sb("tile_e", [1, LOOP])
        tile_expert = sb("tile_expert", [1, LOOP], I32)
        y_one = xn
        y_two = sb("y_two", [P, 4, D])

        def ps(name, n=512):
            return ctx.enter_context(nc.psum_tensor(name, [P, n], F32))

        ps_g = [ps("ps_g0"), ps("ps_g1")]
        ps_u = [ps("ps_u0"), ps("ps_u1")]
        ps_x, ps_h0, ps_h1, ps_y = ps("ps_x"), ps("ps_h0"), ps("ps_h1"), ps("ps_y")

        wts_ld, xn_ld, iota_ok, tri_zero, tri_ok, one_ok = (
            sem(n) for n in ("wts_ld", "xn_ld", "iota_ok", "tri_zero", "tri_ok", "one_ok"))
        step, mask_ok, rank_mm, pos_ok2, tab_ok = (sem(n) for n in ("step", "mask_ok", "rank_mm", "pos_ok2", "tab_ok"))
        sorted_st, out_st = sem("sorted_st"), sem("out_st")
        tok_ld, y_st = [sem("tok_ld0"), sem("tok_ld1")], [sem("y_st0"), sem("y_st1")]

        def so_far(i, p):
            return i * 8 + 16 - 8 * p

        x_mm, xT_ok, gu_mm, silu2_ok, hid_ok, h_mm, hT_ok0, hT_ok1, y_mm, y_ok2 = (
            sem(n) for n in ("x_mm", "xT_ok", "gu_mm", "silu2_ok", "hid_ok", "h_mm", "hT_ok0", "hT_ok1", "y_mm", "y_ok2"))
        one_ld, two_ld, comb, comb_ok = sem("one_ld"), [sem("two_ld0"), sem("two_ld1")], sem("comb"), sem("comb_ok")
        pad_done = sem("pad_done")

        with nc.Block() as block:

            @block.sync
            def _(sp):
                sp.dma_start(xn[:], xn3_dram.rearrange("(g p) d -> p g d", p=P)).then_inc(xn_ld, 16)
                full = (KH - 1) * P
                for e in range(E):
                    for dst, src in ((w1, io["w1T"]), (w2, io["w2T"])):
                        sp.dma_start(dst[:, e * KD * HF:(e + 1) * KD * HF].rearrange("p (k h) -> p k h", k=KD),
                                     src[e].rearrange("(k p) h -> p k h", p=P)).then_inc(wts_ld, 16)
                    w3e = w3[:, e * KH * D:(e + 1) * KH * D].rearrange("p (c d) -> p c d", c=KH)
                    sp.dma_start(w3e[:, 0:KH - 1, :], io["w3T"][e, 0:full, :].rearrange("(c p) d -> p c d", p=P)).then_inc(wts_ld, 16)
                    sp.dma_start(w3e[0:H_LAST, KH - 1, :], io["w3T"][e, full:HF, :]).then_inc(wts_ld, 16)
                sp.wait_ge(sorted_st, 16 * 2 * G)

                def load(i, p):
                    wait(sp, x_mm, i - 1)
                    sp.dma_start(tok[:, p, :], tok_sorted[at(i * P, P), :]).then_inc(tok_ld[p], 16)

                def store(i, p):
                    sp.wait_ge(y_ok2, i + 1)
                    sp.dma_start(ffn_sorted[at(i * P, P), :], y_sb[:, p, :]).then_inc(y_st[p], 16)

                load(0, 0)
                load(1, 1)

                def pair(i):
                    for k in range(2):
                        load(i + k + 2, k)
                        store(i + k, k)

                pair(0)
                with sp.Fori(2, NT - 3, 2) as i:
                    pair(i)
                load(NT - 1, 0)
                store(NT - 3, 0)
                store(NT - 2, 1)
                store(NT - 1, 0)
                out = io["out"].rearrange("(g p) d -> p g d", p=P)
                for g in range(0, G, 4):
                    sp.wait_ge(comb_ok, g + 4)
                    sp.dma_start(out[:, g:g + 4, :], x_all[:, g:g + 4, :]).then_inc(out_st, 16)
                sp.wait_ge(out_st, 16 * (G // 4))

            @block.gpsimd
            def _(pool):
                nc.gpsimd.iota(iot[:], pattern=[[1, 64]], base=0, channel_multiplier=0).then_inc(iota_ok, 1)
                nc.gpsimd.memset(tri[:], 1.0).then_inc(tri_zero, 1)
                nc.gpsimd.memset(ones[:], 1.0).then_inc(one_ok, 1)
                nc.gpsimd.memset(seg[:], 1.0).then_inc(one_ok, 1)
                pool.wait_ge(one_ok, 2)
                nc.gpsimd.memset(seg[:, :, 0:1], 0.0).then_inc(one_ok, 1)
                pool.wait_ge(tri_zero, 1)
                nc.gpsimd.affine_select(out=tri[:], in_=tri[:], compare_op=ALU.is_gt, fill=0.0, base=0,
                                        pattern=[[1, P]], channel_multiplier=-1).then_inc(tri_ok, 1)
                pool.wait_ge(xn_ld, 16)
                pool.wait_ge(pos_ok2, 1)
                for g in range(G):
                    for k in range(2):
                        pool.indirect_dma_start(tok_sorted, bass.IndirectOffsetOnAxis(ap=pos[:, k, g:g + 1], axis=0),
                                                xn[:, g, :], None).then_inc(sorted_st, 16)
                for p in range(2):
                    pool.wait_ge(y_st[p], so_far(NT - 1 if (NT - 1) % 2 == p else NT - 2, p))
                pool.wait_ge(sorted_st, 16 * 2 * G)
                for g in range(G):
                    pool.indirect_dma_start(y_one[:, g, :], None, ffn_sorted,
                                            bass.IndirectOffsetOnAxis(ap=pos[:, 0, g:g + 1], axis=0)).then_inc(one_ld, 16)
                for g in range(G):
                    wait(pool, comb_ok, g - 1)
                    pool.indirect_dma_start(y_two[:, g % 2, :], None, ffn_sorted,
                                            bass.IndirectOffsetOnAxis(ap=pos[:, 1, g:g + 1], axis=0)).then_inc(two_ld[g % 2], 16)

            @block.scalar
            def _(act):
                def evacuate_tokens(i, p):
                    act.wait_ge(x_mm, i + 1)
                    wait(act, gu_mm, 2 * (i - 1))
                    nc.scalar.copy(tokT[:, p, :, :], ps_x[:, 0:D].rearrange("p (k m) -> p k m", k=KD)).then_inc(xT_ok, 1)

                def silu(i):
                    for c in range(2):
                        act.wait_ge(gu_mm, 2 * i + c + 1)
                        wait(act, hid_ok, 2 * (i - 1) + c + 1)
                        nc.scalar.activation(act_[:, c * HH:(c + 1) * HH], ps_g[c][:, 0:HH], ACT.Silu).then_inc(silu2_ok, 1)

                def evacuate_hidden(i):
                    act.wait_ge(h_mm, 2 * i + 1)
                    wait(act, y_mm, i)
                    nc.scalar.copy(hidT[:, 0:4, :], ps_h0[:].rearrange("p (c m) -> p c m", c=4)).then_inc(hT_ok0, 1)

                evacuate_tokens(0, 0)
                silu(0)
                evacuate_tokens(1, 1)

                def pair(i):
                    for k in range(2):
                        silu(i + k)
                        evacuate_tokens(i + k + 1, k)
                        evacuate_hidden(i + k - 1)

                pair(1)
                with act.Fori(3, NT - 2, 2) as i:
                    pair(i)
                silu(NT - 2)
                evacuate_tokens(NT - 1, 0)
                evacuate_hidden(NT - 3)
                silu(NT - 1)
                evacuate_hidden(NT - 2)
                evacuate_hidden(NT - 1)

            @block.vector
            def _(dve):
                count = [0]

                def chain(ins):
                    ins.then_inc(step, 1)
                    count[0] += 1
                    dve.wait_ge(step, count[0])

                def over_e(t):
                    return t.unsqueeze(2).to_broadcast([P, G, E])

                def over_g(t):
                    return t.unsqueeze(1).to_broadcast([P, G, E])

                dve.wait_ge(iota_ok, 1)
                chain(nc.vector.tensor_copy(cnt_f[:], iot[:, 0:E]))
                chain(nc.vector.tensor_scalar(rev[:], cnt_f[:], -1.0, float(E), ALU.mult, ALU.add))
                chain(nc.vector.tensor_copy(tile_id[:], iot[0:1, 0:LOOP]))
                chain(nc.vector.tensor_copy(rest[:], scores[:]))
                for k in range(2):
                    chain(nc.vector.reduce_max(w_top[:, k, :], rest[:], AX_X))
                    chain(nc.vector.tensor_tensor(eq[:], rest[:], over_e(w_top[:, k, :]), ALU.is_equal))
                    chain(nc.vector.tensor_tensor(eq[:], eq[:], over_g(rev[:]), ALU.mult))
                    chain(nc.vector.reduce_max(km[:], eq[:], AX_X))
                    chain(nc.vector.tensor_tensor(oh[:, k, :, :], eq[:], over_e(km[:]), ALU.is_equal))
                    if k == 0:
                        chain(nc.vector.scalar_tensor_tensor(out=rest[:], in0=oh[:, 0, :, :], scalar=NEG_HUGE, in1=rest[:],
                                                             op0=ALU.mult, op1=ALU.add))
                nc.vector.tensor_tensor(both[:], oh[:, 0, :, :], oh[:, 1, :, :], ALU.add).then_inc(mask_ok, 1)
                dve.wait_ge(rank_mm, 1)
                dve.wait_ge(one_ok, 3)
                chain(nc.vector.tensor_copy(tot[:], ps_u[0][:, 0:G * E].rearrange("p (g e) -> p e g", e=E)))
                flat = "p e g -> p (e g)"
                chain(nc.vector.tensor_tensor_scan(inc[:].rearrange(flat), seg[:].rearrange(flat), tot[:].rearrange(flat),
                                                   0.0, ALU.mult, ALU.add))
                chain(nc.vector.tensor_tensor(tot[:], inc[:], tot[:], ALU.subtract))
                chain(nc.vector.tensor_tensor(slot[:], ps_g[0][:, 0:G * E].rearrange("p (g e) -> p g e", e=E),
                                              tot[:].rearrange("p e g -> p g e"), ALU.add))
                chain(nc.vector.tensor_copy(cnt_f[:], inc[:, :, G - 1]))
                chain(nc.vector.tensor_scalar(cnt_f[:], cnt_f[:], float(P - 1), None, ALU.add))
                chain(nc.vector.tensor_copy(cnt_i[:], cnt_f[:]))
                chain(nc.vector.tensor_scalar(cnt_i[:], cnt_i[:], P.bit_length() - 1, None, ALU.arith_shift_right))
                chain(nc.vector.tensor_copy(tiles[:], cnt_i[:]))
                chain(nc.vector.tensor_tensor_scan(tend[:], ones[:, 0:E], tiles[:], 0.0, ALU.mult, ALU.add))
                chain(nc.vector.tensor_tensor(tiles[:], tend[:], tiles[:], ALU.subtract))
                chain(nc.vector.tensor_scalar(tiles[:], tiles[:], float(P), None, ALU.mult))
                chain(nc.vector.tensor_tensor(slot[:], slot[:], over_g(tiles[:]), ALU.add))
                for k in range(2):
                    chain(nc.vector.tensor_tensor(eq[:], oh[:, k, :, :], slot[:], ALU.mult))
                    chain(nc.vector.reduce_sum(pos_f[:, k, :], eq[:], AX_X))
                nc.vector.tensor_copy(pos[:], pos_f[:]).then_inc(pos_ok2, 1)
                shape = [1, LOOP, E]
                chain(nc.vector.tensor_tensor(ge[:], tile_id[:].unsqueeze(2).to_broadcast(shape),
                                              tend[0:1, :].unsqueeze(1).to_broadcast(shape), ALU.is_ge))
                chain(nc.vector.reduce_sum(tile_e[:], ge[:], AX_X))
                chain(nc.vector.tensor_scalar(tile_e[:], tile_e[:], float(E - 1), None, ALU.min))
                nc.vector.tensor_copy(tile_expert[:], tile_e[:]).then_inc(tab_ok, 1)

                def multiply(i, p):
                    for c in range(2):
                        dve.wait_ge(silu2_ok, 2 * i + c + 1)
                        wait(dve, h_mm, 2 * (i - 1))
                        nc.vector.tensor_tensor(hid[:, p, c * HH:(c + 1) * HH], act_[:, c * HH:(c + 1) * HH],
                                                ps_u[c][:, 0:HH], ALU.mult).then_inc(hid_ok, 1)

                def evacuate(i, p):
                    dve.wait_ge(h_mm, 2 * i + 2)
                    wait(dve, y_mm, i)
                    nc.vector.tensor_copy(hidT[:, 4:KH - 1, :], ps_h1[:, 0:(KH - 5) * P].rearrange(
                        "p (c m) -> p c m", m=P)).then_inc(hT_ok1, 1)
                    nc.vector.tensor_copy(hidT[0:H_LAST, KH - 1, :], ps_h1[0:H_LAST, (KH - 5) * P:(KH - 4) * P]).then_inc(hT_ok1, 1)
                    dve.wait_ge(y_mm, i + 1)
                    wait(dve, y_st[p], so_far(i - 2, p))
                    nc.vector.tensor_copy(y_sb[:, p, :], ps_y[:, 0:D]).then_inc(y_ok2, 1)

                def pair(i):
                    for k in range(2):
                        multiply(i + k, 1 - k)
                        evacuate(i + k - 1, k)

                multiply(0, 0)
                pair(1)
                with dve.Fori(3, NT, 2) as i:
                    pair(i)
                evacuate(NT - 1, 0)
                dve.wait_ge(one_ld, 16 * G)
                for g in range(G):
                    nc.vector.scalar_tensor_tensor(out=x_all[:, g, :], in0=y_one[:, g, :], scalar=w_top[:, 0, g:g + 1],
                                                   in1=x_all[:, g, :], op0=ALU.mult, op1=ALU.add).then_inc(comb, 1)
                for g in range(G):
                    dve.wait_ge(comb, g + 1)
                    dve.wait_ge(two_ld[g % 2], 16 * (g // 2 + 1))
                    nc.vector.scalar_tensor_tensor(out=x_all[:, g, :], in0=y_two[:, g % 2, :], scalar=w_top[:, 1, g:g + 1],
                                                   in1=x_all[:, g, :], op0=ALU.mult, op1=ALU.add).then_inc(comb_ok, 1)

            @block.tensor
            def _(pe):
                pe.wait_ge(mask_ok, 1)
                pe.wait_ge(tri_ok, 1)
                pe.wait_ge(one_ok, 3)
                flat = "p g e -> p (g e)"
                nc.tensor.matmul(ps_g[0][:, 0:G * E], tri[:], both[:].rearrange(flat), start=True, stop=True)
                nc.tensor.matmul(ps_u[0][:, 0:G * E], ones[:], both[:].rearrange(flat), start=True, stop=True).then_inc(rank_mm, 1)
                pe.wait_ge(tab_ok, 1)
                pe.wait_ge(wts_ld, 16 * 4 * E)

                def expert(i):
                    return pe.value_load(tile_expert[0:1, at(i)], min_val=0, max_val=E - 1)

                def transpose_tokens(i, p):
                    pe.wait_ge(tok_ld[p], so_far(i, p))
                    wait(pe, xT_ok, i)
                    for k in range(KD):
                        last = nc.tensor.transpose(ps_x[:, k * P:(k + 1) * P], tok[:, p, k * P:(k + 1) * P], ident[:])
                    last.then_inc(x_mm, 1)

                def gate_up(i, p):
                    e = expert(i)
                    pe.wait_ge(xT_ok, i + 1)
                    for c in range(2):
                        wait(pe, hid_ok, 2 * (i - 1) + c + 1)
                        for out, w in ((ps_g[c], w1), (ps_u[c], w2)):
                            for k in range(KD):
                                last = nc.tensor.matmul(out[:, 0:HH], tokT[:, p, k, :],
                                                        w[:, at(e * (KD * HF) + (k * HF + c * HH), HH)],
                                                        start=k == 0, stop=k == KD - 1)
                        last.then_inc(gu_mm, 1)

                def down(i, p):
                    e = expert(i)
                    pe.wait_ge(hid_ok, 2 * i + 2)
                    wait(pe, hT_ok0, i)
                    for c in range(4):
                        last = nc.tensor.transpose(ps_h0[:, c * P:(c + 1) * P], hid[:, p, c * P:(c + 1) * P], ident[:])
                    last.then_inc(h_mm, 1)
                    wait(pe, hT_ok1, 2 * i)
                    for c in range(4, KH):
                        n = P if c < KH - 1 else H_LAST
                        last = nc.tensor.transpose(ps_h1[0:n, (c - 4) * P:(c - 3) * P], hid[:, p, c * P:c * P + n], ident[:])
                    last.then_inc(h_mm, 1)
                    wait(pe, y_ok2, i)
                    pe.wait_ge(hT_ok0, i + 1)
                    pe.wait_ge(hT_ok1, 2 * i + 2)
                    for c in range(KH):
                        n = P if c < KH - 1 else H_LAST
                        last = nc.tensor.matmul(ps_y[:, 0:D], hidT[0:n, c, :], w3[0:n, at(e * (KH * D) + c * D, D)],
                                                start=c == 0, stop=c == KH - 1)
                    last.then_inc(y_mm, 1)

                transpose_tokens(0, 0)
                gate_up(0, 0)
                transpose_tokens(1, 1)

                def pair(i):
                    for k in range(2):
                        gate_up(i + k, 1 - k)
                        transpose_tokens(i + k + 1, k)
                        down(i + k - 1, k)

                pair(1)
                with pe.Fori(3, NT - 2, 2) as i:
                    pair(i)
                gate_up(NT - 2, 1)
                transpose_tokens(NT - 1, 0)
                down(NT - 3, 0)
                gate_up(NT - 1, 0)
                down(NT - 2, 1)
                down(NT - 1, 0)


def kernel(x, ctx_1024, mask_BxSxS2_bk1, L0_attn_W_in, L0_attn_W_conv, L0_attn_b_conv, L0_attn_W_x, L0_attn_W_dt,
           L0_attn_b_dt, L0_attn_W_out, L0_attn_A_log, L0_attn_D, L0_xattn_Wq, L0_xattn_bq, L0_xattn_Wk, L0_xattn_bk,
           L0_xattn_Wv, L0_xattn_bv, L0_xattn_Wo, L0_xattn_bo, L0_ffn_Wg, L0_ffn_W1, L0_ffn_W2, L0_ffn_W3):
    import numpy as np
    from concourse import bacc
    from concourse.bass_utils import run_bass_kernel_spmd

    def lay(a, *axes):
        a = np.asarray(a)
        return np.ascontiguousarray(a.transpose(axes) if axes else a)

    def columns(a):
        return lay(np.asarray(a).reshape(-1, P), 1, 0)

    B, S, D = x.shape
    S2 = ctx_1024.shape[1]
    DI, NST = L0_attn_A_log.shape
    TAPS = L0_attn_W_conv.shape[2]
    E, HF, _ = L0_ffn_W1.shape
    arrays = {
        "x": lay(x).reshape(B * S, D),
        "ctx": lay(ctx_1024),
        "ctxT": lay(ctx_1024, 0, 2, 1),
        "mask": lay(mask_BxSxS2_bk1),
        "w_inT": lay(L0_attn_W_in, 1, 0),
        "w_conv": lay(L0_attn_W_conv).reshape(DI, TAPS),
        "b_conv": columns(L0_attn_b_conv),
        "w_bT": lay(np.asarray(L0_attn_W_x)[NST:2 * NST], 1, 0),
        "w_dtT": lay(L0_attn_W_dt, 1, 0),
        "b_dt": columns(L0_attn_b_dt),
        "w_outT": lay(L0_attn_W_out, 1, 0),
        "a_log": lay(L0_attn_A_log),
        "d_skip": columns(L0_attn_D),
        "wq": lay(L0_xattn_Wq), "wk": lay(L0_xattn_Wk), "wv": lay(L0_xattn_Wv),
        "bq": columns(L0_xattn_bq), "bk": columns(L0_xattn_bk), "bv": columns(L0_xattn_bv), "bo": lay(L0_xattn_bo),
        "woT": lay(L0_xattn_Wo, 1, 0),
        "w_gT": lay(L0_ffn_Wg, 1, 0),
        "w1T": lay(L0_ffn_W1, 0, 2, 1),
        "w2T": lay(L0_ffn_W2, 0, 2, 1),
        "w3T": lay(L0_ffn_W3, 0, 2, 1),
    }
    nc = bacc.Bacc("TRN2", target_bir_lowering=False, num_devices=1)
    io = {k: nc.dram_tensor(f"in_{k}", a.shape, mybir.dt.from_np(a.dtype), kind="ExternalInput").ap()
          for k, a in arrays.items()}
    io["out"] = nc.dram_tensor("out", [B * S, D], F32, kind="ExternalOutput").ap()
    decoder_kernel(nc, io, (B, S, D, S2, DI, NST, TAPS, E, HF))
    result = run_bass_kernel_spmd(nc, [{f"in_{k}": a for k, a in arrays.items()}], core_ids=[0])
    return result.results[0]["out"].reshape(B, S, D)
```

```python
from contextlib import ExitStack

import concourse.bass as bass
from concourse import mybir

F32 = mybir.dt.float32
I32 = mybir.dt.int32
U32 = mybir.dt.uint32
U8 = mybir.dt.uint8
ACT = mybir.ActivationFunctionType
ALU = mybir.AluOpType
AX_X = mybir.AxisListType.X

P = 128
EPS = 1e-5
MASKED = -1000000000.0
NEG_HUGE = -3.0e38


def at(i, n=1):
    return bass.ds(i, n)


def wait(eng, sem, value):
    if isinstance(value, int) and value <= 0:
        return
    eng.wait_ge(sem, value)


def decoder_kernel(nc, io, dims):
    B, S, D, S2, DI, NST, TAPS, E, HF = dims
    KD = D // P
    KI = DI // P
    T = S // P
    G = B * T
    KC = -(-S2 // P)
    S2_LAST = S2 - (KC - 1) * P
    CH = -(-S2 // 4)
    CHUNKS = [(c * CH, min(S2, (c + 1) * CH)) for c in range(4)]
    KH = -(-HF // P)
    H_LAST = HF - (KH - 1) * P
    HH = HF // 2
    NT = (2 * B * S + E * (P - 1)) // P

    tok_sorted = nc.dram_tensor("tok_sorted", [NT * P, D], F32).ap()
    ffn_sorted = nc.dram_tensor("ffn_sorted", [NT * P, D], F32).ap()
    xn3_dram = nc.dram_tensor("xn3_dram", [G * P, D], F32).ap()
    b_dram = nc.dram_tensor("b_dram", [B, NST * S], F32).ap()

    top = ExitStack()
    with top:
        def sem(name):
            return top.enter_context(nc.semaphore(name))

        def buf(ctx, name, shape, dt=F32):
            return ctx.enter_context(nc.sbuf_tensor(name, shape, dt))

        zeros = buf(top, "zeros", [P, D])
        x_all = buf(top, "x_all", [P, G, D])
        ident = buf(top, "ident", [P, P])
        scores = buf(top, "scores", [P, G, E])

        mixer_phase(nc, io, dims, locals(), sem, buf)
        routed_ffn_phase(nc, io, dims, locals(), sem, buf)


def mixer_phase(nc, io, dims, env, sem, buf):
    B, S, D, S2, DI, NST, TAPS, E, HF = dims
    KD, KI, T, KC = env["KD"], env["KI"], env["T"], env["KC"]
    S2_LAST, CHUNKS = env["S2_LAST"], env["CHUNKS"]
    x_all, ident, scores = env["x_all"], env["ident"], env["scores"]
    xn3_dram, b_dram, tok_sorted, zeros, NT = (env[k] for k in ("xn3_dram", "b_dram", "tok_sorted", "zeros", "NT"))
    STEPS = KI * NST
    NPT = -(-KC // 4)
    NB = 4
    HS = 8
    PAIRS = STEPS // 2
    QCH = len(CHUNKS)

    def q_step(q):
        return 15 + 7 * q

    def dt_step(j):
        return (52, 5, 18, 35)[j]

    def o_step(q):
        return q_step(q) + (20 if q == 0 else 19)

    with ExitStack() as ctx:
        def sb(name, shape, dt=F32):
            return buf(ctx, name, shape, dt)

        def ps(name):
            return ctx.enter_context(nc.psum_tensor(name, [P, 512], F32))

        w_in = sb("w_in", [P, KD, 2 * DI])
        w_dt = sb("w_dt", [P, KI, DI])
        w_b = sb("w_b", [P, KI, NST])
        w_out = sb("w_out", [P, KI, D])
        w_conv = sb("w_conv", [P, KI, TAPS])
        b_conv = sb("b_conv", [P, KI])
        b_dt = sb("b_dt", [P, KI])
        d_skip = sb("d_skip", [P, KI])
        a_neg = sb("a_neg", [P, KI, NST])
        w_qk = sb("w_qk", [P, KD, D])
        w_vo = sb("w_vo", [P, KD, D])
        bq_k = sb("bq_k", [P, KD])
        wq_bk = sb("wq_bk", [P, KD])
        neg_c0 = sb("neg_c0", [P, 1])
        c_vo = sb("c_vo", [P, D])
        w_g = sb("w_g", [P, KD, E])
        xn = sb("xn", [P, T, D])
        xnT_m = sb("xnT_m", [P, KD, S])
        xs = sb("xs", [P, 2 * KI, S])
        gate = sb("gate", [P, KI, S])
        dt_ = sb("dt_", [P, 2, S])
        dtx = sb("dtx", [P, 2, S])
        yg = sb("yg", [P, KI, S])
        sp_pos = sb("sp_pos", [P, S])
        b_row = sb("b_row", [NST, S])
        b_all = sb("b_all", [P, NST, S])
        u = sb("u", [P, 2, S])
        da = sb("da", [P, 2, S])
        h = sb("h", [P, HS, S])
        xnT_a = sb("xnT_a", [P, KD, S])
        neg_c = sb("neg_c", [P, T])
        ctx_n = sb("ctx_n", [P, KC, D])
        ctx_t = sb("ctx_t", [P, KD, S2])
        mask = sb("mask", [P, 2, -(-S2 // 4) * 4], U8)
        sim = sb("sim", [P, 2, S2])
        pT = sb("pT", [P, KC, P])
        row_max = sb("row_max", [P, T])
        row_sum = sb("row_sum", [P, T])
        row_inv = sb("row_inv", [P, T])
        attT = sb("attT", [P, KD, P])
        ln_buf = [(sb(f"ln_stat{i}", [P, T, 6]), sb(f"ln_mv{i}", [P, T, 2]), sb(f"ln_var{i}", [P, T]),
                   sb(f"ln_log{i}", [P, T]), sb(f"ln_r{i}", [P, T]), sb(f"ln_t{i}", [P, T])) for i in range(3)]
        wq, wk, wv, wo = (h[:, i, :].rearrange("p (k d) -> p k d", k=KD) for i in range(4))
        bk_b, bv_b = (u[:, i, 0:KD * P].rearrange("p (k m) -> p k m", k=KD) for i in range(2))
        b_qkv = sb("b_qkv", [P, 3, KD])
        scrap = sb("scrap", [P, 64])
        pool_scrap = sb("pool_scrap", [P, T])
        bo_row = sb("bo_row", [1, D])
        ones = sb("ones", [P, P])

        ysum = ps("ysum")
        pm = [ps("pm0"), ps("pm1")]
        pa = [ps("pa0"), ps("pa1")]
        pt = [ps("pt0"), ps("pt1")]
        pv = ps("pv")
        RES_BANKS = (pm[0], pm[1], pt[1], pv)
        CONV_BANKS = (pm[0], pm[1], pm[1], pm[0])
        DT_BANKS = (pm[0], pt[0], pm[0], pm[0])

        x_ld, w_ld, wa_ld, b_st, b_ld, ctx_ld, mask_ld, tok_st = (
            sem(n) for n in ("x_ld", "w_ld", "wa_ld", "b_st", "b_ld", "ctx_ld", "mask_ld", "tok_st"))
        zero_ok, id_zero, id_ok, ones_ok, a_exp, a_ok, bias_b, setup_mm, setup_ok = (
            sem(n) for n in ("zero_ok", "id_zero", "id_ok", "ones_ok", "a_exp", "a_ok", "bias_b", "setup_mm", "setup_ok"))
        ip_mm, res_mm, conv_step, silu_ok, b_mm, b_ev, res_ok, dt_mm, sp_step, pos_ok, dt_ok, dtx_ok = (
            sem(n) for n in ("ip_mm", "res_mm", "conv_step", "silu_ok", "b_mm", "b_ev", "res_ok", "dt_mm", "sp_step",
                             "pos_ok", "dt_ok", "dtx_ok"))
        da_ok, u_ok, scan_ok, pair_ok, sum_ok, y_ok, yg_ok, op_mm, x1_ok = (
            sem(n) for n in ("da_ok", "u_ok", "scan_ok", "pair_ok", "sum_ok", "y_ok", "yg_ok", "op_mm", "x1_ok"))
        q_mm, q_ok, c_mm, c_ok, s_mm, fill_ok, inv_ok, pick_ok, max_ok, nmax_ok, exp_ok, rinv_ok = (
            sem(n) for n in ("q_mm", "q_ok", "c_mm", "c_ok", "s_mm", "fill_ok", "inv_ok", "pick_ok", "max_ok",
                             "nmax_ok", "exp_ok", "rinv_ok"))
        pt_mm, pt_ok, av_mm, av_ok, o_mm, xc_ok, x2_ok, r_mm, r_ok = (
            sem(n) for n in ("pt_mm", "pt_ok", "av_mm", "av_ok", "o_mm", "xc_ok", "x2_ok", "r_mm", "r_ok"))
        LN = [{k: sem(f"ln{i}_{k}") for k in ("stat", "mv", "var", "log", "r0", "newton", "xn", "tr", "xT")}
              for i in range(3)]
        XNT = (xnT_m, xnT_a, xnT_a)
        LN_BANKS = (pm, pa, pa)

        def rows(b, t):
            return x_all[:, at(b * T + t), :].rearrange("p a d -> p (a d)")

        def of_row(t, b, j):
            return t[:, at((b % 2) * KI + j), :].rearrange("p a s -> p (a s)")

        scrap_used = [0]

        def take_wait():
            nc.vector.memset(scrap[:, at(scrap_used[0] % 64)], 0.0)
            scrap_used[0] += 1

        def ln_statistics(dve, i, b):
            s, (stat, mv, var, log, r, tmp) = LN[i], ln_buf[i]
            take_wait()
            for t in range(T):
                nc.vector.bn_stats(stat[:, t, :], rows(b, t)).then_inc(s["stat"], 1)
            dve.wait_ge(s["stat"], b * T + T)
            take_wait()
            for t in range(T):
                nc.vector.bn_aggr(mv[:, t, :], stat[:, t, :]).then_inc(s["mv"], 1)
            dve.wait_ge(s["mv"], b * T + T)
            nc.vector.tensor_scalar(var[:], mv[:, :, 1], EPS, None, ALU.add).then_inc(s["var"], 1)

        def ln_root(act, i, b):
            s, (stat, mv, var, log, r, tmp) = LN[i], ln_buf[i]
            act.wait_ge(s["var"], b + 1)
            nc.scalar.activation(log[:], var[:], ACT.Ln).then_inc(s["log"], 1)
            act.wait_ge(s["log"], b + 1)
            nc.scalar.activation(r[:], log[:], ACT.Exp, scale=-0.5).then_inc(s["r0"], 1)

        def ln_normalise(dve, i, b):
            s, (stat, mv, var, log, r, tmp) = LN[i], ln_buf[i]
            dve.wait_ge(s["r0"], b + 1)
            nc.vector.tensor_tensor(tmp[:], r[:], r[:], ALU.mult).then_inc(s["newton"], 1)
            dve.wait_ge(s["newton"], b * 4 + 1)
            nc.vector.tensor_tensor(tmp[:], tmp[:], var[:], ALU.mult).then_inc(s["newton"], 1)
            dve.wait_ge(s["newton"], b * 4 + 2)
            nc.vector.tensor_scalar(tmp[:], tmp[:], -0.5, 1.5, ALU.mult, ALU.add).then_inc(s["newton"], 1)
            dve.wait_ge(s["newton"], b * 4 + 3)
            nc.vector.tensor_tensor(r[:], r[:], tmp[:], ALU.mult).then_inc(s["newton"], 1)
            dve.wait_ge(s["newton"], b * 4 + 4)
            for t in range(T):
                nc.vector.tensor_scalar(xn[:, t, :], rows(b, t), mv[:, t, 0:1], r[:, t:t + 1],
                                        ALU.subtract, ALU.mult).then_inc(s["xn"], 1)

        def ln_transpose(pe, i, b, k):
            for t in range(T):
                pe.wait_ge(LN[i]["xn"], b * T + t + 1)
                last = nc.tensor.transpose(LN_BANKS[i][k][:, t * P:(t + 1) * P], xn[:, t, k * P:(k + 1) * P], ident[:])
            last.then_inc(LN[i]["tr"], 1)

        def ln_evacuate(act, i, b):
            for k in range(KD):
                act.wait_ge(LN[i]["tr"], b * KD + k + 1)
                nc.scalar.copy(XNT[i][:, k, :], LN_BANKS[i][k][:]).then_inc(LN[i]["xT"], 1)

        with nc.Block() as block:

            @block.sync
            def _(sp):
                sp.dma_start(x_all[:], io["x"].rearrange("(g p) d -> p g d", p=P)).then_inc(x_ld, 16)
                for dst, src in (
                    (w_in, io["w_inT"].rearrange("(k p) o -> p k o", p=P)),
                    (w_conv, io["w_conv"].rearrange("(j p) k -> p j k", p=P)),
                    (b_conv, io["b_conv"]),
                    (w_b, io["w_bT"].rearrange("(k p) n -> p k n", p=P)),
                    (w_dt, io["w_dtT"].rearrange("(k p) o -> p k o", p=P)),
                    (b_dt, io["b_dt"]),
                    (a_neg, io["a_log"].rearrange("(j p) n -> p j n", p=P)),
                    (d_skip, io["d_skip"]),
                    (w_out, io["w_outT"].rearrange("(k p) o -> p k o", p=P)),
                ):
                    sp.dma_start(dst[:], src).then_inc(w_ld, 16)
                sp.wait_ge(zero_ok, 1)
                sp.dma_start(tok_sorted.rearrange("(n p) d -> p n d", p=P),
                             zeros[:].unsqueeze(1).to_broadcast([P, NT, D])).then_inc(tok_st, 16)

                def context(b):
                    wait(sp, av_mm, b * T)
                    wait(sp, s_mm, b * QCH * T)
                    wait(sp, ctx_ld, b * 48)
                    full = (KC - 1) * P
                    sp.dma_start(ctx_t[:], io["ctxT"][b].rearrange("(k p) s -> p k s", p=P)).then_inc(ctx_ld, 16)
                    sp.dma_start(ctx_n[:, 0:KC - 1, :], io["ctx"][b, 0:full, :].rearrange(
                        "(c p) d -> p c d", p=P)).then_inc(ctx_ld, 16)
                    sp.dma_start(ctx_n[0:S2_LAST, KC - 1, :], io["ctx"][b, full:S2, :]).then_inc(ctx_ld, 16)

                def load_mask(b, q):
                    wait(sp, pick_ok, b * QCH * T + QCH * (q - 1))
                    wait(sp, mask_ld, 16 * (b * T + q))
                    sp.dma_start(mask[:, q % 2, 0:S2], io["mask"][b, q * P:(q + 1) * P, :]).then_inc(mask_ld, 16)

                def store_b(b):
                    sp.wait_ge(b_ev, b + 1)
                    sp.dma_start(b_dram[b].rearrange("(n s) -> n s", n=NST), b_row[:]).then_inc(b_st, 16)

                def load_b(b, c):
                    sp.wait_ge(b_st, 16 * (b + 1))
                    n = NST // NB
                    wait(sp, u_ok, b * STEPS - NST + n * (c + 1))
                    wait(sp, b_ld, 16 * (b * NB + c))
                    sp.dma_start(b_all[:, c * n:(c + 1) * n, :], b_dram[at(b), c * n * S:(c + 1) * n * S].to_broadcast(
                        (P, n * S)).rearrange("p (n s) -> p n s", n=n)).then_inc(b_ld, 16)

                def store_tokens(b):
                    for t in range(T):
                        sp.wait_ge(LN[2]["xn"], b * T + t + 1)
                        sp.dma_start(xn3_dram[at(b * S + t * P, P), :], xn[:, t, :]).then_inc(tok_st, 16)

                store_b(0)
                for c in range(NB):
                    load_b(0, c)
                context(0)
                load_mask(0, 0)
                load_mask(0, 1)
                for b in range(B):
                    if b >= 1:
                        load_mask(b - 1, 2)
                        load_mask(b - 1, 3)
                    if b + 1 < B:
                        store_b(b + 1)
                        load_b(b + 1, 0)
                        load_b(b + 1, 1)
                    if b >= 1:
                        context(b)
                        load_mask(b, 0)
                        load_mask(b, 1)
                    if b + 1 < B:
                        load_b(b + 1, 2)
                        load_b(b + 1, 3)
                    if b >= 1:
                        store_tokens(b - 1)
                load_mask(B - 1, 2)
                load_mask(B - 1, 3)
                store_tokens(B - 1)
                sp.wait_ge(tok_st, 16 + 16 * B * T)

            @block.gpsimd
            def _(pool):
                pool.dma_start(wq, io["wq"].rearrange("(k p) d -> p k d", p=P)).then_inc(wa_ld, 16)
                pool.dma_start(wk, io["wk"].rearrange("(k p) d -> p k d", p=P)).then_inc(wa_ld, 16)
                pool.dma_start(wv, io["wv"].rearrange("(k p) d -> p k d", p=P)).then_inc(wa_ld, 16)
                pool.dma_start(wo, io["woT"].rearrange("(k p) d -> p k d", p=P)).then_inc(wa_ld, 16)
                for n, name in enumerate(("bq", "bk", "bv")):
                    pool.dma_start(b_qkv[:, n, :], io[name]).then_inc(wa_ld, 16)
                pool.dma_start(bo_row[:], io["bo"].rearrange("(a d) -> a d", a=1)).then_inc(wa_ld, 16)
                pool.dma_start(w_g[:], io["w_gT"].rearrange("(k p) e -> p k e", p=P)).then_inc(wa_ld, 16)
                nc.gpsimd.memset(ident[:], 0.0).then_inc(id_zero, 1)
                nc.gpsimd.memset(ones[:], 1.0).then_inc(ones_ok, 1)
                nc.gpsimd.memset(zeros[:], 0.0).then_inc(zero_ok, 1)
                pool.wait_ge(id_zero, 1)
                nc.gpsimd.affine_select(out=ident[:], in_=ident[:], compare_op=ALU.not_equal, fill=1.0, base=0,
                                        pattern=[[-1, P]], channel_multiplier=1).then_inc(id_ok, 1)
                pool.wait_ge(setup_mm, 1)

                def times_x(b, j):
                    pool.wait_ge(dt_ok, b * KI + j + 1)
                    nc.gpsimd.tensor_tensor(dtx[:, j % 2, :], dt_[:, j % 2, :], of_row(xs, b, j), ALU.mult).then_inc(dtx_ok, 1)

                def body(b, scan, inp, att_):
                    a, m = b - 1, b + 1
                    for i in range(STEPS):
                        j, n = divmod(i, NST)
                        if scan:
                            if j == 0 and n % (NST // NB) == 0:
                                pool.wait_ge(b_ld, 16 * (b * NB + n // (NST // NB) + 1))
                            if n == 0:
                                pool.wait_ge(dtx_ok, b * KI + j + 1)
                            wait(pool, scan_ok, b * STEPS + i - 1)
                            nc.gpsimd.tensor_tensor(u[:, i % 2, :], dtx[:, j % 2, :], b_all[:, n, :],
                                                    ALU.mult).then_inc(u_ok, 1)
                            for k in range(1, KI):
                                if i == dt_step(k) + 7:
                                    times_x(b, k)
                        if inp and i == dt_step(0) + 8:
                            times_x(m, 0)
                        if att_:
                            if i == 10:
                                for t in range(T):
                                    pool.wait_ge(LN[1]["xn"], a * T + T)
                                    nc.gpsimd.tensor_tensor(rows(a, t), rows(a, t), c_vo[:], ALU.add).then_inc(xc_ok, 1)
                            for q in range(T):
                                if i == q_step(q) - (q > 0):
                                    pool.wait_ge(c_ok, a + 1)
                                    pool.wait_ge(mask_ld, 16 * (a * T + q + 1))
                                    if q >= 2:
                                        pool.wait_ge(pt_mm, a * NPT * T + NPT * (q - 1))
                                    nc.gpsimd.tensor_tensor(pool_scrap[:, q:q + 1], ones[:, 0:1], ones[:, 0:1], ALU.mult)
                                    nc.gpsimd.tensor_scalar(sim[:, q % 2, :], mask[:, q % 2, 0:S2], 0.0, neg_c[:, q:q + 1],
                                                            ALU.mult, ALU.add).then_inc(fill_ok, 1)
                                    nc.gpsimd.tensor_scalar(mask[:, q % 2, 0:S2], mask[:, q % 2, 0:S2], -1.0, 1.0,
                                                            ALU.mult, ALU.add).then_inc(inv_ok, 1)

                body(-1, False, True, False)
                body(0, True, True, False)
                with pool.Fori(1, B - 1) as b:
                    body(b, True, True, True)
                body(B - 1, True, False, True)
                body(B, False, False, True)

            @block.scalar
            def _(act):
                def exp_and_ln():
                    nc.scalar.preload_act_table_set("natural_log_exp_and_others")

                exp_and_ln()
                act.wait_ge(w_ld, 16 * 9)
                nc.scalar.activation(a_neg[:], a_neg[:], ACT.Exp).then_inc(a_exp, 1)
                act.wait_ge(a_ok, 1)

                def softplus(b, j):
                    act.wait_ge(dt_mm, b * KI + j + 1)
                    z, e, n = DT_BANKS[j], dt_[:, j % 2, :], 3 * (b * KI + j)
                    nc.scalar.activation(e, z[:], ACT.Abs, bias=b_dt[:, j:j + 1]).then_inc(sp_step, 1)
                    nc.scalar.activation(sp_pos[:], z[:], ACT.Relu, bias=b_dt[:, j:j + 1]).then_inc(pos_ok, 1)
                    act.wait_ge(sp_step, n + 1)
                    nc.scalar.activation(e, e, ACT.Exp, scale=-1.0).then_inc(sp_step, 1)
                    act.wait_ge(sp_step, n + 2)
                    nc.scalar.activation(e, e, ACT.Ln, bias=1.0).then_inc(sp_step, 1)

                def silu_conv(m):
                    for j in range(KI):
                        act.wait_ge(conv_step, m * TAPS * KI + TAPS * (j + 1))
                        nc.scalar.activation(of_row(xs, m, j), of_row(xs, m, j), ACT.Silu).then_inc(silu_ok, 1)
                    exp_and_ln()

                def silu_res(b):
                    for j in range(KI):
                        act.wait_ge(res_mm, b * KI + j + 1)
                        nc.scalar.activation(gate[:, j, :], RES_BANKS[j][:], ACT.Silu).then_inc(res_ok, 1)
                    exp_and_ln()

                def body(b, scan, inp, att_):
                    a, m = b - 1, b + 1
                    exp_and_ln()
                    for i in range(STEPS):
                        j, n = divmod(i, NST)
                        if scan:
                            if n == 0:
                                act.wait_ge(dt_ok, b * KI + j + 1)
                            wait(act, scan_ok, b * STEPS + i - 1)
                            nc.scalar.activation(da[:, i % 2, :], dt_[:, j % 2, :], ACT.Exp,
                                                 scale=a_neg[:, j, n:n + 1]).then_inc(da_ok, 1)
                            for k in range(1, KI):
                                if i == dt_step(k) + 3:
                                    softplus(b, k)
                            if i == 10:
                                if att_:
                                    act.wait_ge(yg_ok, b * KI)
                                silu_res(b)
                        if inp:
                            if i == 20:
                                ln_root(act, 0, m)
                            if i == 27:
                                ln_evacuate(act, 0, m)
                            if i == 44:
                                silu_conv(m)
                            if i == 49:
                                act.wait_ge(b_mm, m + 1)
                                wait(act, b_st, 16 * m)
                                nc.scalar.copy(b_row[:], pm[0][0:NST, :]).then_inc(b_ev, 1)
                            if i == dt_step(0) + 4:
                                softplus(m, 0)
                        if att_:
                            if i == 7:
                                ln_root(act, 1, a)
                            if i == 11:
                                ln_evacuate(act, 1, a)
                            if i == 14:
                                act.wait_ge(q_mm, a * KD + KD)
                                for k in range(KD):
                                    nc.scalar.activation(xnT_a[:, k, :], pa[k][:], ACT.Identity,
                                                         bias=bq_k[:, k:k + 1]).then_inc(q_ok, 1)
                            for q in range(T):
                                s = i - q_step(q)
                                if s == 7:
                                    act.wait_ge(nmax_ok, a * T + q + 1)
                                    nc.scalar.activation(sim[:, q % 2, :], sim[:, q % 2, :], ACT.Exp,
                                                         bias=row_max[:, q:q + 1],
                                                         accum_out=row_sum[:, q:q + 1]).then_inc(exp_ok, 1)
                                if s in (11, 12, 14, 15):
                                    g = (11, 12, 14, 15).index(s)
                                    act.wait_ge(pt_mm, a * NPT * T + NPT * q + g + 1)
                                    if q:
                                        act.wait_ge(av_mm, a * T + q)
                                    chunks = min(4, KC - 4 * g)
                                    rows_in = S2_LAST if chunks == 1 else P
                                    assert g < NPT - 1 or chunks == 1
                                    nc.scalar.copy(pT[0:rows_in, 4 * g:4 * g + chunks, :],
                                                   pt[g % 2][0:rows_in, 0:chunks * P].rearrange("p (c m) -> p c m", m=P)
                                                   ).then_inc(pt_ok, 1)
                                if s == 18:
                                    act.wait_ge(av_mm, a * T + q + 1)
                                    if q:
                                        act.wait_ge(o_mm, a * T + q)
                                    nc.scalar.copy(attT[:], pv[:, 0:D].rearrange("p (k m) -> p k m", k=KD)).then_inc(av_ok, 1)
                            if i == STEPS - 6:
                                ln_root(act, 2, a)
                            if i == STEPS - 3:
                                ln_evacuate(act, 2, a)

                body(-1, False, True, False)
                body(0, True, True, False)
                with act.Fori(1, B - 1) as b:
                    body(b, True, True, True)
                body(B - 1, True, False, True)
                body(B, False, False, True)

            @block.vector
            def _(dve):
                dve.wait_ge(a_exp, 1)
                nc.vector.tensor_scalar(a_neg[:], a_neg[:], -1.0, None, ALU.mult).then_inc(a_ok, 1)
                dve.wait_ge(ones_ok, 1)
                dve.wait_ge(wa_ld, 16 * 9)
                for k in range(KD):
                    nc.vector.tensor_scalar(bk_b[:, k, :], ones[:], b_qkv[:, 1, k:k + 1], None, ALU.mult).then_inc(bias_b, 1)
                    nc.vector.tensor_scalar(bv_b[:, k, :], ones[:], b_qkv[:, 2, k:k + 1], None, ALU.mult).then_inc(bias_b, 1)
                dve.wait_ge(setup_mm, 1)
                flat = "p k d -> p (k d)"
                nc.vector.tensor_copy(w_qk[:].rearrange(flat), pa[0][:, 0:KD * D]).then_inc(setup_ok, 1)
                nc.vector.tensor_copy(w_vo[:].rearrange(flat), pa[1][:, 0:KD * D]).then_inc(setup_ok, 1)
                nc.vector.tensor_copy(c_vo[:], pm[0][:, 0:D]).then_inc(setup_ok, 1)
                nc.vector.tensor_copy(wq_bk[:], pm[0][:, D:D + KD]).then_inc(setup_ok, 1)
                nc.vector.tensor_copy(bq_k[:], pm[0][:, D + KD:D + 2 * KD]).then_inc(setup_ok, 1)
                nc.vector.tensor_scalar(neg_c0[:], pm[0][:, D + 2 * KD:D + 2 * KD + 1], -1.0, MASKED, ALU.mult,
                                        ALU.add).then_inc(setup_ok, 1)
                dve.wait_ge(setup_ok, 6)
                dve.wait_ge(x_ld, 16)

                def convolve(m, j):
                    dve.wait_ge(ip_mm, m * KI + j + 1)
                    x_ps, c, n = CONV_BANKS[j], of_row(xs, m, j), TAPS * (m * KI + j)
                    nc.vector.tensor_scalar(c, x_ps[:], w_conv[:, j, TAPS - 1:TAPS], b_conv[:, j:j + 1],
                                            ALU.mult, ALU.add).then_inc(conv_step, 1)
                    for s in range(1, TAPS):
                        dve.wait_ge(conv_step, n + s)
                        tail = xs[:, at((m % 2) * KI + j), s:S].rearrange("p a s -> p (a s)")
                        nc.vector.scalar_tensor_tensor(
                            out=tail, in0=x_ps[:, 0:S - s], scalar=w_conv[:, j, TAPS - 1 - s:TAPS - s],
                            in1=tail, op0=ALU.mult, op1=ALU.add).then_inc(conv_step, 1)

                def add_softplus(b, j):
                    dve.wait_ge(pos_ok, b * KI + j + 1)
                    dve.wait_ge(sp_step, 3 * (b * KI + j + 1))
                    nc.vector.tensor_tensor(dt_[:, j % 2, :], sp_pos[:], dt_[:, j % 2, :], ALU.add).then_inc(dt_ok, 1)

                def read_out(b, j):
                    dve.wait_ge(sum_ok, b * PAIRS + NST // 2 * (j + 1))
                    nc.vector.scalar_tensor_tensor(out=dtx[:, j % 2, :], in0=of_row(xs, b, j), scalar=d_skip[:, j:j + 1],
                                                   in1=ysum[:], op0=ALU.mult, op1=ALU.add).then_inc(y_ok, 1)
                    dve.wait_ge(y_ok, b * KI + j + 1)
                    nc.vector.tensor_tensor(yg[:, j, :], dtx[:, j % 2, :], gate[:, j, :], ALU.mult).then_inc(yg_ok, 1)

                def pick(a, q, c):
                    lo, hi = CHUNKS[c]
                    if c == 0:
                        dve.wait_ge(inv_ok, a * T + q + 1)
                    dve.wait_ge(s_mm, a * QCH * T + QCH * q + c + 1)
                    take_wait()
                    nc.vector.copy_predicated(sim[:, q % 2, lo:hi], mask[:, q % 2, lo:hi], pa[c % 2][:, 0:hi - lo]).then_inc(pick_ok, 1)

                def maximum(a, q):
                    dve.wait_ge(pick_ok, a * QCH * T + QCH * (q + 1))
                    nc.vector.reduce_max(row_max[:, q:q + 1], sim[:, q % 2, :], AX_X).then_inc(max_ok, 1)
                    dve.wait_ge(max_ok, a * T + q + 1)
                    nc.vector.tensor_scalar(row_max[:, q:q + 1], row_max[:, q:q + 1], -1.0, None,
                                            ALU.mult).then_inc(nmax_ok, 1)

                def add_pair(b, p):
                    k = 2 * p % HS
                    dve.wait_ge(scan_ok, b * STEPS + 2 * p + 2)
                    nc.vector.tensor_tensor(h[:, k, :], h[:, k, :], h[:, k + 1, :], ALU.add).then_inc(pair_ok, 1)

                def body(b, scan, inp, att_):
                    a, m = b - 1, b + 1
                    for i in range(STEPS):
                        j, n = divmod(i, NST)
                        if scan:
                            dve.wait_ge(da_ok, b * STEPS + i + 1)
                            dve.wait_ge(u_ok, b * STEPS + i + 1)
                            if i % 2 == 0:
                                wait(dve, sum_ok, b * PAIRS + i // 2 - HS // 2 + 1)
                            nc.vector.tensor_tensor_scan(h[:, i % HS, :], da[:, i % 2, :], u[:, i % 2, :], 0.0,
                                                         ALU.mult, ALU.add).then_inc(scan_ok, 1)
                            if i >= 2 and i % 2 == 0:
                                add_pair(b, i // 2 - 1)
                            if j > 0 and n == 2:
                                read_out(b, j - 1)
                            for k in range(1, KI):
                                if i == dt_step(k) + 5:
                                    add_softplus(b, k)
                        if att_:
                            if i == 0:
                                add_pair(a, PAIRS - 1)
                            if i == 2:
                                read_out(a, KI - 1)
                            for t in range(T):
                                if i == 5 + t // 2:
                                    dve.wait_ge(op_mm, a * T + t // 2 * 2 + 2)
                                    nc.vector.tensor_tensor(rows(a, t), rows(a, t), pm[t // 2][:, t % 2 * D:t % 2 * D + D],
                                                            ALU.add).then_inc(x1_ok, 1)
                        if inp:
                            if i == 18:
                                ln_statistics(dve, 0, m)
                            if i == 22:
                                if att_:
                                    dve.wait_ge(LN[1]["tr"], a * KD + KD)
                                ln_normalise(dve, 0, m)
                            for k in range(KI):
                                if i == (32, 34, 40, 42)[k]:
                                    convolve(m, k)
                            if i == dt_step(0) + 6:
                                add_softplus(m, 0)
                        if att_:
                            if i == 6:
                                dve.wait_ge(x1_ok, a * T + T)
                                ln_statistics(dve, 1, a)
                            if i == 8:
                                dve.wait_ge(tok_st, 16 + 16 * T * a)
                                ln_normalise(dve, 1, a)
                            if i == 14:
                                dve.wait_ge(c_mm, a + 1)
                                nc.vector.tensor_scalar(neg_c[:], pv[:, 0:T], -1.0, neg_c0[:], ALU.mult,
                                                        ALU.add).then_inc(c_ok, 1)
                            for q in range(T):
                                s = i - q_step(q)
                                if s in (2, 3, 5, 6):
                                    pick(a, q, (2, 3, 5, 6).index(s))
                                if s == 6:
                                    maximum(a, q)
                                if s == 8:
                                    dve.wait_ge(exp_ok, a * T + q + 1)
                                    nc.vector.reciprocal(row_inv[:, q:q + 1], row_sum[:, q:q + 1]).then_inc(rinv_ok, 1)
                                if i == o_step(q) + 2:
                                    dve.wait_ge(o_mm, a * T + q + 1)
                                    dve.wait_ge(xc_ok, a * T + q + 1)
                                    dve.wait_ge(rinv_ok, a * T + q + 1)
                                    nc.vector.scalar_tensor_tensor(out=rows(a, q), in0=pm[1][:, 0:D], scalar=row_inv[:, q:q + 1],
                                                                   in1=rows(a, q), op0=ALU.mult, op1=ALU.add).then_inc(x2_ok, 1)
                            if i == STEPS - 7:
                                dve.wait_ge(x2_ok, a * T + T)
                                ln_statistics(dve, 2, a)
                            if i == STEPS - 5:
                                if inp:
                                    dve.wait_ge(LN[0]["tr"], m * KD + KD)
                                ln_normalise(dve, 2, a)
                            if i == STEPS - 1:
                                dve.wait_ge(r_mm, a + 1)
                                nc.vector.tensor_copy(scores[:, at(a * T, T), :], pv[:, 0:T * E].rearrange(
                                    "p (t e) -> p t e", e=E)).then_inc(r_ok, 1)

                body(-1, False, True, False)
                body(0, True, True, False)
                with dve.Fori(1, B - 1) as b:
                    body(b, True, True, True)
                body(B - 1, True, False, True)
                body(B, False, False, True)

            @block.tensor
            def _(pe):
                pe.wait_ge(id_ok, 1)
                pe.wait_ge(wa_ld, 16 * 9)
                pe.wait_ge(bias_b, 2 * KD)
                for k in range(KD):
                    for out, lhs, rhs in ((pa[0], wq, wk), (pa[1], wv, wo)):
                        for e in range(KD):
                            nc.tensor.matmul(out[:, k * D:(k + 1) * D], lhs[:, e, k * P:(k + 1) * P], rhs[:, e, :],
                                             start=e == 0, stop=e == KD - 1)
                for e in range(KD):
                    nc.tensor.matmul(pm[0][:, 0:D], bv_b[:, e, :], wo[:, e, :], start=e == 0, stop=False)
                nc.tensor.matmul(pm[0][:, 0:D], ones[0:1, :], bo_row[:], start=False, stop=True)
                for k in range(KD):
                    for col, w, v in ((D + k, wq, 1), (D + KD + k, wk, 0)):
                        for e in range(KD):
                            nc.tensor.matmul(pm[0][:, col:col + 1], w[:, e, k * P:(k + 1) * P], b_qkv[:, v, e:e + 1],
                                             start=e == 0, stop=e == KD - 1)
                col = D + 2 * KD
                for e in range(KD):
                    last = nc.tensor.matmul(pm[0][:, col:col + 1], bk_b[:, e, :], b_qkv[:, 0, e:e + 1],
                                            start=e == 0, stop=e == KD - 1)
                last.then_inc(setup_mm, 1)
                pe.wait_ge(setup_ok, 6)
                pe.wait_ge(w_ld, 16 * 9)

                def project_in(m, j, bank, done):
                    for k in range(KD):
                        last = nc.tensor.matmul(bank[:], w_in[:, k, j * P:(j + 1) * P], xnT_m[:, k, :],
                                                start=k == 0, stop=k == KD - 1)
                    last.then_inc(done, 1)

                def project_dt(b, j, half):
                    for k in range(half * KI // 2, (half + 1) * KI // 2):
                        last = nc.tensor.matmul(DT_BANKS[j][:], w_dt[:, k, j * P:(j + 1) * P], of_row(xs, b, k),
                                                start=k == 0, stop=k == KI - 1)
                    if half == 1:
                        last.then_inc(dt_mm, 1)

                def sum_pair(b, p):
                    if p % (NST // 2) == 0:
                        wait(pe, y_ok, b * KI + p // (NST // 2))
                    pe.wait_ge(pair_ok, b * PAIRS + p + 1)
                    nc.tensor.matmul(ysum[:], ident[:], h[:, 2 * p % HS, :], start=p % (NST // 2) == 0,
                                     stop=(p + 1) % (NST // 2) == 0).then_inc(sum_ok, 1)

                def mamba_in(b, i, scan, att_):
                    m = b + 1
                    if i == 24:
                        if scan:
                            pe.wait_ge(pos_ok, b * KI + 3)
                            pe.wait_ge(res_ok, b * KI + 2)
                        for k in range(KD):
                            ln_transpose(pe, 0, m, k)
                    for j in range(KI):
                        if i == (29, 30, 38, 40)[j]:
                            if j < 2:
                                pe.wait_ge(LN[0]["xT"], m * KD + KD)
                            elif j == 2 and att_:
                                pe.wait_ge(x2_ok, (b - 1) * T + 1)
                            elif j == 2:
                                pe.wait_ge(conv_step, TAPS * (m * KI + 2))
                            elif scan:
                                pe.wait_ge(pos_ok, b * KI + KI)
                            else:
                                pe.wait_ge(conv_step, TAPS * (m * KI + 1))
                            project_in(m, j, CONV_BANKS[j], ip_mm)
                    if i == 46:
                        pe.wait_ge(silu_ok, m * KI + KI)
                        for k in range(KI):
                            last = nc.tensor.matmul(pm[0][0:NST, :], w_b[:, k, :], of_row(xs, m, k),
                                                    start=k == 0, stop=k == KI - 1)
                        last.then_inc(b_mm, 1)
                    for half in range(2):
                        if i == dt_step(0) + half:
                            if half == 0:
                                pe.wait_ge(b_ev, m + 1)
                            project_dt(m, 0, half)

                def mamba_rest(b, i, inp, att_):
                    for half in range(2):
                        if i == dt_step(1) + half:
                            project_dt(b, 1, half)
                        if i == dt_step(2) + half:
                            if half == 0:
                                pe.wait_ge(res_ok, b * KI + 1)
                            project_dt(b, 2, half)
                        if i == dt_step(3) + half:
                            if half == 0 and inp:
                                pe.wait_ge(conv_step, TAPS * ((b + 1) * KI + 1))
                            elif half == 0:
                                pe.wait_ge(pos_ok, b * KI + 3)
                            project_dt(b, 3, half)
                    for j in range(KI):
                        if i == (6, 7, 8, 8)[j]:
                            if att_:
                                pe.wait_ge(x1_ok, (b - 1) * T + (2 if j == 0 else T))
                            elif j == 0:
                                pe.wait_ge(pos_ok, b * KI + 1)
                            project_in(b, KI + j, RES_BANKS[j], res_mm)

                def attention(a, i, scan, inp):
                    b = a + 1
                    for t in range(T):
                        if i == 3 + t // 2:
                            if t == 0:
                                pe.wait_ge(yg_ok, a * KI + KI)
                                pe.wait_ge(pos_ok, b * KI + 1 if scan else B * KI)
                            for j in range(KI):
                                last = nc.tensor.matmul(pm[t // 2][:, t % 2 * D:t % 2 * D + D], yg[:, j, t * P:(t + 1) * P],
                                                        w_out[:, j, :], start=j == 0, stop=j == KI - 1)
                            last.then_inc(op_mm, 1)
                    if i == 9:
                        for k in range(KD):
                            ln_transpose(pe, 1, a, k)
                    if i == 12:
                        pe.wait_ge(LN[1]["xT"], a * KD + KD)
                        if scan:
                            pe.wait_ge(res_ok, b * KI + KI)
                        for t in range(T):
                            for k in range(KD):
                                last = nc.tensor.matmul(pv[:, t:t + 1], xnT_a[:, k, t * P:(t + 1) * P],
                                                        wq_bk[:, k:k + 1], start=k == 0, stop=k == KD - 1)
                        last.then_inc(c_mm, 1)
                        for o in range(KD):
                            for k in range(KD):
                                last = nc.tensor.matmul(pa[o][:], w_qk[:, k, o * P:(o + 1) * P], xnT_a[:, k, :],
                                                        start=k == 0, stop=k == KD - 1)
                            last.then_inc(q_mm, 1)
                    for q in range(T):
                        s = i - q_step(q)
                        if s in (0, 1, 3, 4):
                            c = (0, 1, 3, 4).index(s)
                            lo, hi = CHUNKS[c]
                            if q == 0 and c == 0:
                                pe.wait_ge(q_ok, a * KD + KD)
                                pe.wait_ge(ctx_ld, 48 * (a + 1))
                            if q > 0 or c >= 2:
                                pe.wait_ge(pick_ok, QCH * (a * T + q) + c - 1)
                            for k in range(KD):
                                last = nc.tensor.matmul(pa[c % 2][:, 0:hi - lo], xnT_a[:, k, q * P:(q + 1) * P],
                                                        ctx_t[:, k, lo:hi], start=k == 0, stop=k == KD - 1)
                            last.then_inc(s_mm, 1)
                        if s in (8, 9, 11, 12):
                            g = (8, 9, 11, 12).index(s)
                            if g == 0:
                                pe.wait_ge(exp_ok, a * T + q + 1)
                            if q > 0 or g >= 2:
                                pe.wait_ge(pt_ok, NPT * (a * T + q) + g - 1)
                            elif scan and g == 0:
                                pe.wait_ge(pos_ok, b * KI + 2)
                            elif scan:
                                pe.wait_ge(res_ok, b * KI + 3)
                            for c in range(4 * g, min(4 * g + 4, KC)):
                                w = P if c < KC - 1 else S2_LAST
                                last = nc.tensor.transpose(pt[g % 2][0:w, (c - 4 * g) * P:(c - 4 * g + 1) * P],
                                                           sim[:, q % 2, c * P:c * P + w], ident[:])
                            last.then_inc(pt_mm, 1)
                        if s in (12, 13, 15, 16):
                            g = (12, 13, 15, 16).index(s)
                            if q > 0 and g == 0:
                                pe.wait_ge(av_ok, a * T + q)
                            elif g == 0:
                                pe.wait_ge(c_ok, a + 1)
                            pe.wait_ge(pt_ok, NPT * (a * T + q) + g + 1)
                            for c in range(4 * g, min(4 * g + 4, KC)):
                                w = P if c < KC - 1 else S2_LAST
                                for k in range(KD):
                                    last = nc.tensor.matmul(pv[:, k * P:(k + 1) * P], ctx_n[0:w, c, k * P:(k + 1) * P],
                                                            pT[0:w, c, :], start=c == 0 and k == 0,
                                                            stop=c == KC - 1 and k == KD - 1)
                            if g == NPT - 1:
                                last.then_inc(av_mm, 1)
                        if i == o_step(q):
                            pe.wait_ge(av_ok, a * T + q + 1)
                            if q > 0:
                                pe.wait_ge(x2_ok, a * T + q)
                            if q < 2 and inp:
                                pe.wait_ge(conv_step, TAPS * ((a + 2) * KI + q + 2))
                            for k in range(KD):
                                last = nc.tensor.matmul(pm[1][:, 0:D], attT[:, k, :], w_vo[:, k, :],
                                                        start=k == 0, stop=k == KD - 1)
                            last.then_inc(o_mm, 1)
                    if i == STEPS - 4:
                        for k in range(KD):
                            ln_transpose(pe, 2, a, k)
                    if i == STEPS - 2:
                        pe.wait_ge(LN[2]["xT"], a * KD + KD)
                        for t in range(T):
                            for k in range(KD):
                                last = nc.tensor.matmul(pv[:, t * E:(t + 1) * E], xnT_a[:, k, t * P:(t + 1) * P],
                                                        w_g[:, k, :], start=k == 0, stop=k == KD - 1)
                        last.then_inc(r_mm, 1)

                def body(b, scan, inp, att_):
                    for i in range(STEPS):
                        if att_ and i == 0:
                            sum_pair(b - 1, PAIRS - 1)
                        if scan and i >= 2 and i % 2 == 0:
                            sum_pair(b, i // 2 - 1)
                        if att_:
                            attention(b - 1, i, scan, inp)
                        if scan:
                            mamba_rest(b, i, inp, att_)
                        if inp:
                            mamba_in(b, i, scan, att_)

                body(-1, False, True, False)
                body(0, True, True, False)
                with pe.Fori(1, B - 1) as b:
                    body(b, True, True, True)
                body(B - 1, True, False, True)
                body(B, False, False, True)


def routed_ffn_phase(nc, io, dims, env, sem, buf):
    B, S, D, S2, DI, NST, TAPS, E, HF = dims
    KD, G, KH, H_LAST, HH, NT = (env[k] for k in ("KD", "G", "KH", "H_LAST", "HH", "NT"))
    x_all, ident, scores = env["x_all"], env["ident"], env["scores"]
    tok_sorted, ffn_sorted, xn3_dram = env["tok_sorted"], env["ffn_sorted"], env["xn3_dram"]
    LOOP = NT + 2

    with ExitStack() as ctx:
        def sb(name, shape, dt=F32):
            return buf(ctx, name, shape, dt)

        w1 = sb("w1", [P, E * KD * HF])
        w2 = sb("w2", [P, E * KD * HF])
        w3 = sb("w3", [P, E * KH * D])
        xn = sb("xn_sorted", [P, G, D])
        tok = sb("tok", [P, 2, D])
        tokT = sb("tokT", [P, 2, KD, P])
        act_ = sb("act_", [P, HF])
        hid = sb("hid", [P, 2, HF])
        hidT = sb("hidT", [P, KH, P])
        y_sb = sb("y_sb", [P, 2, D])
        tri = sb("tri", [P, P])
        ones = sb("ones2", [P, P])
        iot = sb("iot", [P, 64], I32)
        rev = sb("rev", [P, E])
        tile_id = sb("tile_id", [1, LOOP])
        w_top = sb("w_top", [P, 2, G])
        eq = sb("eq", [P, G, E])
        oh = sb("oh", [P, 2, G, E])
        rest = sb("rest", [P, G, E])
        km = sb("km", [P, G])
        both = sb("both", [P, G, E])
        tot = sb("tot", [P, E, G])
        seg = sb("seg", [P, E, G])
        inc = sb("inc", [P, E, G])
        slot = sb("slot", [P, G, E])
        pos_f = sb("pos_f", [P, 2, G])
        pos = sb("pos", [P, 2, G], U32)
        cnt_i = sb("cnt_i", [P, E], I32)
        cnt_f = sb("cnt_f", [P, E])
        tiles = sb("tiles", [P, E])
        tend = sb("tend", [P, E])
        ge = sb("ge", [1, LOOP, E])
        tile_e = sb("tile_e", [1, LOOP])
        tile_expert = sb("tile_expert", [1, LOOP], I32)
        y_one = xn
        y_two = sb("y_two", [P, 4, D])

        def ps(name, n=512):
            return ctx.enter_context(nc.psum_tensor(name, [P, n], F32))

        ps_g = [ps("ps_g0"), ps("ps_g1")]
        ps_u = [ps("ps_u0"), ps("ps_u1")]
        ps_x, ps_h0, ps_h1, ps_y = ps("ps_x"), ps("ps_h0"), ps("ps_h1"), ps("ps_y")

        wts_ld, xn_ld, iota_ok, tri_zero, tri_ok, one_ok = (
            sem(n) for n in ("wts_ld", "xn_ld", "iota_ok", "tri_zero", "tri_ok", "one_ok"))
        step, mask_ok, rank_mm, pos_ok2, tab_ok = (sem(n) for n in ("step", "mask_ok", "rank_mm", "pos_ok2", "tab_ok"))
        sorted_st, out_st = sem("sorted_st"), sem("out_st")
        tok_ld, y_st = [sem("tok_ld0"), sem("tok_ld1")], [sem("y_st0"), sem("y_st1")]

        def so_far(i, p):
            return i * 8 + 16 - 8 * p

        x_mm, xT_ok, gu_mm, silu2_ok, hid_ok, h_mm, hT_ok0, hT_ok1, y_mm, y_ok2 = (
            sem(n) for n in ("x_mm", "xT_ok", "gu_mm", "silu2_ok", "hid_ok", "h_mm", "hT_ok0", "hT_ok1", "y_mm", "y_ok2"))
        one_ld, two_ld, comb, comb_ok = sem("one_ld"), [sem("two_ld0"), sem("two_ld1")], sem("comb"), sem("comb_ok")
        pad_done = sem("pad_done")

        with nc.Block() as block:

            @block.sync
            def _(sp):
                sp.dma_start(xn[:], xn3_dram.rearrange("(g p) d -> p g d", p=P)).then_inc(xn_ld, 16)
                full = (KH - 1) * P
                for e in range(E):
                    for dst, src in ((w1, io["w1T"]), (w2, io["w2T"])):
                        sp.dma_start(dst[:, e * KD * HF:(e + 1) * KD * HF].rearrange("p (k h) -> p k h", k=KD),
                                     src[e].rearrange("(k p) h -> p k h", p=P)).then_inc(wts_ld, 16)
                    w3e = w3[:, e * KH * D:(e + 1) * KH * D].rearrange("p (c d) -> p c d", c=KH)
                    sp.dma_start(w3e[:, 0:KH - 1, :], io["w3T"][e, 0:full, :].rearrange("(c p) d -> p c d", p=P)).then_inc(wts_ld, 16)
                    sp.dma_start(w3e[0:H_LAST, KH - 1, :], io["w3T"][e, full:HF, :]).then_inc(wts_ld, 16)
                sp.wait_ge(sorted_st, 16 * 2 * G)

                def load(i, p):
                    wait(sp, x_mm, i - 1)
                    sp.dma_start(tok[:, p, :], tok_sorted[at(i * P, P), :]).then_inc(tok_ld[p], 16)

                def store(i, p):
                    sp.wait_ge(y_ok2, i + 1)
                    sp.dma_start(ffn_sorted[at(i * P, P), :], y_sb[:, p, :]).then_inc(y_st[p], 16)

                load(0, 0)
                load(1, 1)

                def pair(i):
                    for k in range(2):
                        load(i + k + 2, k)
                        store(i + k, k)

                pair(0)
                with sp.Fori(2, NT - 3, 2) as i:
                    pair(i)
                load(NT - 1, 0)
                store(NT - 3, 0)
                store(NT - 2, 1)
                store(NT - 1, 0)
                out = io["out"].rearrange("(g p) d -> p g d", p=P)
                for g in range(0, G, 4):
                    sp.wait_ge(comb_ok, g + 4)
                    sp.dma_start(out[:, g:g + 4, :], x_all[:, g:g + 4, :]).then_inc(out_st, 16)
                sp.wait_ge(out_st, 16 * (G // 4))

            @block.gpsimd
            def _(pool):
                nc.gpsimd.iota(iot[:], pattern=[[1, 64]], base=0, channel_multiplier=0).then_inc(iota_ok, 1)
                nc.gpsimd.memset(tri[:], 1.0).then_inc(tri_zero, 1)
                nc.gpsimd.memset(ones[:], 1.0).then_inc(one_ok, 1)
                nc.gpsimd.memset(seg[:], 1.0).then_inc(one_ok, 1)
                pool.wait_ge(one_ok, 2)
                nc.gpsimd.memset(seg[:, :, 0:1], 0.0).then_inc(one_ok, 1)
                pool.wait_ge(tri_zero, 1)
                nc.gpsimd.affine_select(out=tri[:], in_=tri[:], compare_op=ALU.is_gt, fill=0.0, base=0,
                                        pattern=[[1, P]], channel_multiplier=-1).then_inc(tri_ok, 1)
                pool.wait_ge(xn_ld, 16)
                pool.wait_ge(pos_ok2, 1)
                for g in range(G):
                    for k in range(2):
                        pool.indirect_dma_start(tok_sorted, bass.IndirectOffsetOnAxis(ap=pos[:, k, g:g + 1], axis=0),
                                                xn[:, g, :], None).then_inc(sorted_st, 16)
                for p in range(2):
                    pool.wait_ge(y_st[p], so_far(NT - 1 if (NT - 1) % 2 == p else NT - 2, p))
                pool.wait_ge(sorted_st, 16 * 2 * G)
                for g in range(G):
                    pool.indirect_dma_start(y_one[:, g, :], None, ffn_sorted,
                                            bass.IndirectOffsetOnAxis(ap=pos[:, 0, g:g + 1], axis=0)).then_inc(one_ld, 16)
                for g in range(G):
                    wait(pool, comb_ok, g - 1)
                    pool.indirect_dma_start(y_two[:, g % 2, :], None, ffn_sorted,
                                            bass.IndirectOffsetOnAxis(ap=pos[:, 1, g:g + 1], axis=0)).then_inc(two_ld[g % 2], 16)

            @block.scalar
            def _(act):
                def evacuate_tokens(i, p):
                    act.wait_ge(x_mm, i + 1)
                    wait(act, gu_mm, 2 * (i - 1))
                    nc.scalar.copy(tokT[:, p, :, :], ps_x[:, 0:D].rearrange("p (k m) -> p k m", k=KD)).then_inc(xT_ok, 1)

                def silu(i):
                    for c in range(2):
                        act.wait_ge(gu_mm, 2 * i + c + 1)
                        wait(act, hid_ok, 2 * (i - 1) + c + 1)
                        nc.scalar.activation(act_[:, c * HH:(c + 1) * HH], ps_g[c][:, 0:HH], ACT.Silu).then_inc(silu2_ok, 1)

                def evacuate_hidden(i):
                    act.wait_ge(h_mm, 2 * i + 1)
                    wait(act, y_mm, i)
                    nc.scalar.copy(hidT[:, 0:4, :], ps_h0[:].rearrange("p (c m) -> p c m", c=4)).then_inc(hT_ok0, 1)

                evacuate_tokens(0, 0)
                silu(0)
                evacuate_tokens(1, 1)

                def pair(i):
                    for k in range(2):
                        silu(i + k)
                        evacuate_tokens(i + k + 1, k)
                        evacuate_hidden(i + k - 1)

                pair(1)
                with act.Fori(3, NT - 2, 2) as i:
                    pair(i)
                silu(NT - 2)
                evacuate_tokens(NT - 1, 0)
                evacuate_hidden(NT - 3)
                silu(NT - 1)
                evacuate_hidden(NT - 2)
                evacuate_hidden(NT - 1)

            @block.vector
            def _(dve):
                count = [0]

                def chain(ins):
                    ins.then_inc(step, 1)
                    count[0] += 1
                    dve.wait_ge(step, count[0])

                def over_e(t):
                    return t.unsqueeze(2).to_broadcast([P, G, E])

                def over_g(t):
                    return t.unsqueeze(1).to_broadcast([P, G, E])

                dve.wait_ge(iota_ok, 1)
                chain(nc.vector.tensor_copy(cnt_f[:], iot[:, 0:E]))
                chain(nc.vector.tensor_scalar(rev[:], cnt_f[:], -1.0, float(E), ALU.mult, ALU.add))
                chain(nc.vector.tensor_copy(tile_id[:], iot[0:1, 0:LOOP]))
                chain(nc.vector.tensor_copy(rest[:], scores[:]))
                for k in range(2):
                    chain(nc.vector.reduce_max(w_top[:, k, :], rest[:], AX_X))
                    chain(nc.vector.tensor_tensor(eq[:], rest[:], over_e(w_top[:, k, :]), ALU.is_equal))
                    chain(nc.vector.tensor_tensor(eq[:], eq[:], over_g(rev[:]), ALU.mult))
                    chain(nc.vector.reduce_max(km[:], eq[:], AX_X))
                    chain(nc.vector.tensor_tensor(oh[:, k, :, :], eq[:], over_e(km[:]), ALU.is_equal))
                    if k == 0:
                        chain(nc.vector.scalar_tensor_tensor(out=rest[:], in0=oh[:, 0, :, :], scalar=NEG_HUGE, in1=rest[:],
                                                             op0=ALU.mult, op1=ALU.add))
                nc.vector.tensor_tensor(both[:], oh[:, 0, :, :], oh[:, 1, :, :], ALU.add).then_inc(mask_ok, 1)
                dve.wait_ge(rank_mm, 1)
                dve.wait_ge(one_ok, 3)
                chain(nc.vector.tensor_copy(tot[:], ps_u[0][:, 0:G * E].rearrange("p (g e) -> p e g", e=E)))
                flat = "p e g -> p (e g)"
                chain(nc.vector.tensor_tensor_scan(inc[:].rearrange(flat), seg[:].rearrange(flat), tot[:].rearrange(flat),
                                                   0.0, ALU.mult, ALU.add))
                chain(nc.vector.tensor_tensor(tot[:], inc[:], tot[:], ALU.subtract))
                chain(nc.vector.tensor_tensor(slot[:], ps_g[0][:, 0:G * E].rearrange("p (g e) -> p g e", e=E),
                                              tot[:].rearrange("p e g -> p g e"), ALU.add))
                chain(nc.vector.tensor_copy(cnt_f[:], inc[:, :, G - 1]))
                chain(nc.vector.tensor_scalar(cnt_f[:], cnt_f[:], float(P - 1), None, ALU.add))
                chain(nc.vector.tensor_copy(cnt_i[:], cnt_f[:]))
                chain(nc.vector.tensor_scalar(cnt_i[:], cnt_i[:], P.bit_length() - 1, None, ALU.arith_shift_right))
                chain(nc.vector.tensor_copy(tiles[:], cnt_i[:]))
                chain(nc.vector.tensor_tensor_scan(tend[:], ones[:, 0:E], tiles[:], 0.0, ALU.mult, ALU.add))
                chain(nc.vector.tensor_tensor(tiles[:], tend[:], tiles[:], ALU.subtract))
                chain(nc.vector.tensor_scalar(tiles[:], tiles[:], float(P), None, ALU.mult))
                chain(nc.vector.tensor_tensor(slot[:], slot[:], over_g(tiles[:]), ALU.add))
                for k in range(2):
                    chain(nc.vector.tensor_tensor(eq[:], oh[:, k, :, :], slot[:], ALU.mult))
                    chain(nc.vector.reduce_sum(pos_f[:, k, :], eq[:], AX_X))
                nc.vector.tensor_copy(pos[:], pos_f[:]).then_inc(pos_ok2, 1)
                shape = [1, LOOP, E]
                chain(nc.vector.tensor_tensor(ge[:], tile_id[:].unsqueeze(2).to_broadcast(shape),
                                              tend[0:1, :].unsqueeze(1).to_broadcast(shape), ALU.is_ge))
                chain(nc.vector.reduce_sum(tile_e[:], ge[:], AX_X))
                chain(nc.vector.tensor_scalar(tile_e[:], tile_e[:], float(E - 1), None, ALU.min))
                nc.vector.tensor_copy(tile_expert[:], tile_e[:]).then_inc(tab_ok, 1)

                def multiply(i, p):
                    for c in range(2):
                        dve.wait_ge(silu2_ok, 2 * i + c + 1)
                        wait(dve, h_mm, 2 * (i - 1))
                        nc.vector.tensor_tensor(hid[:, p, c * HH:(c + 1) * HH], act_[:, c * HH:(c + 1) * HH],
                                                ps_u[c][:, 0:HH], ALU.mult).then_inc(hid_ok, 1)

                def evacuate(i, p):
                    dve.wait_ge(h_mm, 2 * i + 2)
                    wait(dve, y_mm, i)
                    nc.vector.tensor_copy(hidT[:, 4:KH - 1, :], ps_h1[:, 0:(KH - 5) * P].rearrange(
                        "p (c m) -> p c m", m=P)).then_inc(hT_ok1, 1)
                    nc.vector.tensor_copy(hidT[0:H_LAST, KH - 1, :], ps_h1[0:H_LAST, (KH - 5) * P:(KH - 4) * P]).then_inc(hT_ok1, 1)
                    dve.wait_ge(y_mm, i + 1)
                    wait(dve, y_st[p], so_far(i - 2, p))
                    nc.vector.tensor_copy(y_sb[:, p, :], ps_y[:, 0:D]).then_inc(y_ok2, 1)

                def pair(i):
                    for k in range(2):
                        multiply(i + k, 1 - k)
                        evacuate(i + k - 1, k)

                multiply(0, 0)
                pair(1)
                with dve.Fori(3, NT, 2) as i:
                    pair(i)
                evacuate(NT - 1, 0)
                dve.wait_ge(one_ld, 16 * G)
                for g in range(G):
                    nc.vector.scalar_tensor_tensor(out=x_all[:, g, :], in0=y_one[:, g, :], scalar=w_top[:, 0, g:g + 1],
                                                   in1=x_all[:, g, :], op0=ALU.mult, op1=ALU.add).then_inc(comb, 1)
                for g in range(G):
                    dve.wait_ge(comb, g + 1)
                    dve.wait_ge(two_ld[g % 2], 16 * (g // 2 + 1))
                    nc.vector.scalar_tensor_tensor(out=x_all[:, g, :], in0=y_two[:, g % 2, :], scalar=w_top[:, 1, g:g + 1],
                                                   in1=x_all[:, g, :], op0=ALU.mult, op1=ALU.add).then_inc(comb_ok, 1)

            @block.tensor
            def _(pe):
                pe.wait_ge(mask_ok, 1)
                pe.wait_ge(tri_ok, 1)
                pe.wait_ge(one_ok, 3)
                flat = "p g e -> p (g e)"
                nc.tensor.matmul(ps_g[0][:, 0:G * E], tri[:], both[:].rearrange(flat), start=True, stop=True)
                nc.tensor.matmul(ps_u[0][:, 0:G * E], ones[:], both[:].rearrange(flat), start=True, stop=True).then_inc(rank_mm, 1)
                pe.wait_ge(tab_ok, 1)
                pe.wait_ge(wts_ld, 16 * 4 * E)

                def expert(i):
                    return pe.value_load(tile_expert[0:1, at(i)], min_val=0, max_val=E - 1)

                def transpose_tokens(i, p):
                    pe.wait_ge(tok_ld[p], so_far(i, p))
                    wait(pe, xT_ok, i)
                    for k in range(KD):
                        last = nc.tensor.transpose(ps_x[:, k * P:(k + 1) * P], tok[:, p, k * P:(k + 1) * P], ident[:])
                    last.then_inc(x_mm, 1)

                def gate_up(i, p):
                    e = expert(i)
                    pe.wait_ge(xT_ok, i + 1)
                    for c in range(2):
                        wait(pe, hid_ok, 2 * (i - 1) + c + 1)
                        for out, w in ((ps_g[c], w1), (ps_u[c], w2)):
                            for k in range(KD):
                                last = nc.tensor.matmul(out[:, 0:HH], tokT[:, p, k, :],
                                                        w[:, at(e * (KD * HF) + (k * HF + c * HH), HH)],
                                                        start=k == 0, stop=k == KD - 1)
                        last.then_inc(gu_mm, 1)

                def down(i, p):
                    e = expert(i)
                    pe.wait_ge(hid_ok, 2 * i + 2)
                    wait(pe, hT_ok0, i)
                    for c in range(4):
                        last = nc.tensor.transpose(ps_h0[:, c * P:(c + 1) * P], hid[:, p, c * P:(c + 1) * P], ident[:])
                    last.then_inc(h_mm, 1)
                    wait(pe, hT_ok1, 2 * i)
                    for c in range(4, KH):
                        n = P if c < KH - 1 else H_LAST
                        last = nc.tensor.transpose(ps_h1[0:n, (c - 4) * P:(c - 3) * P], hid[:, p, c * P:c * P + n], ident[:])
                    last.then_inc(h_mm, 1)
                    wait(pe, y_ok2, i)
                    pe.wait_ge(hT_ok0, i + 1)
                    pe.wait_ge(hT_ok1, 2 * i + 2)
                    for c in range(KH):
                        n = P if c < KH - 1 else H_LAST
                        last = nc.tensor.matmul(ps_y[:, 0:D], hidT[0:n, c, :], w3[0:n, at(e * (KH * D) + c * D, D)],
                                                start=c == 0, stop=c == KH - 1)
                    last.then_inc(y_mm, 1)

                transpose_tokens(0, 0)
                gate_up(0, 0)
                transpose_tokens(1, 1)

                def pair(i):
                    for k in range(2):
                        gate_up(i + k, 1 - k)
                        transpose_tokens(i + k + 1, k)
                        down(i + k - 1, k)

                pair(1)
                with pe.Fori(3, NT - 2, 2) as i:
                    pair(i)
                gate_up(NT - 2, 1)
                transpose_tokens(NT - 1, 0)
                down(NT - 3, 0)
                gate_up(NT - 1, 0)
                down(NT - 2, 1)
                down(NT - 1, 0)


def kernel(x, ctx_1024, mask_BxSxS2_bk1, L0_attn_W_in, L0_attn_W_conv, L0_attn_b_conv, L0_attn_W_x, L0_attn_W_dt,
           L0_attn_b_dt, L0_attn_W_out, L0_attn_A_log, L0_attn_D, L0_xattn_Wq, L0_xattn_bq, L0_xattn_Wk, L0_xattn_bk,
           L0_xattn_Wv, L0_xattn_bv, L0_xattn_Wo, L0_xattn_bo, L0_ffn_Wg, L0_ffn_W1, L0_ffn_W2, L0_ffn_W3):
    import numpy as np
    from concourse import bacc
    from concourse.bass_utils import run_bass_kernel_spmd

    def lay(a, *axes):
        a = np.asarray(a)
        return np.ascontiguousarray(a.transpose(axes) if axes else a)

    def columns(a):
        return lay(np.asarray(a).reshape(-1, P), 1, 0)

    B, S, D = x.shape
    S2 = ctx_1024.shape[1]
    DI, NST = L0_attn_A_log.shape
    TAPS = L0_attn_W_conv.shape[2]
    E, HF, _ = L0_ffn_W1.shape
    arrays = {
        "x": lay(x).reshape(B * S, D),
        "ctx": lay(ctx_1024),
        "ctxT": lay(ctx_1024, 0, 2, 1),
        "mask": lay(mask_BxSxS2_bk1),
        "w_inT": lay(L0_attn_W_in, 1, 0),
        "w_conv": lay(L0_attn_W_conv).reshape(DI, TAPS),
        "b_conv": columns(L0_attn_b_conv),
        "w_bT": lay(np.asarray(L0_attn_W_x)[NST:2 * NST], 1, 0),
        "w_dtT": lay(L0_attn_W_dt, 1, 0),
        "b_dt": columns(L0_attn_b_dt),
        "w_outT": lay(L0_attn_W_out, 1, 0),
        "a_log": lay(L0_attn_A_log),
        "d_skip": columns(L0_attn_D),
        "wq": lay(L0_xattn_Wq), "wk": lay(L0_xattn_Wk), "wv": lay(L0_xattn_Wv),
        "bq": columns(L0_xattn_bq), "bk": columns(L0_xattn_bk), "bv": columns(L0_xattn_bv), "bo": lay(L0_xattn_bo),
        "woT": lay(L0_xattn_Wo, 1, 0),
        "w_gT": lay(L0_ffn_Wg, 1, 0),
        "w1T": lay(L0_ffn_W1, 0, 2, 1),
        "w2T": lay(L0_ffn_W2, 0, 2, 1),
        "w3T": lay(L0_ffn_W3, 0, 2, 1),
    }
    nc = bacc.Bacc("TRN2", target_bir_lowering=False, num_devices=1)
    io = {k: nc.dram_tensor(f"in_{k}", a.shape, mybir.dt.from_np(a.dtype), kind="ExternalInput").ap()
          for k, a in arrays.items()}
    io["out"] = nc.dram_tensor("out", [B * S, D], F32, kind="ExternalOutput").ap()
    decoder_kernel(nc, io, (B, S, D, S2, DI, NST, TAPS, E, HF))
    result = run_bass_kernel_spmd(nc, [{f"in_{k}": a for k, a in arrays.items()}], core_ids=[0])
    return result.results[0]["out"].reshape(B, S, D)
```

```python
from contextlib import ExitStack

import concourse.bass as bass
from concourse import mybir

F32 = mybir.dt.float32
F32R = mybir.dt.float32r
I32 = mybir.dt.int32
U32 = mybir.dt.uint32
U8 = mybir.dt.uint8
ACT = mybir.ActivationFunctionType
ALU = mybir.AluOpType
AX_X = mybir.AxisListType.X

P = 128
EPS = 1e-5
MASKED = -1000000000.0
NEG_HUGE = -3.0e38


def at(i, n=1):
    return bass.ds(i, n)


def wait(eng, sem, value):
    if isinstance(value, int) and value <= 0:
        return
    eng.wait_ge(sem, value)


def decoder_kernel(nc, io, dims):
    B, S, D, S2, DI, NST, TAPS, E, HF = dims
    KD = D // P
    KI = DI // P
    T = S // P
    G = B * T
    KC = -(-S2 // P)
    S2_LAST = S2 - (KC - 1) * P
    CH = -(-S2 // 4)
    CHUNKS = [(c * CH, min(S2, (c + 1) * CH)) for c in range(4)]
    KH = -(-HF // P)
    H_LAST = HF - (KH - 1) * P
    HH = HF // 2
    NT = (2 * B * S + E * (P - 1)) // P

    ffn_sorted = nc.dram_tensor("ffn_sorted", [NT * P, D], F32).ap()
    xn3_dram = nc.dram_tensor("xn3_dram", [G * P, D], F32).ap()
    b_dram = nc.dram_tensor("b_dram", [B, NST * S], F32).ap()

    top = ExitStack()
    with top:
        def sem(name):
            return top.enter_context(nc.semaphore(name))

        def buf(ctx, name, shape, dt=F32):
            return ctx.enter_context(nc.sbuf_tensor(name, shape, dt))

        x_all = buf(top, "x_all", [P, G, D])
        ident = buf(top, "ident", [P, P])
        scores = buf(top, "scores", [P, G, E])

        mixer_phase(nc, io, dims, locals(), sem, buf)
        routed_ffn_phase(nc, io, dims, locals(), sem, buf)


AT = {
    "last_y": 2, "out_proj": (3, 3), "x1": (5, 6),
    "ln_a_stat": 7, "ln_a_root": 7, "ln_a_norm": 8, "ln_a_turn": 7, "ln_a_copy": 11, "x_bias": 10,
    "query": 10, "row_const": 14, "query_copy": 15,
    "tile": (15, 22, 29, 35), "fill": (16, 23, 32, 36), "score": (0, 1, 3, 4), "pick": (2, 3, 5, 6), "max": 6,
    "exp": 9, "inverse": 9, "p_turn": (9, 10, 11, 13), "p_copy": (11, 12, 14, 16), "av": (11, 13, 15, 16), "av_copy": 18,
    "out": (35, 41, 48, 55), "x2": (36, 42, 51, 56),
    "ln_f_stat": 57, "ln_f_root": 58, "ln_f_norm": 58, "ln_f_turn": 58, "ln_f_copy": 60, "router": 60, "scores": 63,
    "res_proj": (6, 7, 8, 8), "res_silu": 14,
    "dt_proj": (52, 5, 19, 34), "softplus": (57, 9, 25, 39), "dt_add": (58, 10, 26, 40), "dtx": (60, 12, 28, 42),
    "ln_m_stat": 21, "ln_m_root": 22, "ln_m_norm": 23, "ln_m_turn": 25, "ln_m_copy": 28,
    "in_proj": (29, 31, 37, 39), "tap": (32, 34, 40, 42), "conv": (33, 35, 41, 43), "conv_silu": 46,
    "b_proj": 47, "b_copy": 50,
}
ALONE = {
    "last_y": 4, "out_proj": (2, 5), "x1": (5, 6),
    "ln_a_stat": 10, "ln_a_root": 7, "ln_a_norm": 13, "ln_a_turn": 7, "ln_a_copy": 19, "x_bias": 13,
    "query": 10, "row_const": 13, "query_copy": 21,
    "tile": (15, 22, 29, 35), "fill": (15, 21, 31, 33), "score": (0, 1, 3, 4), "pick": (2, 3, 5, 6), "max": 8,
    "exp": 11, "inverse": 9, "p_turn": (9, 10, 11, 13), "p_copy": (13, 15, 16, 18), "av": (13, 14, 16, 17), "av_copy": 19,
    "out": (34, 40, 49, 52), "x2": (34, 41, 49, 54),
    "ln_f_stat": 55, "ln_f_root": 59, "ln_f_norm": 61, "ln_f_turn": 58, "ln_f_copy": 61, "router": 58, "scores": 63,
    "dt_proj": (49, 4, 16, 34), "softplus": (52, 7, 22, 37), "dt_add": (56, 9, 24, 38), "dtx": (61, 16, 34, 46),
    "ln_m_stat": 20, "ln_m_root": 23, "ln_m_norm": 21, "ln_m_turn": 20, "ln_m_copy": 27,
    "in_proj": (30, 31, 38, 40), "tap": (35, 36, 44, 44), "conv": (38, 40, 46, 47), "conv_silu": 46,
    "b_proj": 48, "b_copy": 50,
}


def mixer_phase(nc, io, dims, env, sem, buf):
    B, S, D, S2, DI, NST, TAPS, E, HF = dims
    KD, KI, T, KC = env["KD"], env["KI"], env["T"], env["KC"]
    S2_LAST, CHUNKS = env["S2_LAST"], env["CHUNKS"]
    x_all, ident, scores = env["x_all"], env["ident"], env["scores"]
    xn3_dram, b_dram, NT = (env[k] for k in ("xn3_dram", "b_dram", "NT"))
    STEPS = KI * NST
    NPT = -(-KC // 4)
    NB = 4
    HS = 8
    DS = 4
    PAIRS = STEPS // 2
    QCH = len(CHUNKS)

    with ExitStack() as ctx:
        def sb(name, shape, dt=F32):
            return buf(ctx, name, shape, dt)

        def ps(name):
            return ctx.enter_context(nc.psum_tensor(name, [P, 512], F32))

        w_in = sb("w_in", [P, KD, 2 * DI])
        w_dt = sb("w_dt", [P, KI, DI])
        w_b = sb("w_b", [P, KI, NST])
        w_out = sb("w_out", [P, KI, D])
        w_conv = sb("w_conv", [P, KI, TAPS])
        b_conv = sb("b_conv", [P, KI])
        b_dt = sb("b_dt", [P, KI])
        d_skip = sb("d_skip", [P, KI])
        a_neg = sb("a_neg", [P, KI, NST])
        w_qk = sb("w_qk", [P, KD, D])
        w_vo = sb("w_vo", [P, KD, D])
        bq_k = sb("bq_k", [P, KD])
        wq_bk = sb("wq_bk", [P, KD])
        neg_c0 = sb("neg_c0", [P, 1])
        c_vo = sb("c_vo", [P, D])
        w_g = sb("w_g", [P, KD, E])
        xn = sb("xn", [P, T, D])
        xnT_m = sb("xnT_m", [P, KD, S])
        xs = sb("xs", [P, 2 * KI, S])
        gate = sb("gate", [P, KI, S])
        dt_ = sb("dt_", [P, 2, S])
        dtx = sb("dtx", [P, 2, S])
        yg = sb("yg", [P, KI, S])
        sp_pos = sb("sp_pos", [P, S])
        b_row = sp_pos[0:NST, :]
        b_all = sb("b_all", [P, NST, S])
        u = sb("u", [P, 2, S])
        da = sb("da", [P, DS, S])
        h = sb("h", [P, HS, S])
        xnT_a = sb("xnT_a", [P, KD, S])
        neg_c = sb("neg_c", [P, T])
        ctx_n = sb("ctx_n", [P, KC, D])
        ctx_t = sb("ctx_t", [P, KD, S2])
        mask = sb("mask", [P, 2, -(-S2 // 4) * 4], U8)
        sim = sb("sim", [P, 2, S2])
        pT = sb("pT", [P, KC, P])
        row_max = sb("row_max", [P, T])
        row_sum = sb("row_sum", [P, T])
        row_inv = sb("row_inv", [P, T])
        attT = sb("attT", [P, KD, P])
        ln_buf = [(sb(f"ln_stat{i}", [P, T, 6]), sb(f"ln_mv{i}", [P, T, 2]), sb(f"ln_var{i}", [P, T]),
                   sb(f"ln_log{i}", [P, T]), sb(f"ln_r{i}", [P, T]), sb(f"ln_t{i}", [P, T])) for i in range(3)]
        wq, wk, wv, wo = (h[:, i, :].rearrange("p (k d) -> p k d", k=KD) for i in range(4))
        bk_b, bv_b = (u[:, i, 0:KD * P].rearrange("p (k m) -> p k m", k=KD) for i in range(2))
        b_qkv = sb("b_qkv", [P, 3, KD])
        scrap = sb("scrap", [P, 64])
        act_scrap = sb("act_scrap", [P, KI + 1])
        pool_scrap = sb("pool_scrap", [P, T])
        zeros, ones, bo_row = yg[:, 0, 0:D], yg[:, 1, 0:P], yg[0:1, 2, 0:D]

        ysum = ps("ysum")
        pm = [ps("pm0"), ps("pm1")]
        pa = [ps("pa0"), ps("pa1")]
        pt = [ps("pt0"), ps("pt1")]
        pv = ps("pv")
        RES_BANKS = (pm[0], pm[1], pt[1], pv)
        CONV_BANKS = (pm[0], pm[1], pm[1], pm[0])
        DT_BANKS = (pm[0], pt[0], pm[0], pm[0])

        x_ld, xr_ld, wi_ld, w_ld, wa_ld, b_st, b_ld, ctx_ld, mask_ld, tok_st, res_st = (
            sem(n) for n in ("x_ld", "xr_ld", "wi_ld", "w_ld", "wa_ld", "b_st", "b_ld", "ctx_ld", "mask_ld", "tok_st", "res_st"))
        zero_ok, id_zero, id_ok, ones_ok, a_exp, a_ok, bias_b, setup_mm, setup_ok = (
            sem(n) for n in ("zero_ok", "id_zero", "id_ok", "ones_ok", "a_exp", "a_ok", "bias_b", "setup_mm", "setup_ok"))
        ip_mm, res_mm, conv_step, silu_ok, b_mm, b_ev, res_ok, dt_mm, sp_step, pos_ok, dt_ok, dtx_ok, tap_ok = (
            sem(n) for n in ("ip_mm", "res_mm", "conv_step", "silu_ok", "b_mm", "b_ev", "res_ok", "dt_mm", "sp_step",
                             "pos_ok", "dt_ok", "dtx_ok", "tap_ok"))
        da_ok, u_ok, scan_ok, pair_ok, sum_ok, y_ok, yg_ok, op_mm, x1_ok = (
            sem(n) for n in ("da_ok", "u_ok", "scan_ok", "pair_ok", "sum_ok", "y_ok", "yg_ok", "op_mm", "x1_ok"))
        q_mm, q_ok, c_mm, c_ok, s_mm, fill_ok, inv_ok, pick_ok, max_ok, nmax_ok, exp_ok, rinv_ok = (
            sem(n) for n in ("q_mm", "q_ok", "c_mm", "c_ok", "s_mm", "fill_ok", "inv_ok", "pick_ok", "max_ok",
                             "nmax_ok", "exp_ok", "rinv_ok"))
        pt_mm, pt_ok, av_mm, av_ok, o_mm, xc_ok, x2_ok, r_mm, r_ok = (
            sem(n) for n in ("pt_mm", "pt_ok", "av_mm", "av_ok", "o_mm", "xc_ok", "x2_ok", "r_mm", "r_ok"))
        LN = [{k: sem(f"ln{i}_{k}") for k in ("stat", "mv", "var", "log", "r0", "newton", "xn", "tr", "xT")}
              for i in range(3)]
        XNT = (xnT_m, xnT_a, xnT_a)
        LN_BANKS = (pm, pa, pa)

        def rows(b, t):
            return x_all[:, at(b * T + t), :].rearrange("p a d -> p (a d)")

        def of_row(t, b, j):
            return t[:, at((b % 2) * KI + j), :].rearrange("p a s -> p (a s)")

        scrap_used = [0]

        def take_wait():
            nc.vector.memset(scrap[:, at(scrap_used[0] % 64)], 0.0)
            scrap_used[0] += 1

        def ln_statistics(dve, i, b):
            s, (stat, mv, var, log, r, tmp) = LN[i], ln_buf[i]
            take_wait()
            for t in range(T):
                nc.vector.bn_stats(stat[:, t, :], rows(b, t)).then_inc(s["stat"], 1)
            dve.wait_ge(s["stat"], b * T + T)
            take_wait()
            for t in range(T):
                nc.vector.bn_aggr(mv[:, t, :], stat[:, t, :]).then_inc(s["mv"], 1)
            dve.wait_ge(s["mv"], b * T + T)
            nc.vector.tensor_scalar(var[:], mv[:, :, 1], EPS, None, ALU.add).then_inc(s["var"], 1)

        def ln_root(act, i, b):
            s, (stat, mv, var, log, r, tmp) = LN[i], ln_buf[i]
            act.wait_ge(s["var"], b + 1)
            nc.scalar.activation(log[:], var[:], ACT.Ln).then_inc(s["log"], 1)
            act.wait_ge(s["log"], b + 1)
            nc.scalar.activation(r[:], log[:], ACT.Exp, scale=-0.5).then_inc(s["r0"], 1)

        def ln_normalise(dve, i, b):
            s, (stat, mv, var, log, r, tmp) = LN[i], ln_buf[i]
            dve.wait_ge(s["r0"], b + 1)
            nc.vector.tensor_tensor(tmp[:], r[:], r[:], ALU.mult).then_inc(s["newton"], 1)
            dve.wait_ge(s["newton"], b * 4 + 1)
            nc.vector.tensor_tensor(tmp[:], tmp[:], var[:], ALU.mult).then_inc(s["newton"], 1)
            dve.wait_ge(s["newton"], b * 4 + 2)
            nc.vector.tensor_scalar(tmp[:], tmp[:], -0.5, 1.5, ALU.mult, ALU.add).then_inc(s["newton"], 1)
            dve.wait_ge(s["newton"], b * 4 + 3)
            nc.vector.tensor_tensor(r[:], r[:], tmp[:], ALU.mult).then_inc(s["newton"], 1)
            dve.wait_ge(s["newton"], b * 4 + 4)
            for t in range(T):
                nc.vector.tensor_scalar(xn[:, t, :], rows(b, t), mv[:, t, 0:1], r[:, t:t + 1],
                                        ALU.subtract, ALU.mult).then_inc(s["xn"], 1)

        def ln_transpose(pe, i, b, k):
            for t in range(T):
                pe.wait_ge(LN[i]["xn"], b * T + t + 1)
                last = nc.tensor.transpose(LN_BANKS[i][k][:, t * P:(t + 1) * P], xn[:, t, k * P:(k + 1) * P], ident[:])
            last.then_inc(LN[i]["tr"], 1)

        def ln_evacuate(act, i, b):
            for k in range(KD):
                act.wait_ge(LN[i]["tr"], b * KD + k + 1)
                nc.scalar.copy(XNT[i][:, k, :], LN_BANKS[i][k][:]).then_inc(LN[i]["xT"], 1)

        with nc.Block() as block:

            @block.sync
            def _(sp):
                x = io["x"].rearrange("(g p) d -> p g d", p=P)
                sp.dma_start(x_all[:, 0:T, :], x[:, 0:T, :]).then_inc(x_ld, 16)
                sp.dma_start(w_in[:], io["w_inT"].rearrange("(k p) o -> p k o", p=P)).then_inc(wi_ld, 16)
                sp.dma_start(w_conv[:], io["w_conv"].rearrange("(j p) k -> p j k", p=P)).then_inc(wi_ld, 16)
                sp.dma_start(b_conv[:], io["b_conv"]).then_inc(wi_ld, 16)
                for dst, src in (
                    (w_b, io["w_bT"].rearrange("(k p) n -> p k n", p=P)),
                    (w_dt, io["w_dtT"].rearrange("(k p) o -> p k o", p=P)),
                    (b_dt, io["b_dt"]),
                    (a_neg, io["a_log"].rearrange("(j p) n -> p j n", p=P)),
                    (d_skip, io["d_skip"]),
                    (w_out, io["w_outT"].rearrange("(k p) o -> p k o", p=P)),
                ):
                    sp.dma_start(dst[:], src).then_inc(w_ld, 16)
                sp.dma_start(x_all[:, T:B * T, :], x[:, T:B * T, :]).then_inc(xr_ld, 16)
                sp.wait_ge(zero_ok, 1)
                sp.dma_start(env["ffn_sorted"].rearrange("(n p) d -> p n d", p=P),
                             zeros.unsqueeze(1).to_broadcast([P, NT, D])).then_inc(res_st, 16)

                def context(b):
                    wait(sp, av_mm, b * T)
                    wait(sp, s_mm, b * QCH * T)
                    wait(sp, ctx_ld, b * 48)
                    full = (KC - 1) * P
                    sp.dma_start(ctx_t[:], io["ctxT"][b].rearrange("(k p) s -> p k s", p=P)).then_inc(ctx_ld, 16)
                    sp.dma_start(ctx_n[:, 0:KC - 1, :], io["ctx"][b, 0:full, :].rearrange(
                        "(c p) d -> p c d", p=P)).then_inc(ctx_ld, 16)
                    sp.dma_start(ctx_n[0:S2_LAST, KC - 1, :], io["ctx"][b, full:S2, :]).then_inc(ctx_ld, 16)

                def load_mask(b, q):
                    wait(sp, pick_ok, b * QCH * T + QCH * (q - 1))
                    wait(sp, mask_ld, 16 * (b * T + q))
                    sp.dma_start(mask[:, q % 2, 0:S2], io["mask"][b, q * P:(q + 1) * P, :]).then_inc(mask_ld, 16)

                def store_b(b):
                    sp.wait_ge(b_ev, b + 1)
                    sp.dma_start(b_dram[b].rearrange("(n s) -> n s", n=NST), b_row).then_inc(b_st, 16)

                def load_b(b, c):
                    sp.wait_ge(b_st, 16 * (b + 1))
                    n = NST // NB
                    wait(sp, u_ok, b * STEPS - NST + n * (c + 1))
                    wait(sp, b_ld, 16 * (b * NB + c))
                    sp.dma_start(b_all[:, c * n:(c + 1) * n, :], b_dram[at(b), c * n * S:(c + 1) * n * S].to_broadcast(
                        (P, n * S)).rearrange("p (n s) -> p n s", n=n)).then_inc(b_ld, 16)

                def store_tokens(b):
                    for t in range(T):
                        sp.wait_ge(LN[2]["xn"], b * T + t + 1)
                        sp.dma_start(xn3_dram[at(b * S + t * P, P), :], xn[:, t, :]).then_inc(tok_st, 16)

                store_b(0)
                for c in range(NB):
                    load_b(0, c)
                context(0)
                load_mask(0, 0)
                load_mask(0, 1)
                for b in range(B):
                    if b >= 1:
                        load_mask(b - 1, 2)
                        load_mask(b - 1, 3)
                    if b + 1 < B:
                        store_b(b + 1)
                        load_b(b + 1, 0)
                        load_b(b + 1, 1)
                    if b >= 1:
                        context(b)
                        load_mask(b, 0)
                        load_mask(b, 1)
                    if b + 1 < B:
                        load_b(b + 1, 2)
                        load_b(b + 1, 3)
                    if b >= 1:
                        store_tokens(b - 1)
                load_mask(B - 1, 2)
                load_mask(B - 1, 3)
                store_tokens(B - 1)
                sp.wait_ge(tok_st, 16 * B * T)

            @block.gpsimd
            def _(pool):
                pool.dma_start(wq, io["wq"].rearrange("(k p) d -> p k d", p=P)).then_inc(wa_ld, 16)
                pool.dma_start(wk, io["wk"].rearrange("(k p) d -> p k d", p=P)).then_inc(wa_ld, 16)
                pool.dma_start(wv, io["wv"].rearrange("(k p) d -> p k d", p=P)).then_inc(wa_ld, 16)
                pool.dma_start(wo, io["woT"].rearrange("(k p) d -> p k d", p=P)).then_inc(wa_ld, 16)
                for n, name in enumerate(("bq", "bk", "bv")):
                    pool.dma_start(b_qkv[:, n, :], io[name]).then_inc(wa_ld, 16)
                pool.dma_start(bo_row, io["bo"].rearrange("(a d) -> a d", a=1)).then_inc(wa_ld, 16)
                pool.dma_start(w_g[:], io["w_gT"].rearrange("(k p) e -> p k e", p=P)).then_inc(wa_ld, 16)
                nc.gpsimd.memset(ident[:], 0.0).then_inc(id_zero, 1)
                nc.gpsimd.memset(ones, 1.0).then_inc(ones_ok, 1)
                nc.gpsimd.memset(zeros, 0.0).then_inc(zero_ok, 1)
                pool.wait_ge(id_zero, 1)
                nc.gpsimd.affine_select(out=ident[:], in_=ident[:], compare_op=ALU.not_equal, fill=1.0, base=0,
                                        pattern=[[-1, P]], channel_multiplier=1).then_inc(id_ok, 1)
                def times_x(b, j):
                    pool.wait_ge(dt_ok, b * KI + j + 1)
                    nc.gpsimd.tensor_tensor(dtx[:, j % 2, :], dt_[:, j % 2, :], of_row(xs, b, j), ALU.mult).then_inc(dtx_ok, 1)

                def body(b, scan, inp, att_):
                    when = AT if scan else ALONE
                    a, m = b - 1, b + 1
                    for i in range(STEPS):
                        j, n = divmod(i, NST)
                        if scan:
                            if i == 0 and not att_:
                                pool.wait_ge(setup_mm, 1)
                            if j == 0 and n % (NST // NB) == 0:
                                pool.wait_ge(b_ld, 16 * (b * NB + n // (NST // NB) + 1))
                            if n == 0:
                                pool.wait_ge(dtx_ok, b * KI + j + 1)
                            wait(pool, scan_ok, b * STEPS + i - 1)
                            nc.gpsimd.tensor_tensor(u[:, i % 2, :], dtx[:, j % 2, :], b_all[:, n, :],
                                                    ALU.mult).then_inc(u_ok, 1)
                            for k in range(1, KI):
                                if i == when["dtx"][k]:
                                    times_x(b, k)
                        if inp and i == when["dtx"][0]:
                            times_x(m, 0)
                        if att_:
                            if i == when["x_bias"]:
                                for t in range(T):
                                    pool.wait_ge(LN[1]["xn"], a * T + T)
                                    nc.gpsimd.tensor_tensor(rows(a, t), rows(a, t), c_vo[:], ALU.add).then_inc(xc_ok, 1)
                            for q in range(T):
                                if i == when["fill"][q]:
                                    pool.wait_ge(c_ok, a + 1)
                                    pool.wait_ge(mask_ld, 16 * (a * T + q + 1))
                                    if q >= 2:
                                        pool.wait_ge(pt_mm, a * NPT * T + NPT * (q - 1))
                                    nc.gpsimd.tensor_tensor(pool_scrap[:, q:q + 1], ident[:, 0:1], ident[:, 0:1], ALU.mult)
                                    nc.gpsimd.tensor_scalar(sim[:, q % 2, :], mask[:, q % 2, 0:S2], 0.0, neg_c[:, q:q + 1],
                                                            ALU.mult, ALU.add).then_inc(fill_ok, 1)
                                    nc.gpsimd.tensor_scalar(mask[:, q % 2, 0:S2], mask[:, q % 2, 0:S2], -1.0, 1.0,
                                                            ALU.mult, ALU.add).then_inc(inv_ok, 1)

                body(-1, False, True, False)
                body(0, True, True, False)
                with pool.Fori(1, B - 1) as b:
                    body(b, True, True, True)
                body(B - 1, True, False, True)
                body(B, False, False, True)

            @block.scalar
            def _(act):
                def exp_and_ln():
                    nc.scalar.preload_act_table_set("natural_log_exp_and_others")

                exp_and_ln()

                def softplus(b, j):
                    act.wait_ge(dt_mm, b * KI + j + 1)
                    if j == 0:
                        act.wait_ge(b_st, 16 * (b + 1))
                    z, e, n = DT_BANKS[j], dt_[:, j % 2, :], 3 * (b * KI + j)
                    nc.scalar.activation(e, z[:], ACT.Abs, bias=b_dt[:, j:j + 1]).then_inc(sp_step, 1)
                    nc.scalar.activation(sp_pos[:], z[:], ACT.Relu, bias=b_dt[:, j:j + 1]).then_inc(pos_ok, 1)
                    act.wait_ge(sp_step, n + 1)
                    nc.scalar.activation(e, e, ACT.Exp, scale=-1.0).then_inc(sp_step, 1)
                    act.wait_ge(sp_step, n + 2)
                    nc.scalar.activation(e, e, ACT.Ln, bias=1.0).then_inc(sp_step, 1)

                def silu_conv(m):
                    act.wait_ge(conv_step, (TAPS - 1) * (m * KI + KI))
                    nc.scalar.copy(act_scrap[:, KI:KI + 1], ident[:, 0:1])
                    for j in range(KI):
                        nc.scalar.activation(of_row(xs, m, j), of_row(xs, m, j), ACT.Silu).then_inc(silu_ok, 1)
                    exp_and_ln()

                def silu_res(b):
                    for j in range(KI):
                        act.wait_ge(res_mm, b * KI + j + 1)
                        nc.scalar.activation(gate[:, j, :], RES_BANKS[j][:], ACT.Silu).then_inc(res_ok, 1)
                    exp_and_ln()

                def body(b, scan, inp, att_):
                    when = AT if scan else ALONE
                    a, m = b - 1, b + 1
                    exp_and_ln()
                    for i in range(STEPS):
                        j, n = divmod(i, NST)
                        if scan:
                            if i == 0 and not att_:
                                act.wait_ge(a_ok, 1)
                            if n == 0:
                                act.wait_ge(dt_ok, b * KI + j + 1)
                            wait(act, scan_ok, b * STEPS + i - DS + 1)
                            nc.scalar.activation(da[:, i % DS, :], dt_[:, j % 2, :], ACT.Exp,
                                                 scale=a_neg[:, j, n:n + 1]).then_inc(da_ok, 1)
                            for k in range(1, KI):
                                if i == when["softplus"][k]:
                                    softplus(b, k)
                            if i == when["res_silu"]:
                                if att_:
                                    act.wait_ge(yg_ok, b * KI)
                                silu_res(b)
                        if inp:
                            if i == when["ln_m_root"]:
                                ln_root(act, 0, m)
                            if i == when["ln_m_copy"]:
                                ln_evacuate(act, 0, m)
                            for k in range(KI):
                                if i == when["tap"][k]:
                                    if not scan:
                                        act.wait_ge(wi_ld, 48)
                                    act.wait_ge(ip_mm, m * KI + k + 1)
                                    nc.scalar.copy(act_scrap[:, k:k + 1], ident[:, 0:1])
                                    nc.scalar.activation(of_row(xs, m, k), CONV_BANKS[k][:], ACT.Identity, bias=b_conv[:, k:k + 1],
                                                         scale=w_conv[:, k, TAPS - 1:TAPS]).then_inc(tap_ok, 1)
                            if i == when["conv_silu"]:
                                silu_conv(m)
                            if i == when["b_copy"]:
                                act.wait_ge(b_mm, m + 1)
                                if scan:
                                    act.wait_ge(dt_ok, b * KI + KI)
                                nc.scalar.copy(b_row, pm[0][0:NST, :]).then_inc(b_ev, 1)
                            if i == when["softplus"][0]:
                                if not scan:
                                    act.wait_ge(w_ld, 16 * 6)
                                    nc.scalar.activation(a_neg[:], a_neg[:], ACT.Exp).then_inc(a_exp, 1)
                                softplus(m, 0)
                        if att_:
                            if i == when["ln_a_root"]:
                                ln_root(act, 1, a)
                            if i == when["ln_a_copy"]:
                                ln_evacuate(act, 1, a)
                            if i == when["query_copy"]:
                                act.wait_ge(q_mm, a * KD + KD)
                                for k in range(KD):
                                    nc.scalar.activation(xnT_a[:, k, :], pa[k][:], ACT.Identity,
                                                         bias=bq_k[:, k:k + 1]).then_inc(q_ok, 1)
                            for q in range(T):
                                s = i - when["tile"][q]
                                if s == when["exp"]:
                                    act.wait_ge(nmax_ok, a * T + q + 1)
                                    nc.scalar.activation(sim[:, q % 2, :], sim[:, q % 2, :], ACT.Exp,
                                                         bias=row_max[:, q:q + 1],
                                                         accum_out=row_sum[:, q:q + 1]).then_inc(exp_ok, 1)
                                if s in when["p_copy"]:
                                    g = when["p_copy"].index(s)
                                    act.wait_ge(pt_mm, a * NPT * T + NPT * q + g + 1)
                                    if q:
                                        act.wait_ge(av_mm, a * T + q)
                                    chunks = min(4, KC - 4 * g)
                                    rows_in = S2_LAST if chunks == 1 else P
                                    assert g < NPT - 1 or chunks == 1
                                    nc.scalar.copy(pT[0:rows_in, 4 * g:4 * g + chunks, :],
                                                   pt[g % 2][0:rows_in, 0:chunks * P].rearrange("p (c m) -> p c m", m=P)
                                                   ).then_inc(pt_ok, 1)
                                if s == when["av_copy"]:
                                    act.wait_ge(av_mm, a * T + q + 1)
                                    if q:
                                        act.wait_ge(o_mm, a * T + q)
                                    nc.scalar.copy(attT[:], pv[:, 0:D].rearrange("p (k m) -> p k m", k=KD)).then_inc(av_ok, 1)
                            if i == when["ln_f_root"]:
                                ln_root(act, 2, a)
                            if i == when["ln_f_copy"]:
                                ln_evacuate(act, 2, a)

                body(-1, False, True, False)
                body(0, True, True, False)
                with act.Fori(1, B - 1) as b:
                    body(b, True, True, True)
                body(B - 1, True, False, True)
                body(B, False, False, True)

            @block.vector
            def _(dve):
                def set_up_biases():
                    dve.wait_ge(ones_ok, 1)
                    dve.wait_ge(wa_ld, 16 * 9)
                    for k in range(KD):
                        nc.vector.tensor_scalar(bk_b[:, k, :], ones, b_qkv[:, 1, k:k + 1], None, ALU.mult).then_inc(bias_b, 1)
                        nc.vector.tensor_scalar(bv_b[:, k, :], ones, b_qkv[:, 2, k:k + 1], None, ALU.mult).then_inc(bias_b, 1)

                def set_up_products():
                    dve.wait_ge(a_exp, 1)
                    nc.vector.tensor_scalar(a_neg[:], a_neg[:], -1.0, None, ALU.mult).then_inc(a_ok, 1)
                    dve.wait_ge(setup_mm, 1)
                    flat = "p k d -> p (k d)"
                    nc.vector.tensor_copy(w_qk[:].rearrange(flat), pa[0][:, 0:KD * D]).then_inc(setup_ok, 1)
                    nc.vector.tensor_copy(w_vo[:].rearrange(flat), pa[1][:, 0:KD * D]).then_inc(setup_ok, 1)
                    nc.vector.tensor_copy(c_vo[:], pt[0][:, 0:D]).then_inc(setup_ok, 1)
                    nc.vector.tensor_copy(wq_bk[:], pt[0][:, D:D + KD]).then_inc(setup_ok, 1)
                    nc.vector.tensor_copy(bq_k[:], pt[0][:, D + KD:D + 2 * KD]).then_inc(setup_ok, 1)
                    nc.vector.tensor_scalar(neg_c0[:], pt[0][:, D + 2 * KD:D + 2 * KD + 1], -1.0, MASKED, ALU.mult,
                                            ALU.add).then_inc(setup_ok, 1)
                    dve.wait_ge(setup_ok, 6)

                def convolve(m, j):
                    x_ps, n = CONV_BANKS[j], (TAPS - 1) * (m * KI + j)
                    if isinstance(m, int) and m == 0:
                        dve.wait_ge(wi_ld, 48)
                    dve.wait_ge(tap_ok, m * KI + j + 1)
                    for s in range(1, TAPS):
                        if s > 1:
                            dve.wait_ge(conv_step, n + s - 1)
                        tail = xs[:, at((m % 2) * KI + j), s:S].rearrange("p a s -> p (a s)")
                        nc.vector.scalar_tensor_tensor(
                            out=tail, in0=x_ps[:, 0:S - s], scalar=w_conv[:, j, TAPS - 1 - s:TAPS - s],
                            in1=tail, op0=ALU.mult, op1=ALU.add).then_inc(conv_step, 1)

                def add_softplus(b, j):
                    dve.wait_ge(pos_ok, b * KI + j + 1)
                    dve.wait_ge(sp_step, 3 * (b * KI + j + 1))
                    nc.vector.tensor_tensor(dt_[:, j % 2, :], sp_pos[:], dt_[:, j % 2, :], ALU.add).then_inc(dt_ok, 1)

                def read_out(b, j):
                    dve.wait_ge(sum_ok, b * PAIRS + NST // 2 * (j + 1))
                    nc.vector.scalar_tensor_tensor(out=dtx[:, j % 2, :], in0=of_row(xs, b, j), scalar=d_skip[:, j:j + 1],
                                                   in1=ysum[:], op0=ALU.mult, op1=ALU.add).then_inc(y_ok, 1)
                    dve.wait_ge(y_ok, b * KI + j + 1)
                    if isinstance(b, int) and b == 0 and j == 0:
                        dve.wait_ge(res_st, 16)
                        dve.wait_ge(res_st, 16)
                    nc.vector.tensor_tensor(yg[:, j, :], dtx[:, j % 2, :], gate[:, j, :], ALU.mult).then_inc(yg_ok, 1)

                def pick(a, q, c):
                    lo, hi = CHUNKS[c]
                    if c == 0:
                        dve.wait_ge(inv_ok, a * T + q + 1)
                    dve.wait_ge(s_mm, a * QCH * T + QCH * q + c + 1)
                    take_wait()
                    nc.vector.copy_predicated(sim[:, q % 2, lo:hi], mask[:, q % 2, lo:hi], pa[c % 2][:, 0:hi - lo]).then_inc(pick_ok, 1)

                def maximum(a, q):
                    dve.wait_ge(pick_ok, a * QCH * T + QCH * (q + 1))
                    nc.vector.reduce_max(row_max[:, q:q + 1], sim[:, q % 2, :], AX_X).then_inc(max_ok, 1)
                    dve.wait_ge(max_ok, a * T + q + 1)
                    nc.vector.tensor_scalar(row_max[:, q:q + 1], row_max[:, q:q + 1], -1.0, None,
                                            ALU.mult).then_inc(nmax_ok, 1)

                def add_pair(b, p):
                    k = 2 * p % HS
                    dve.wait_ge(scan_ok, b * STEPS + 2 * p + 2)
                    nc.vector.tensor_tensor(h[:, k, :], h[:, k, :], h[:, k + 1, :], ALU.add).then_inc(pair_ok, 1)

                def body(b, scan, inp, att_):
                    when = AT if scan else ALONE
                    a, m = b - 1, b + 1
                    for i in range(STEPS):
                        j, n = divmod(i, NST)
                        if scan:
                            dve.wait_ge(da_ok, b * STEPS + i + 1)
                            dve.wait_ge(u_ok, b * STEPS + i + 1)
                            if i % 2 == 0:
                                wait(dve, sum_ok, b * PAIRS + i // 2 - HS // 2 + 1)
                            nc.vector.tensor_tensor_scan(h[:, i % HS, :], da[:, i % DS, :], u[:, i % 2, :], 0.0,
                                                         ALU.mult, ALU.add).then_inc(scan_ok, 1)
                            if i >= 2 and i % 2 == 0:
                                add_pair(b, i // 2 - 1)
                            if j > 0 and n == 2:
                                read_out(b, j - 1)
                            for k in range(1, KI):
                                if i == when["dt_add"][k]:
                                    add_softplus(b, k)
                        if att_:
                            if i == 0:
                                add_pair(a, PAIRS - 1)
                            if i == when["last_y"]:
                                read_out(a, KI - 1)
                            for t in range(T):
                                if i == when["x1"][t // 2]:
                                    dve.wait_ge(op_mm, a * T + t // 2 * 2 + 2)
                                    nc.vector.tensor_tensor(rows(a, t), rows(a, t), pm[t // 2][:, t % 2 * D:t % 2 * D + D],
                                                            ALU.add).then_inc(x1_ok, 1)
                        if inp:
                            if i == when["ln_m_stat"]:
                                if not scan:
                                    dve.wait_ge(x_ld, 16)
                                elif not att_:
                                    dve.wait_ge(xr_ld, 16)
                                ln_statistics(dve, 0, m)
                            if i == when["ln_m_norm"]:
                                if att_:
                                    dve.wait_ge(LN[1]["tr"], a * KD + KD)
                                ln_normalise(dve, 0, m)
                            for k in range(KI):
                                if i == when["conv"][k]:
                                    convolve(m, k)
                            if not scan and i == when["conv_silu"]:
                                set_up_biases()
                            if i == when["dt_add"][0]:
                                add_softplus(m, 0)
                                if not scan:
                                    set_up_products()
                        if att_:
                            if i == when["ln_a_stat"]:
                                dve.wait_ge(x1_ok, a * T + T)
                                ln_statistics(dve, 1, a)
                            if i == when["ln_a_norm"]:
                                dve.wait_ge(tok_st, 16 * T * a)
                                ln_normalise(dve, 1, a)
                            if i == when["row_const"]:
                                dve.wait_ge(c_mm, a + 1)
                                nc.vector.tensor_scalar(neg_c[:], pt[0][:, 0:T], -1.0, neg_c0[:], ALU.mult,
                                                        ALU.add).then_inc(c_ok, 1)
                            for q in range(T):
                                s = i - when["tile"][q]
                                if s in when["pick"]:
                                    pick(a, q, when["pick"].index(s))
                                if s == when["max"]:
                                    maximum(a, q)
                                if s == when["inverse"]:
                                    dve.wait_ge(exp_ok, a * T + q + 1)
                                    nc.vector.reciprocal(row_inv[:, q:q + 1], row_sum[:, q:q + 1]).then_inc(rinv_ok, 1)
                                if i == when["x2"][q]:
                                    dve.wait_ge(o_mm, a * T + q + 1)
                                    dve.wait_ge(xc_ok, a * T + q + 1)
                                    dve.wait_ge(rinv_ok, a * T + q + 1)
                                    nc.vector.scalar_tensor_tensor(out=rows(a, q), in0=pm[1][:, 0:D], scalar=row_inv[:, q:q + 1],
                                                                   in1=rows(a, q), op0=ALU.mult, op1=ALU.add).then_inc(x2_ok, 1)
                            if i == when["ln_f_stat"]:
                                dve.wait_ge(x2_ok, a * T + T)
                                ln_statistics(dve, 2, a)
                            if i == when["ln_f_norm"]:
                                if inp:
                                    dve.wait_ge(LN[0]["tr"], m * KD + KD)
                                ln_normalise(dve, 2, a)
                            if i == when["scores"]:
                                dve.wait_ge(r_mm, a + 1)
                                nc.vector.tensor_copy(scores[:, at(a * T, T), :], pv[:, 0:T * E].rearrange(
                                    "p (t e) -> p t e", e=E)).then_inc(r_ok, 1)

                body(-1, False, True, False)
                body(0, True, True, False)
                with dve.Fori(1, B - 1) as b:
                    body(b, True, True, True)
                body(B - 1, True, False, True)
                body(B, False, False, True)

            @block.tensor
            def _(pe):
                def set_up():
                    pe.wait_ge(wa_ld, 16 * 9)
                    pe.wait_ge(bias_b, 2 * KD)
                    for k in range(KD):
                        for out, lhs, rhs in ((pa[0], wq, wk), (pa[1], wv, wo)):
                            for e in range(KD):
                                nc.tensor.matmul(out[:, k * D:(k + 1) * D], lhs[:, e, k * P:(k + 1) * P], rhs[:, e, :],
                                                 start=e == 0, stop=e == KD - 1)
                    for e in range(KD):
                        nc.tensor.matmul(pt[0][:, 0:D], bv_b[:, e, :], wo[:, e, :], start=e == 0, stop=False)
                    nc.tensor.matmul(pt[0][:, 0:D], ones[0:1, :], bo_row, start=False, stop=True)
                    for k in range(KD):
                        for col, w, v in ((D + k, wq, 1), (D + KD + k, wk, 0)):
                            for e in range(KD):
                                nc.tensor.matmul(pt[0][:, col:col + 1], w[:, e, k * P:(k + 1) * P], b_qkv[:, v, e:e + 1],
                                                 start=e == 0, stop=e == KD - 1)
                    col = D + 2 * KD
                    for e in range(KD):
                        last = nc.tensor.matmul(pt[0][:, col:col + 1], bk_b[:, e, :], b_qkv[:, 0, e:e + 1],
                                                start=e == 0, stop=e == KD - 1)
                    last.then_inc(setup_mm, 1)

                def project_in(m, j, bank, done):
                    for k in range(KD):
                        last = nc.tensor.matmul(bank[:], w_in[:, k, j * P:(j + 1) * P], xnT_m[:, k, :],
                                                start=k == 0, stop=k == KD - 1)
                    last.then_inc(done, 1)

                def project_dt(b, j, half):
                    for k in range(half * KI // 2, (half + 1) * KI // 2):
                        last = nc.tensor.matmul(DT_BANKS[j][:], w_dt[:, k, j * P:(j + 1) * P], of_row(xs, b, k),
                                                start=k == 0, stop=k == KI - 1)
                    if half == 1:
                        last.then_inc(dt_mm, 1)

                def sum_pair(b, p):
                    if p % (NST // 2) == 0:
                        wait(pe, y_ok, b * KI + p // (NST // 2))
                    pe.wait_ge(pair_ok, b * PAIRS + p + 1)
                    nc.tensor.matmul(ysum[:], ident[:], h[:, 2 * p % HS, :], start=p % (NST // 2) == 0,
                                     stop=(p + 1) % (NST // 2) == 0).then_inc(sum_ok, 1)

                def mamba_in(b, i, scan, att_):
                    when = AT if scan else ALONE
                    m = b + 1
                    if i == when["ln_m_turn"]:
                        if not scan:
                            pe.wait_ge(id_ok, 1)
                        if scan:
                            pe.wait_ge(pos_ok, b * KI + 3)
                            pe.wait_ge(res_ok, b * KI + 2)
                        for k in range(KD):
                            ln_transpose(pe, 0, m, k)
                    for j in range(KI):
                        if i == when["in_proj"][j]:
                            if not scan:
                                pe.wait_ge(wi_ld, 48)
                            if j < 2:
                                pe.wait_ge(LN[0]["xT"], m * KD + KD)
                            elif j == 2 and att_:
                                pe.wait_ge(x2_ok, (b - 1) * T + 1)
                            elif j == 2:
                                pe.wait_ge(conv_step, (TAPS - 1) * (m * KI + 2))
                            elif scan:
                                pe.wait_ge(pos_ok, b * KI + KI)
                            else:
                                pe.wait_ge(conv_step, (TAPS - 1) * (m * KI + 1))
                            project_in(m, j, CONV_BANKS[j], ip_mm)
                    if i == when["b_proj"]:
                        if not scan:
                            pe.wait_ge(w_ld, 16 * 6)
                        pe.wait_ge(silu_ok, m * KI + KI)
                        for k in range(KI):
                            last = nc.tensor.matmul(pm[0][0:NST, :], w_b[:, k, :], of_row(xs, m, k),
                                                    start=k == 0, stop=k == KI - 1)
                        last.then_inc(b_mm, 1)
                    for half in range(2):
                        if i == when["dt_proj"][0] + half:
                            if half == 0:
                                pe.wait_ge(b_ev, m + 1)
                            project_dt(m, 0, half)
                            if half == 1 and not scan:
                                set_up()

                def mamba_rest(b, i, inp, att_):
                    when = AT
                    for half in range(2):
                        if i == when["dt_proj"][1] + half:
                            project_dt(b, 1, half)
                        if i == when["dt_proj"][2] + half:
                            if half == 0:
                                pe.wait_ge(res_ok, b * KI + 1)
                            project_dt(b, 2, half)
                        if i == when["dt_proj"][3] + half:
                            if half == 0 and inp:
                                pe.wait_ge(conv_step, (TAPS - 1) * ((b + 1) * KI + 1))
                            elif half == 0:
                                pe.wait_ge(pos_ok, b * KI + 3)
                            project_dt(b, 3, half)
                    for j in range(KI):
                        if i == when["res_proj"][j]:
                            if att_:
                                pe.wait_ge(x1_ok, (b - 1) * T + (2 if j == 0 else T))
                            elif j == 0:
                                pe.wait_ge(pos_ok, b * KI + 1)
                            project_in(b, KI + j, RES_BANKS[j], res_mm)

                def attention(a, i, scan, inp):
                    when = AT if scan else ALONE
                    b = a + 1
                    for t in range(T):
                        if i == when["out_proj"][t // 2]:
                            if t == 0:
                                pe.wait_ge(yg_ok, a * KI + KI)
                                pe.wait_ge(pos_ok, b * KI + 1 if scan else B * KI)
                            for j in range(KI):
                                last = nc.tensor.matmul(pm[t // 2][:, t % 2 * D:t % 2 * D + D], yg[:, j, t * P:(t + 1) * P],
                                                        w_out[:, j, :], start=j == 0, stop=j == KI - 1)
                            last.then_inc(op_mm, 1)
                    if i == when["ln_a_turn"]:
                        for k in range(KD):
                            ln_transpose(pe, 1, a, k)
                    if i == when["query"]:
                        pe.wait_ge(LN[1]["xT"], a * KD + KD)
                        if scan:
                            pe.wait_ge(pos_ok, b * KI + 2)
                        for t in range(T):
                            for k in range(KD):
                                last = nc.tensor.matmul(pt[0][:, t:t + 1], xnT_a[:, k, t * P:(t + 1) * P],
                                                        wq_bk[:, k:k + 1], start=k == 0, stop=k == KD - 1)
                        last.then_inc(c_mm, 1)
                        for o in range(KD):
                            for k in range(KD):
                                last = nc.tensor.matmul(pa[o][:], w_qk[:, k, o * P:(o + 1) * P], xnT_a[:, k, :],
                                                        start=k == 0, stop=k == KD - 1)
                            last.then_inc(q_mm, 1)
                    for q in range(T):
                        s = i - when["tile"][q]
                        if s in when["score"]:
                            c = when["score"].index(s)
                            lo, hi = CHUNKS[c]
                            if q == 0 and c == 0:
                                pe.wait_ge(q_ok, a * KD + KD)
                                pe.wait_ge(ctx_ld, 48 * (a + 1))
                            if q > 0 or c >= 2:
                                pe.wait_ge(pick_ok, QCH * (a * T + q) + c - 1)
                            for k in range(KD):
                                last = nc.tensor.matmul(pa[c % 2][:, 0:hi - lo], xnT_a[:, k, q * P:(q + 1) * P],
                                                        ctx_t[:, k, lo:hi], start=k == 0, stop=k == KD - 1)
                            last.then_inc(s_mm, 1)
                        if s in when["p_turn"]:
                            g = when["p_turn"].index(s)
                            if g == 0:
                                pe.wait_ge(exp_ok, a * T + q + 1)
                            if q > 0 or g >= 2:
                                pe.wait_ge(pt_ok, NPT * (a * T + q) + g - 1)
                            elif g == 0:
                                pe.wait_ge(c_ok, a + 1)
                            elif scan:
                                pe.wait_ge(res_ok, b * KI + 3)
                            for c in range(4 * g, min(4 * g + 4, KC)):
                                w = P if c < KC - 1 else S2_LAST
                                last = nc.tensor.transpose(pt[g % 2][0:w, (c - 4 * g) * P:(c - 4 * g + 1) * P],
                                                           sim[:, q % 2, c * P:c * P + w], ident[:])
                            last.then_inc(pt_mm, 1)
                        if s in when["av"]:
                            g = when["av"].index(s)
                            if q > 0 and g == 0:
                                pe.wait_ge(av_ok, a * T + q)
                            elif scan and g == 0:
                                pe.wait_ge(res_ok, b * KI + KI)
                            pe.wait_ge(pt_ok, NPT * (a * T + q) + g + 1)
                            for c in range(4 * g, min(4 * g + 4, KC)):
                                w = P if c < KC - 1 else S2_LAST
                                for k in range(KD):
                                    last = nc.tensor.matmul(pv[:, k * P:(k + 1) * P], ctx_n[0:w, c, k * P:(k + 1) * P],
                                                            pT[0:w, c, :], start=c == 0 and k == 0,
                                                            stop=c == KC - 1 and k == KD - 1)
                            if g == NPT - 1:
                                last.then_inc(av_mm, 1)
                        if i == when["out"][q]:
                            pe.wait_ge(av_ok, a * T + q + 1)
                            if q > 0:
                                pe.wait_ge(x2_ok, a * T + q)
                            if q < 2 and inp:
                                pe.wait_ge(conv_step, (TAPS - 1) * ((a + 2) * KI + q + 2))
                            for k in range(KD):
                                last = nc.tensor.matmul(pm[1][:, 0:D], attT[:, k, :], w_vo[:, k, :],
                                                        start=k == 0, stop=k == KD - 1)
                            last.then_inc(o_mm, 1)
                    if i == when["ln_f_turn"]:
                        for k in range(KD):
                            ln_transpose(pe, 2, a, k)
                    if i == when["router"]:
                        pe.wait_ge(LN[2]["xT"], a * KD + KD)
                        for t in range(T):
                            for k in range(KD):
                                last = nc.tensor.matmul(pv[:, t * E:(t + 1) * E], xnT_a[:, k, t * P:(t + 1) * P],
                                                        w_g[:, k, :], start=k == 0, stop=k == KD - 1)
                        last.then_inc(r_mm, 1)

                def body(b, scan, inp, att_):
                    when = AT if scan else ALONE
                    for i in range(STEPS):
                        if att_ and i == 0:
                            sum_pair(b - 1, PAIRS - 1)
                        if scan and i >= 2 and i % 2 == 0:
                            sum_pair(b, i // 2 - 1)
                        if att_:
                            attention(b - 1, i, scan, inp)
                        if scan:
                            mamba_rest(b, i, inp, att_)
                        if inp:
                            mamba_in(b, i, scan, att_)

                body(-1, False, True, False)
                body(0, True, True, False)
                with pe.Fori(1, B - 1) as b:
                    body(b, True, True, True)
                body(B - 1, True, False, True)
                body(B, False, False, True)


def routed_ffn_phase(nc, io, dims, env, sem, buf):
    B, S, D, S2, DI, NST, TAPS, E, HF = dims
    KD, G, KH, H_LAST, HH, NT = (env[k] for k in ("KD", "G", "KH", "H_LAST", "HH", "NT"))
    x_all, ident, scores = env["x_all"], env["ident"], env["scores"]
    ffn_sorted, xn3_dram = env["ffn_sorted"], env["xn3_dram"]
    NGU = KD * HF
    NW = 2 * NGU + KH * D
    PARTS = ((0, 2 * NGU), (2 * NGU, NW))
    COLS = NT + NT % 2
    LOOP = NT + 2

    with ExitStack() as ctx:
        def sb(name, shape, dt=F32):
            return buf(ctx, name, shape, dt)

        w_raw = sb("w_raw", [P, 2, NW])
        w_hi = sb("w_hi", [P, 2 * NW], F32R)
        w_lo = sb("w_lo", [P, 2 * NW], F32R)
        tok_in = sb("tok_in", [P, 2, D])
        tok = sb("tok", [P, NT, D])
        tokT_hi = sb("tokT_hi", [P, 2, KD * P], F32R)
        tokT_lo = sb("tokT_lo", [P, 2, KD * P], F32R)
        act_ = sb("act_", [P, HF])
        hid = sb("hid", [P, 2, HF])
        hidT_hi = sb("hidT_hi", [P, KH, P], F32R)
        hidT_lo = sb("hidT_lo", [P, KH, P], F32R)
        y_sb = sb("y_sb", [P, 2, D])
        tri = sb("tri", [P, P])
        ones = sb("ones2", [P, P])
        iot = sb("iot", [P, P], I32)
        iot_f = sb("iot_f", [P, P])
        num = sb("num", [P, G], I32)
        num_f = sb("num_f", [P, G])
        q_i = sb("q_i", [P, 2, G], I32)
        q_f = sb("q_f", [P, 2, G])
        r_f = sb("r_f", [P, 2, G])
        tok_id = sb("tok_id", [P, NT], U32)
        rev = sb("rev", [P, E])
        tile_id = sb("tile_id", [1, LOOP])
        w_top = sb("w_top", [P, 2, G])
        first = sb("first", [P, 2, G])
        w_low = sb("w_low", [P, 2, G])
        w_part = sb("w_part", [P, 2, G])
        eq = sb("eq", [P, G, E])
        oh = sb("oh", [P, 2, G, E])
        rest = sb("rest", [P, G, E])
        km = sb("km", [P, G])
        both = sb("both", [P, G, E])
        tot = sb("tot", [P, E, G])
        seg = sb("seg", [P, E, G])
        inc = sb("inc", [P, E, G])
        slot = sb("slot", [P, G, E])
        pos_f = sb("pos_f", [P, 2, G])
        pos = sb("pos", [P, 2, G], U32)
        cnt_i = sb("cnt_i", [P, E], I32)
        cnt_f = sb("cnt_f", [P, E])
        tiles = sb("tiles", [P, E])
        tend = sb("tend", [P, E])
        ge = sb("ge", [1, LOOP, E])
        tile_e = sb("tile_e", [1, LOOP])
        tile_expert = sb("tile_expert", [1, LOOP], I32)
        y_one = sb("y_one", [P, G, D])
        y_two = tok[:, 0:G, :]
        place_row = w_lo[:, NW:NW + 2 * G * P].rearrange("p (k g m) -> p k g m", k=2, g=G)
        place_tile = w_lo[:, 0:2 * G * COLS].rearrange("p (k g t) -> p k g t", k=2, g=G)
        hot_tile = tok[:].rearrange("p i d -> p (i d)")[:, 0:2 * G * COLS].rearrange("p (k g t) -> p k g t", k=2, g=G)
        tile_end = sb("tile_end", [1, E + 2], I32)
        silu_scrap = sb("silu_scrap", [P, 1])
        pool_scrap2 = sb("pool_scrap2", [P, 16])

        def ps(name, n=512):
            return ctx.enter_context(nc.psum_tensor(name, [P, n], F32))

        ps_g = [ps("ps_g0"), ps("ps_g1")]
        ps_u = [ps("ps_u0"), ps("ps_u1")]
        ps_x, ps_h0, ps_h1, ps_y = ps("ps_x"), ps("ps_h0"), ps("ps_h1"), ps("ps_y")

        iota_ok, tri_zero, tri_ok, one_ok = (sem(n) for n in ("iota_ok", "tri_zero", "tri_ok", "one_ok"))
        step, mask_ok, rank_mm, pos_ok2, tab_ok = (sem(n) for n in ("step", "mask_ok", "rank_mm", "pos_ok2", "tab_ok"))
        tile_hot, row_hot, id_mm, id_ok = (sem(n) for n in ("tile_hot", "row_hot", "id_mm", "tok_id_ok"))
        out_st = sem("out_st")
        first_ld, wts_ld = ([sem(f"{n}{p}") for p in range(2)] for n in ("first_ld", "wts_ld"))
        w_pad, hi_ok, w_ok = sem("w_pad"), sem("hi_ok"), sem("w_ok")
        tile_ld, y_st = ([sem(f"{n}{p}") for p in range(2)] for n in ("tile_ld", "y_st"))
        PAIRS = 4
        tok_ld = [sem(f"tok_ld{n}") for n in range(PAIRS)]
        AHEAD = 4

        def so_far(i, p):
            return i * 8 + 16 - 8 * p

        x_mm, xT_hi, xT_lo, gu_mm, silu2_ok, hid_ok, h_mm, hT_hi, hT_lo, y_mm, y_ok2 = (
            sem(n) for n in ("x_mm", "xT_hi", "xT_lo", "gu_mm", "silu2_ok", "hid_ok", "h_mm", "hT_hi", "hT_lo", "y_mm",
                             "y_ok2"))
        low_ld, up_ld, comb = sem("low_ld"), [sem(f"up_ld{g}") for g in range(G // 2)], sem("comb")

        def load_expert(eng, e, p, done):
            w, full, last = w_raw[:, p, :], (KH - 1) * P, NW - D
            for n, src in enumerate((io["w1T"], io["w2T"])):
                eng.dma_start(w[:, n * NGU:(n + 1) * NGU].rearrange("p (k h) -> p k h", k=KD),
                              src[at(e)].rearrange("a (k p) h -> p (a k) h", p=P)).then_inc(done, 16)
            eng.dma_start(w[:, 2 * NGU:last].rearrange("p (c d) -> p c d", d=D),
                          io["w3T"][at(e), 0:full, :].rearrange("a (c p) d -> p (a c) d", p=P)).then_inc(done, 16)
            eng.dma_start(w[0:H_LAST, last:NW], io["w3T"][at(e), full:HF, :].rearrange("a p d -> p (a d)")
                          ).then_inc(done, 16)

        def gathered(i):
            return 32 * (i // (2 * PAIRS) + 1) - (16 if i == NT - 1 and NT % 2 else 0)

        def reload(eng, e, p, done):
            eng.wait_ge(w_ok, 2 * e + 2)
            load_expert(eng, e + 2, p, done)

        with nc.Block() as block:

            @block.sync
            def _(sp):
                load_expert(sp, 0, 0, first_ld[0])
                load_expert(sp, 1, 1, first_ld[1])

                def load(i, q):
                    come = gathered(i) if isinstance(i, int) else (i - q) * (16 // PAIRS) + 32
                    sp.wait_ge(tok_ld[q // 2], come)
                    sp.dma_start(tok_in[:, q % 2, :], tok[:, at(i), :].rearrange("p a d -> p (a d)")
                                 ).then_inc(tile_ld[q % 2], 16)

                def store(i, p):
                    sp.wait_ge(y_ok2, i + 1)
                    sp.dma_start(ffn_sorted[at(i * P, P), :], y_sb[:, p, :]).then_inc(y_st[p], 16)

                for e in range(2):
                    reload(sp, e, e, first_ld[e])

                def store_and_load(i, q):
                    store(i, q % 2)
                    load(i + AHEAD, (q + AHEAD) % GROUP)

                GROUP = 2 * PAIRS
                LAST = (NT - AHEAD) // GROUP * GROUP
                with sp.Fori(0, LAST // GROUP) as j:
                    for q in range(GROUP):
                        store_and_load(GROUP * j + q, q)
                for i in range(LAST, NT - AHEAD):
                    store_and_load(i, i % GROUP)
                for i in range(NT - AHEAD, NT):
                    store(i, i % 2)
                out = io["out"].rearrange("(g p) d -> p g d", p=P)
                for g in range(0, G, 2):
                    sp.wait_ge(comb, G + g + 2)
                    sp.dma_start(out[:, g:g + 2, :], x_all[:, g:g + 2, :]).then_inc(out_st, 16)
                sp.wait_ge(out_st, 16 * (G // 2))

            @block.gpsimd
            def _(pool):
                nc.gpsimd.iota(iot[:], pattern=[[1, P]], base=0, channel_multiplier=0).then_inc(iota_ok, 1)
                nc.gpsimd.iota(num[:], pattern=[[P, G]], base=0, channel_multiplier=1).then_inc(iota_ok, 1)
                nc.gpsimd.memset(tri[:], 1.0).then_inc(tri_zero, 1)
                nc.gpsimd.memset(ones[:], 1.0).then_inc(one_ok, 1)
                nc.gpsimd.memset(seg[:], 1.0).then_inc(one_ok, 1)
                pool.wait_ge(one_ok, 2)
                nc.gpsimd.memset(seg[:, :, 0:1], 0.0).then_inc(one_ok, 1)
                pool.wait_ge(tri_zero, 1)
                nc.gpsimd.affine_select(out=tri[:], in_=tri[:], compare_op=ALU.is_gt, fill=0.0, base=0,
                                        pattern=[[1, P]], channel_multiplier=-1).then_inc(tri_ok, 1)
                def split(e, p):
                    for n, (lo, hi) in enumerate(PARTS):
                        nc.gpsimd.tensor_copy(w_hi[:, p * NW + lo:p * NW + hi], w_raw[:, p, lo:hi]).then_inc(hi_ok, 1)
                        pool.wait_ge(hi_ok, 2 * e + n + 1)
                        take_wait()
                        nc.gpsimd.tensor_tensor(w_lo[:, p * NW + lo:p * NW + hi], w_raw[:, p, lo:hi],
                                                w_hi[:, p * NW + lo:p * NW + hi].bitcast(F32), ALU.subtract).then_inc(w_ok, 1)

                taken = [0]

                def take_wait():
                    k = taken[0] % 16
                    nc.gpsimd.tensor_tensor(pool_scrap2[:, k:k + 1], ident[:, 0:1], ident[:, 0:1], ALU.mult)
                    taken[0] += 1

                def next_expert(e, p, loaded, count):
                    last_tile = pool.value_load(tile_end[0:1, at(e - 2)], min_val=1, max_val=NT)
                    pool.wait_ge(y_mm, last_tile)
                    take_wait()
                    pool.wait_ge(loaded, count)
                    take_wait()
                    split(e, p)

                pool.wait_ge(id_ok, 1)
                for i in range(NT):
                    if i % 2 == 0 and i >= 2 * PAIRS:
                        pool.wait_ge(tok_ld[i // 2 % PAIRS], gathered(i - 2 * PAIRS))
                    pool.indirect_dma_start(tok[:, i, :], None, xn3_dram,
                                            bass.IndirectOffsetOnAxis(ap=tok_id[:, i:i + 1], axis=0)
                                            ).then_inc(tok_ld[i // 2 % PAIRS], 16)
                pool.wait_ge(tab_ok, 1)
                for p in range(2):
                    next_expert(2 + p, p, first_ld[p], 128)
                    reload(pool, 2 + p, p, wts_ld[p])
                with pool.Fori(2, E // 2 - 1) as j:
                    for p in range(2):
                        next_expert(2 * j + p, p, wts_ld[p], 64 * (j - 1))
                        reload(pool, 2 * j + p, p, wts_ld[p])
                for p in range(2):
                    next_expert(E - 2 + p, p, wts_ld[p], 64 * (E // 2 - 2))
                def fetch(y, k, done):
                    for g in range(G):
                        pool.indirect_dma_start(y[:, g, :], None, ffn_sorted,
                                                bass.IndirectOffsetOnAxis(ap=pos[:, k, g:g + 1], axis=0)).then_inc(done(g), 16)

                pool.wait_ge(pos_ok2, 1)
                for p in range(2):
                    stores = pool.value_load(tile_end[0:1, E + p:E + p + 1], min_val=1, max_val=NT)
                    pool.wait_ge(y_st[p], stores * 16)
                    take_wait()
                fetch(y_one, 0, lambda g: low_ld)
                for p in range(2):
                    pool.wait_ge(y_st[p], so_far(NT - 1 if (NT - 1) % 2 == p else NT - 2, p))
                fetch(y_two, 1, lambda g: up_ld[g // 2])

            @block.scalar
            def _(act):
                def round_tokens(i, p):
                    act.wait_ge(x_mm, i + 1)
                    wait(act, gu_mm, 2 * (i - 1))
                    nc.scalar.copy(tokT_hi[:, p, :], ps_x[:, 0:KD * P]).then_inc(xT_hi, 1)

                def silu(i):
                    for c in range(2):
                        act.wait_ge(gu_mm, 2 * i + c + 1)
                        wait(act, hid_ok, 2 * (i - 1) + c + 1)
                        nc.scalar.activation(act_[:, c * HH:(c + 1) * HH], ps_g[c][:, 0:HH], ACT.Silu).then_inc(silu2_ok, 1)

                def round_hidden(i):
                    act.wait_ge(h_mm, 2 * i + 2)
                    wait(act, y_mm, i)
                    nc.scalar.copy(hidT_hi[:, 0:4, :], ps_h0[:].rearrange("p (c m) -> p c m", c=4)).then_inc(hT_hi, 1)
                    nc.scalar.copy(hidT_hi[:, 4:KH - 1, :], ps_h1[:, 0:(KH - 5) * P].rearrange("p (c m) -> p c m", m=P)
                                   ).then_inc(hT_hi, 1)
                    nc.scalar.copy(hidT_hi[0:H_LAST, KH - 1, :], ps_h1[0:H_LAST, (KH - 5) * P:(KH - 4) * P]).then_inc(hT_hi, 1)

                act.wait_ge(w_pad, 1)
                for p in range(2):
                    act.wait_ge(first_ld[p], 64)
                    for lo, hi in PARTS:
                        nc.scalar.copy(w_hi[:, p * NW + lo:p * NW + hi], w_raw[:, p, lo:hi]).then_inc(hi_ok, 1)
                nc.scalar.activation(silu_scrap[:], ident[:, 0:1], ACT.Silu)
                round_tokens(0, 0)
                round_tokens(1, 1)
                silu(0)

                def pair(i):
                    for k in range(2):
                        round_hidden(i + k - 1)
                        round_tokens(i + k + 1, k)
                        silu(i + k)

                pair(1)
                with act.Fori(3, NT - 2, 2) as i:
                    pair(i)
                round_hidden(NT - 3)
                round_tokens(NT - 1, 0)
                silu(NT - 2)
                round_hidden(NT - 2)
                silu(NT - 1)
                round_hidden(NT - 1)

            @block.vector
            def _(dve):
                count = [0]

                def chain(ins):
                    ins.then_inc(step, 1)
                    count[0] += 1
                    dve.wait_ge(step, count[0])

                def over_e(t):
                    return t.unsqueeze(2).to_broadcast([P, G, E])

                def over_g(t):
                    return t.unsqueeze(1).to_broadcast([P, G, E])

                nc.vector.memset(w_raw[H_LAST:P, :, NW - D:NW], 0.0).then_inc(w_pad, 1)
                dve.wait_ge(iota_ok, 2)
                chain(nc.vector.tensor_copy(num_f[:], num[:]))
                chain(nc.vector.tensor_copy(iot_f[:], iot[:]))
                chain(nc.vector.tensor_copy(cnt_f[:], iot[:, 0:E]))
                chain(nc.vector.tensor_scalar(rev[:], cnt_f[:], -1.0, float(E), ALU.mult, ALU.add))
                chain(nc.vector.tensor_copy(tile_id[:], iot[0:1, 0:LOOP]))
                chain(nc.vector.tensor_copy(rest[:], scores[:]))
                for k in range(2):
                    chain(nc.vector.reduce_max(w_top[:, k, :], rest[:], AX_X))
                    chain(nc.vector.tensor_tensor(eq[:], rest[:], over_e(w_top[:, k, :]), ALU.is_equal))
                    chain(nc.vector.tensor_tensor(eq[:], eq[:], over_g(rev[:]), ALU.mult))
                    chain(nc.vector.reduce_max(km[:], eq[:], AX_X))
                    chain(nc.vector.tensor_tensor(oh[:, k, :, :], eq[:], over_e(km[:]), ALU.is_equal))
                    if k == 0:
                        chain(nc.vector.scalar_tensor_tensor(out=rest[:], in0=oh[:, 0, :, :], scalar=NEG_HUGE, in1=rest[:],
                                                             op0=ALU.mult, op1=ALU.add))
                nc.vector.tensor_tensor(both[:], oh[:, 0, :, :], oh[:, 1, :, :], ALU.add).then_inc(mask_ok, 1)
                dve.wait_ge(rank_mm, 1)
                dve.wait_ge(one_ok, 3)
                chain(nc.vector.tensor_copy(tot[:], ps_u[0][:, 0:G * E].rearrange("p (g e) -> p e g", e=E)))
                flat = "p e g -> p (e g)"
                chain(nc.vector.tensor_tensor_scan(inc[:].rearrange(flat), seg[:].rearrange(flat), tot[:].rearrange(flat),
                                                   0.0, ALU.mult, ALU.add))
                chain(nc.vector.tensor_tensor(tot[:], inc[:], tot[:], ALU.subtract))
                chain(nc.vector.tensor_tensor(slot[:], ps_g[0][:, 0:G * E].rearrange("p (g e) -> p g e", e=E),
                                              tot[:].rearrange("p e g -> p g e"), ALU.add))
                chain(nc.vector.tensor_copy(cnt_f[:], inc[:, :, G - 1]))
                chain(nc.vector.tensor_scalar(cnt_f[:], cnt_f[:], float(P - 1), float(P), ALU.add, ALU.max))
                chain(nc.vector.tensor_copy(cnt_i[:], cnt_f[:]))
                chain(nc.vector.tensor_scalar(cnt_i[:], cnt_i[:], P.bit_length() - 1, None, ALU.arith_shift_right))
                chain(nc.vector.tensor_copy(tiles[:], cnt_i[:]))
                chain(nc.vector.tensor_tensor_scan(tend[:], ones[:, 0:E], tiles[:], 0.0, ALU.mult, ALU.add))
                chain(nc.vector.tensor_tensor(tiles[:], tend[:], tiles[:], ALU.subtract))
                chain(nc.vector.tensor_scalar(tiles[:], tiles[:], float(P), None, ALU.mult))
                chain(nc.vector.tensor_tensor(slot[:], slot[:], over_g(tiles[:]), ALU.add))
                for k in range(2):
                    chain(nc.vector.tensor_tensor(eq[:], oh[:, k, :, :], slot[:], ALU.mult))
                    chain(nc.vector.reduce_sum(pos_f[:, k, :], eq[:], AX_X))
                chain(nc.vector.tensor_tensor(first[:, 0, :], pos_f[:, 0, :], pos_f[:, 1, :], ALU.is_lt))
                chain(nc.vector.tensor_scalar(first[:, 1, :], first[:, 0, :], -1.0, 1.0, ALU.mult, ALU.add))
                chain(nc.vector.tensor_tensor(w_part[:, 0, :], pos_f[:, 0, :], pos_f[:, 1, :], ALU.min))
                chain(nc.vector.tensor_tensor(pos_f[:, 1, :], pos_f[:, 0, :], pos_f[:, 1, :], ALU.max))
                chain(nc.vector.tensor_copy(pos_f[:, 0, :], w_part[:, 0, :]))
                nc.vector.tensor_copy(pos[:], pos_f[:]).then_inc(pos_ok2, 1)
                chain(nc.vector.tensor_copy(q_i[:], pos_f[:]))
                chain(nc.vector.tensor_scalar(q_i[:], q_i[:], P.bit_length() - 1, None, ALU.arith_shift_right))
                chain(nc.vector.tensor_copy(q_f[:], q_i[:]))
                chain(nc.vector.scalar_tensor_tensor(out=r_f[:], in0=q_f[:], scalar=float(-P), in1=pos_f[:],
                                                     op0=ALU.mult, op1=ALU.add))
                for k in range(2):
                    hot = [P, G, COLS]
                    chain(nc.vector.tensor_tensor(hot_tile[:, k], iot_f[:, 0:COLS].unsqueeze(1).to_broadcast(hot),
                                                  q_f[:, k, :].unsqueeze(2).to_broadcast(hot), ALU.is_equal))
                    nc.vector.tensor_tensor(place_tile[:, k, :, :], hot_tile[:, k],
                                            num_f[:].unsqueeze(2).to_broadcast(hot), ALU.mult).then_inc(tile_hot, 1)
                    for g in range(0, G, G // 2):
                        hot_r = [P, G // 2, P]
                        nc.vector.tensor_tensor(place_row[:, k, g:g + G // 2, :], iot_f[:].unsqueeze(1).to_broadcast(hot_r),
                                                r_f[:, k, g:g + G // 2].unsqueeze(2).to_broadcast(hot_r), ALU.is_equal
                                                ).then_inc(row_hot, 1)
                for k in range(2):
                    chain(nc.vector.tensor_tensor(w_part[:, 0, :], w_top[:, 0, :], first[:, k, :], ALU.mult))
                    chain(nc.vector.tensor_tensor(w_part[:, 1, :], w_top[:, 1, :], first[:, 1 - k, :], ALU.mult))
                    chain(nc.vector.tensor_tensor(w_low[:, k, :], w_part[:, 0, :], w_part[:, 1, :], ALU.add))
                dve.wait_ge(id_mm, 1)
                nc.vector.tensor_copy(tok_id[:], ps_y[:, 0:NT]).then_inc(id_ok, 1)
                shape = [1, LOOP, E]
                chain(nc.vector.tensor_tensor(ge[:], tile_id[:].unsqueeze(2).to_broadcast(shape),
                                              tend[0:1, :].unsqueeze(1).to_broadcast(shape), ALU.is_ge))
                chain(nc.vector.reduce_sum(tile_e[:], ge[:], AX_X))
                chain(nc.vector.tensor_scalar(tile_e[:], tile_e[:], float(E - 1), None, ALU.min))
                chain(nc.vector.tensor_copy(tile_end[:, 0:E], tend[0:1, :]))
                chain(nc.vector.tensor_scalar(tile_end[:, E:E + 1], tend[0:1, E - 2:E - 1], 1.0, None, ALU.add))
                chain(nc.vector.tensor_copy(tile_end[:, E + 1:E + 2], tend[0:1, E - 2:E - 1]))
                chain(nc.vector.tensor_scalar(tile_end[:, E:E + 2], tile_end[:, E:E + 2], 1, None, ALU.arith_shift_right))
                nc.vector.tensor_copy(tile_expert[:], tile_e[:]).then_inc(tab_ok, 1)

                def multiply(i, p):
                    for c in range(2):
                        dve.wait_ge(silu2_ok, 2 * i + c + 1)
                        wait(dve, h_mm, 2 * (i - 1))
                        nc.vector.tensor_tensor(hid[:, p, c * HH:(c + 1) * HH], act_[:, c * HH:(c + 1) * HH],
                                                ps_u[c][:, 0:HH], ALU.mult).then_inc(hid_ok, 1)

                def rest_of_tokens(i, p):
                    dve.wait_ge(xT_hi, i + 1)
                    wait(dve, gu_mm, 2 * (i - 1))
                    nc.vector.tensor_tensor(tokT_lo[:, p, :], ps_x[:, 0:KD * P], tokT_hi[:, p, :].bitcast(F32),
                                            ALU.subtract).then_inc(xT_lo, 1)

                def rest_of_hidden(i):
                    for k, (c, n, rows_in, bank) in enumerate(((0, 4, P, ps_h0), (4, KH - 5, P, ps_h1), (KH - 1, 1, H_LAST, ps_h1))):
                        dve.wait_ge(hT_hi, 3 * i + (1 if k == 0 else 3))
                        wait(dve, y_mm, i)
                        col = c % 4 * P if k < 2 else (KH - 5) * P
                        nc.vector.tensor_tensor(hidT_lo[0:rows_in, c:c + n, :],
                                                bank[0:rows_in, col:col + n * P].rearrange("p (c m) -> p c m", m=P),
                                                hidT_hi[0:rows_in, c:c + n, :].bitcast(F32), ALU.subtract).then_inc(hT_lo, 1)

                def evacuate(i, p):
                    dve.wait_ge(y_mm, i + 1)
                    wait(dve, y_st[p], so_far(i - 2, p))
                    nc.vector.tensor_copy(y_sb[:, p, :], ps_y[:, 0:D]).then_inc(y_ok2, 1)

                def split_rest(e):
                    for n, (lo, hi) in enumerate(PARTS):
                        dve.wait_ge(hi_ok, 2 * e + n + 1)
                        nc.vector.tensor_tensor(w_lo[:, e * NW + lo:e * NW + hi], w_raw[:, e, lo:hi],
                                                w_hi[:, e * NW + lo:e * NW + hi].bitcast(F32), ALU.subtract).then_inc(w_ok, 1)

                split_rest(0)
                rest_of_tokens(0, 0)
                rest_of_tokens(1, 1)
                multiply(0, 0)
                split_rest(1)

                def pair(i):
                    for k in range(2):
                        rest_of_hidden(i + k - 1)
                        rest_of_tokens(i + k + 1, k)
                        multiply(i + k, 1 - k)
                        evacuate(i + k - 1, k)

                pair(1)
                with dve.Fori(3, NT - 2, 2) as i:
                    pair(i)
                rest_of_hidden(NT - 3)
                rest_of_tokens(NT - 1, 0)
                multiply(NT - 2, 1)
                evacuate(NT - 3, 0)
                rest_of_hidden(NT - 2)
                multiply(NT - 1, 0)
                evacuate(NT - 2, 1)
                rest_of_hidden(NT - 1)
                evacuate(NT - 1, 0)
                dve.wait_ge(low_ld, 16 * G)
                for g in range(G):
                    nc.vector.scalar_tensor_tensor(out=x_all[:, g, :], in0=y_one[:, g, :], scalar=w_low[:, 0, g:g + 1],
                                                   in1=x_all[:, g, :], op0=ALU.mult, op1=ALU.add).then_inc(comb, 1)
                for g in range(G):
                    dve.wait_ge(comb, g + 1)
                    dve.wait_ge(up_ld[g // 2], 32)
                    nc.vector.scalar_tensor_tensor(out=x_all[:, g, :], in0=y_two[:, g, :], scalar=w_low[:, 1, g:g + 1],
                                                   in1=x_all[:, g, :], op0=ALU.mult, op1=ALU.add).then_inc(comb, 1)

            @block.tensor
            def _(pe):
                pe.wait_ge(mask_ok, 1)
                pe.wait_ge(tri_ok, 1)
                pe.wait_ge(one_ok, 3)
                flat = "p g e -> p (g e)"
                nc.tensor.matmul(ps_g[0][:, 0:G * E], tri[:], both[:].rearrange(flat), start=True, stop=True)
                nc.tensor.matmul(ps_u[0][:, 0:G * E], ones[:], both[:].rearrange(flat), start=True, stop=True).then_inc(rank_mm, 1)
                for k in range(2):
                    pe.wait_ge(tile_hot, k + 1)
                    for g in range(G):
                        if g % (G // 2) == 0:
                            pe.wait_ge(row_hot, 2 * k + g // (G // 2) + 1)
                        last = nc.tensor.matmul(ps_y[:, 0:COLS], place_row[:, k, g, :], place_tile[:, k, g, :],
                                                start=k == 0 and g == 0, stop=k == 1 and g == G - 1)
                last.then_inc(id_mm, 1)
                pe.wait_ge(tab_ok, 1)

                def expert(i):
                    return pe.value_load(tile_expert[0:1, at(i)], min_val=0, max_val=E - 1)

                def transpose_tokens(i, p):
                    if isinstance(i, int) and i < AHEAD:
                        pe.wait_ge(tok_ld[i // 2 % PAIRS], gathered(i))
                        x = tok[:, i, :]
                    else:
                        pe.wait_ge(tile_ld[p], so_far(i - AHEAD, p))
                        x = tok_in[:, p, :]
                    wait(pe, xT_lo, i)
                    for k in range(KD):
                        last = nc.tensor.transpose(ps_x[:, k * P:(k + 1) * P], x[:, k * P:(k + 1) * P], ident[:])
                    last.then_inc(x_mm, 1)

                def gate_up(i, p):
                    e = expert(i)
                    pe.wait_ge(w_ok, 2 * e + 1)
                    pe.wait_ge(xT_lo, i + 1)
                    parts = ((tokT_hi, w_hi), (tokT_hi, w_lo), (tokT_lo, w_hi))
                    for c in range(2):
                        wait(pe, hid_ok, 2 * (i - 1) + c + 1)
                        for out, first in ((ps_g[c], c * HH), (ps_u[c], NGU + c * HH)):
                            for k in range(KD):
                                for n, (x, w) in enumerate(parts):
                                    last = nc.tensor.matmul(out[:, 0:HH], x[:, p, k * P:(k + 1) * P],
                                                            w[:, at(e % 2 * NW + (first + k * HF), HH)],
                                                            start=k == 0 and n == 0, stop=k == KD - 1 and n == 2)
                        last.then_inc(gu_mm, 1)

                def transpose_hidden(i, p):
                    pe.wait_ge(hid_ok, 2 * i + 2)
                    wait(pe, hT_lo, 3 * i)
                    for c in range(4):
                        last = nc.tensor.transpose(ps_h0[:, c * P:(c + 1) * P], hid[:, p, c * P:(c + 1) * P], ident[:])
                    last.then_inc(h_mm, 1)
                    for c in range(4, KH):
                        n = P if c < KH - 1 else H_LAST
                        last = nc.tensor.transpose(ps_h1[0:n, (c - 4) * P:(c - 3) * P], hid[:, p, c * P:c * P + n], ident[:])
                    last.then_inc(h_mm, 1)

                def down(i):
                    e = expert(i)
                    pe.wait_ge(w_ok, 2 * e + 2)
                    wait(pe, y_ok2, i)
                    pe.wait_ge(hT_lo, 3 * i + 3)
                    parts = ((hidT_hi, w_hi), (hidT_hi, w_lo), (hidT_lo, w_hi))
                    for c in range(KH):
                        rows_in = P if c < KH - 1 else H_LAST
                        for n, (x, w) in enumerate(parts):
                            last = nc.tensor.matmul(ps_y[:, 0:D], x[0:rows_in, c, :],
                                                    w[0:rows_in, at(e % 2 * NW + (2 * NGU + c * D), D)],
                                                    start=c == 0 and n == 0, stop=c == KH - 1 and n == 2)
                    last.then_inc(y_mm, 1)

                transpose_tokens(0, 0)
                transpose_tokens(1, 1)
                gate_up(0, 0)

                def pair(i):
                    for k in range(2):
                        transpose_hidden(i + k - 1, k)
                        transpose_tokens(i + k + 1, k)
                        gate_up(i + k, 1 - k)
                        down(i + k - 1)

                pair(1)
                with pe.Fori(3, NT - 2, 2) as i:
                    pair(i)
                transpose_hidden(NT - 3, 0)
                transpose_tokens(NT - 1, 0)
                gate_up(NT - 2, 1)
                down(NT - 3)
                transpose_hidden(NT - 2, 1)
                gate_up(NT - 1, 0)
                down(NT - 2)
                transpose_hidden(NT - 1, 0)
                down(NT - 1)


def kernel(x, ctx_1024, mask_BxSxS2_bk1, L0_attn_W_in, L0_attn_W_conv, L0_attn_b_conv, L0_attn_W_x, L0_attn_W_dt,
           L0_attn_b_dt, L0_attn_W_out, L0_attn_A_log, L0_attn_D, L0_xattn_Wq, L0_xattn_bq, L0_xattn_Wk, L0_xattn_bk,
           L0_xattn_Wv, L0_xattn_bv, L0_xattn_Wo, L0_xattn_bo, L0_ffn_Wg, L0_ffn_W1, L0_ffn_W2, L0_ffn_W3):
    import numpy as np
    from concourse import bacc
    from concourse.bass_utils import run_bass_kernel_spmd

    def lay(a, *axes):
        a = np.asarray(a)
        return np.ascontiguousarray(a.transpose(axes) if axes else a)

    def columns(a):
        return lay(np.asarray(a).reshape(-1, P), 1, 0)

    B, S, D = x.shape
    S2 = ctx_1024.shape[1]
    DI, NST = L0_attn_A_log.shape
    TAPS = L0_attn_W_conv.shape[2]
    E, HF, _ = L0_ffn_W1.shape
    arrays = {
        "x": lay(x).reshape(B * S, D),
        "ctx": lay(ctx_1024),
        "ctxT": lay(ctx_1024, 0, 2, 1),
        "mask": lay(mask_BxSxS2_bk1),
        "w_inT": lay(L0_attn_W_in, 1, 0),
        "w_conv": lay(L0_attn_W_conv).reshape(DI, TAPS),
        "b_conv": columns(L0_attn_b_conv),
        "w_bT": lay(np.asarray(L0_attn_W_x)[NST:2 * NST], 1, 0),
        "w_dtT": lay(L0_attn_W_dt, 1, 0),
        "b_dt": columns(L0_attn_b_dt),
        "w_outT": lay(L0_attn_W_out, 1, 0),
        "a_log": lay(L0_attn_A_log),
        "d_skip": columns(L0_attn_D),
        "wq": lay(L0_xattn_Wq), "wk": lay(L0_xattn_Wk), "wv": lay(L0_xattn_Wv),
        "bq": columns(L0_xattn_bq), "bk": columns(L0_xattn_bk), "bv": columns(L0_xattn_bv), "bo": lay(L0_xattn_bo),
        "woT": lay(L0_xattn_Wo, 1, 0),
        "w_gT": lay(L0_ffn_Wg, 1, 0),
        "w1T": lay(L0_ffn_W1, 0, 2, 1),
        "w2T": lay(L0_ffn_W2, 0, 2, 1),
        "w3T": lay(L0_ffn_W3, 0, 2, 1),
    }
    nc = bacc.Bacc("TRN2", target_bir_lowering=False, num_devices=1)
    io = {k: nc.dram_tensor(f"in_{k}", a.shape, mybir.dt.from_np(a.dtype), kind="ExternalInput").ap()
          for k, a in arrays.items()}
    io["out"] = nc.dram_tensor("out", [B * S, D], F32, kind="ExternalOutput").ap()
    decoder_kernel(nc, io, (B, S, D, S2, DI, NST, TAPS, E, HF))
    result = run_bass_kernel_spmd(nc, [{f"in_{k}": a for k, a in arrays.items()}], core_ids=[0])
    return result.results[0]["out"].reshape(B, S, D)
```
